# Optimizing a Trainium2 kernel written in Bass

```python
import numpy as np
import jax
import jax.numpy as jnp

def _softmax(x, axis=-1):
    return jax.nn.softmax(x, axis=axis)

def _gelu(x):
    return jax.nn.gelu(x, approximate=True)

def _silu(x):
    return jax.nn.silu(x)

def _sigmoid(x):
    return jax.nn.sigmoid(x)

def _layernorm(x, axis=-1, eps=1e-05):
    m = jnp.mean(x, axis=axis, keepdims=True)
    v = jnp.var(x, axis=axis, keepdims=True)
    return (x - m) / jnp.sqrt(v + eps)

def _scatter_add(tgt, idx, src, axis=0):
    return tgt.at[idx].add(src)

def _segment_sum(src, seg, n):
    return jax.ops.segment_sum(src, seg, n)
kernel_name = 'mk_hybrid_d2_jaxref_r8_2f9783'

def setup_inputs(seed: int=0):
    np.random.seed(seed)
    _w = jnp.asarray

    def _L0_attn_a_setup():
        import math
        import jax, jax.numpy as jnp
        import numpy as np
        D_MODEL = 128
        N_HEAD = 16
        HEAD_DIM = D_MODEL // N_HEAD
        T = 1.0
        EPS = 1e-05

        def _layernorm(t, gamma, beta):
            m = t.mean(axis=-1, keepdims=True)
            var = ((t - m) ** 2).mean(axis=-1, keepdims=True)
            return (t - m) * jax.lax.rsqrt(var + EPS) * gamma + beta
        key = jax.random.key(seed)
        k1, k2, k3 = jax.random.split(key, 3)
        B, S = (4, 256)
        scale = 1.0 / math.sqrt(D_MODEL)
        return {'x': jax.random.normal(k1, (B, S, D_MODEL), dtype=jnp.float32), 'w_qkv': jax.random.normal(k2, (D_MODEL, 3 * D_MODEL), dtype=jnp.float32) * scale, 'w_proj': jax.random.normal(k3, (D_MODEL, D_MODEL), dtype=jnp.float32) * scale, 'q_gamma': jnp.ones((HEAD_DIM,), dtype=jnp.float32), 'q_beta': jnp.zeros((HEAD_DIM,), dtype=jnp.float32), 'k_gamma': jnp.ones((HEAD_DIM,), dtype=jnp.float32), 'k_beta': jnp.zeros((HEAD_DIM,), dtype=jnp.float32)}
    _L0_attn_a_in = _L0_attn_a_setup()

    def _L0_attn_b_setup():
        import math
        import jax, jax.numpy as jnp
        import numpy as np
        D_MODEL = 128
        N_HEADS = 16
        D_K = D_MODEL // N_HEADS
        D_C = 32
        B, S = (2, 256)
        key = jax.random.key(seed)
        ks = jax.random.split(key, 7)
        sd = lambda fan_in: 1.0 / math.sqrt(fan_in)
        return {'x': jax.random.normal(ks[0], (B, S, D_MODEL), dtype=jnp.float32), 'W_dq': jax.random.uniform(ks[1], (D_MODEL, D_C), minval=-sd(D_MODEL), maxval=sd(D_MODEL), dtype=jnp.float32), 'W_uq': jax.random.uniform(ks[2], (D_C, N_HEADS * D_K), minval=-sd(D_C), maxval=sd(D_C), dtype=jnp.float32), 'W_dkv': jax.random.uniform(ks[3], (D_MODEL, D_C), minval=-sd(D_MODEL), maxval=sd(D_MODEL), dtype=jnp.float32), 'W_uk': jax.random.uniform(ks[4], (D_C, N_HEADS * D_K), minval=-sd(D_C), maxval=sd(D_C), dtype=jnp.float32), 'W_uv': jax.random.uniform(ks[5], (D_C, N_HEADS * D_K), minval=-sd(D_C), maxval=sd(D_C), dtype=jnp.float32), 'W_o': jax.random.uniform(ks[6], (N_HEADS * D_K, D_MODEL), minval=-sd(N_HEADS * D_K), maxval=sd(N_HEADS * D_K), dtype=jnp.float32)}
    _L0_attn_b_in = _L0_attn_b_setup()

    def _L0_ffn_setup():
        import jax, jax.numpy as jnp
        import numpy as np
        DIM = 128
        DEPTH = 6
        HEADS = 16
        DIM_HEAD = 64
        WINDOW = 32
        INNER = HEADS * DIM_HEAD
        DIM_INNER = int(DIM * 4 * 2 / 3)
        QK_SCALE = 8.0

        def shift_tokens(t):
            a, s = jnp.split(t, 2, -1)
            s = jnp.pad(s, ((0, 0), (1, 0), (0, 0)))[:, :-1]
            return jnp.concatenate([a, s], -1)

        def l2norm(t):
            return t / jnp.maximum(jnp.linalg.norm(t, axis=-1, keepdims=True), 1e-12)

        def rotate_half(x):
            x1, x2 = jnp.split(x, 2, -1)
            return jnp.concatenate([-x2, x1], -1)

        def rotary_tables(n):
            half = jnp.arange(0, DIM_HEAD, 2, dtype=jnp.float32)
            inv_freq = 1.0 / 10000.0 ** (half / DIM_HEAD)
            t = jnp.arange(n, dtype=jnp.float32)
            freqs = t[:, None] * inv_freq[None, :]
            freqs = jnp.concatenate([freqs, freqs], -1)
            base_scale = (half + 0.4 * DIM_HEAD) / (1.4 * DIM_HEAD)
            power = (t - n // 2) / (WINDOW // 2)
            scale = base_scale[None, :] ** power[:, None]
            scale = jnp.concatenate([scale, scale], -1)
            return (freqs, scale)

        def local_attention(q, k, v):
            b, h, n, d = q.shape
            w = WINDOW
            nw = n // w
            bq = q.reshape(b, h, nw, w, d)
            bk = k.reshape(b, h, nw, w, d)
            bv = v.reshape(b, h, nw, w, d)

            def look(t):
                p = jnp.pad(t, ((0, 0), (0, 0), (1, 0), (0, 0), (0, 0)))
                return jnp.concatenate([p[:, :, :nw], p[:, :, 1:]], axis=3)
            bk2, bv2 = (look(bk), look(bv))
            seq = jnp.arange(n).reshape(nw, w)
            seq_p = jnp.pad(seq, ((1, 0), (0, 0)), constant_values=-1)
            jt = jnp.concatenate([seq_p[:nw], seq_p[1:]], axis=1)
            it = seq[:, :, None]
            jb = jt[:, None, :]
            mask = (it < jb) | (it > jb + w) | (jb == -1)
            sim = jnp.einsum('bhwie,bhwje->bhwij', bq, bk2) * QK_SCALE
            sim = jnp.where(mask, -jnp.finfo(sim.dtype).max, sim)
            attn = jax.nn.softmax(sim, -1)
            out = jnp.einsum('bhwij,bhwje->bhwie', attn, bv2)
            return out.reshape(b, h, n, d)

        def attn_layer(x, Wqkv, qs, ksc, Wo):
            b, n, _ = x.shape
            qkv = x @ Wqkv
            q, k, v = jnp.split(qkv, 3, -1)
            sh = lambda t: t.reshape(b, n, HEADS, DIM_HEAD).transpose(0, 2, 1, 3)
            q, k, v = (sh(q), sh(k), sh(v))
            q = l2norm(q) * qs
            k = l2norm(k) * ksc
            freqs, scale = rotary_tables(n)
            cos, sin = (jnp.cos(freqs), jnp.sin(freqs))
            q = q * cos * scale + rotate_half(q) * sin * scale
            inv = 1.0 / scale
            k = k * cos * inv + rotate_half(k) * sin * inv
            out = local_attention(q, k, v)
            out = out.transpose(0, 2, 1, 3).reshape(b, n, INNER)
            return out @ Wo

        def ffn_layer(x, g, bln, W1, b1, W2, b2):
            mu = x.mean(-1, keepdims=True)
            var = ((x - mu) ** 2).mean(-1, keepdims=True)
            xn = (x - mu) / jnp.sqrt(var + 1e-05) * g + bln
            hg = xn @ W1 + b1
            a, gate = jnp.split(hg, 2, -1)
            return a * jax.nn.gelu(gate, approximate=False) @ W2 + b2
        key = jax.random.key(seed)
        ks = jax.random.split(key, 8)
        B, N = (2, 256)
        init = lambda k, shape: jax.random.normal(k, shape, jnp.float32) * 0.02
        return {'x': jax.random.normal(ks[0], (B, N, DIM), jnp.float32), 'Wqkv': init(ks[1], (DEPTH, DIM, 3 * INNER)), 'q_scale': jnp.ones((DEPTH, DIM_HEAD), jnp.float32), 'k_scale': jnp.ones((DEPTH, DIM_HEAD), jnp.float32), 'Wo': init(ks[2], (DEPTH, INNER, DIM)), 'ln_g': jnp.ones((DEPTH, DIM), jnp.float32), 'ln_b': jnp.zeros((DEPTH, DIM), jnp.float32), 'W1': init(ks[3], (DEPTH, DIM, 2 * DIM_INNER)), 'b1': jnp.zeros((DEPTH, 2 * DIM_INNER), jnp.float32), 'W2': init(ks[4], (DEPTH, DIM_INNER, DIM)), 'b2': jnp.zeros((DEPTH, DIM), jnp.float32)}
    _L0_ffn_in = _L0_ffn_setup()

    def _L1_attn_a_setup():
        import jax, jax.numpy as jnp
        import numpy as np
        DIM = 128
        HEADS = 16
        HEAD_DIM = DIM // HEADS
        FEAT = 32
        B, N = (4, 512)

        def _elu1(x):
            return jnp.where(x > 0, x + 1.0, jnp.exp(x))
        key = jax.random.key(seed)
        k_x, k_qkv, k_proj, k_wo, k_bo = jax.random.split(key, 5)
        x = jax.random.normal(k_x, (B, N, DIM), dtype=jnp.float32)
        w_qkv = jax.random.normal(k_qkv, (DIM, 3 * DIM), dtype=jnp.float32) * (1.0 / np.sqrt(DIM))
        proj_matrix = jax.random.normal(k_proj, (HEADS, HEAD_DIM, FEAT), dtype=jnp.float32) * (1.0 / np.sqrt(HEAD_DIM))
        w_out = jax.random.normal(k_wo, (DIM, DIM), dtype=jnp.float32) * (1.0 / np.sqrt(DIM))
        b_out = jax.random.normal(k_bo, (DIM,), dtype=jnp.float32) * 0.01
        return {'x': x, 'w_qkv': w_qkv, 'proj_matrix': proj_matrix, 'w_out': w_out, 'b_out': b_out}
    _L1_attn_a_in = _L1_attn_a_setup()

    def _L1_attn_b_setup():
        import jax, jax.numpy as jnp
        import numpy as np
        D_MODEL = 128
        NUM_HEADS = 16
        D_K = D_MODEL // NUM_HEADS
        B, S = (4, 256)
        key = jax.random.key(seed)
        k1, k2, k3 = jax.random.split(key, 3)
        x = jax.random.normal(k1, (B, S, D_MODEL), dtype=jnp.float32)
        w_qkv = jax.random.normal(k2, (3, NUM_HEADS, D_K, D_MODEL), dtype=jnp.float32) / np.sqrt(D_MODEL)
        w_o = jax.random.normal(k3, (D_MODEL, D_MODEL), dtype=jnp.float32) / np.sqrt(D_MODEL)
        return {'x': x, 'w_qkv': w_qkv, 'w_o': w_o}
    _L1_attn_b_in = _L1_attn_b_setup()

    def _L1_ffn_setup():
        import jax, jax.numpy as jnp
        import numpy as np
        DIM = 128
        HIDDEN = 384
        SCALE = 1.0 / 127.0

        def _dequant(w_int, dtype):
            return w_int.astype(dtype) * jnp.asarray(SCALE, dtype)
        key = jax.random.key(seed)
        k_x, k_g, k_u, k_d = jax.random.split(key, 4)
        x = jax.random.normal(k_x, (4, 256, DIM), dtype=jnp.float32)
        w_gate = jax.random.randint(k_g, (HIDDEN, DIM), -127, 128, dtype=jnp.int32)
        w_up = jax.random.randint(k_u, (HIDDEN, DIM), -127, 128, dtype=jnp.int32)
        w_down = jax.random.randint(k_d, (DIM, HIDDEN), -127, 128, dtype=jnp.int32)
        return {'x': x, 'w_gate': w_gate, 'w_up': w_up, 'w_down': w_down}
    _L1_ffn_in = _L1_ffn_setup()
    _d = {'L0_attn_a_x': _L0_attn_a_in['x'], 'L0_attn_a_w_qkv': _L0_attn_a_in['w_qkv'], 'L0_attn_a_w_proj': _L0_attn_a_in['w_proj'], 'L0_attn_a_q_gamma': _L0_attn_a_in['q_gamma'], 'L0_attn_a_q_beta': _L0_attn_a_in['q_beta'], 'L0_attn_a_k_gamma': _L0_attn_a_in['k_gamma'], 'L0_attn_a_k_beta': _L0_attn_a_in['k_beta'], 'L0_attn_b_W_dq': _L0_attn_b_in['W_dq'], 'L0_attn_b_W_uq': _L0_attn_b_in['W_uq'], 'L0_attn_b_W_dkv': _L0_attn_b_in['W_dkv'], 'L0_attn_b_W_uk': _L0_attn_b_in['W_uk'], 'L0_attn_b_W_uv': _L0_attn_b_in['W_uv'], 'L0_attn_b_W_o': _L0_attn_b_in['W_o'], 'L0_ffn_Wqkv': _L0_ffn_in['Wqkv'], 'L0_ffn_q_scale': _L0_ffn_in['q_scale'], 'L0_ffn_k_scale': _L0_ffn_in['k_scale'], 'L0_ffn_Wo': _L0_ffn_in['Wo'], 'L0_ffn_ln_g': _L0_ffn_in['ln_g'], 'L0_ffn_ln_b': _L0_ffn_in['ln_b'], 'L0_ffn_W1': _L0_ffn_in['W1'], 'L0_ffn_b1': _L0_ffn_in['b1'], 'L0_ffn_W2': _L0_ffn_in['W2'], 'L0_ffn_b2': _L0_ffn_in['b2'], 'L1_attn_a_w_qkv': _L1_attn_a_in['w_qkv'], 'L1_attn_a_proj_matrix': _L1_attn_a_in['proj_matrix'], 'L1_attn_a_w_out': _L1_attn_a_in['w_out'], 'L1_attn_a_b_out': _L1_attn_a_in['b_out'], 'L1_attn_b_w_qkv': _L1_attn_b_in['w_qkv'], 'L1_attn_b_w_o': _L1_attn_b_in['w_o'], 'L1_ffn_w_gate': _L1_ffn_in['w_gate'], 'L1_ffn_w_up': _L1_ffn_in['w_up'], 'L1_ffn_w_down': _L1_ffn_in['w_down']}
    _x0 = _d['L0_attn_a_x']
    _d['L0_attn_a_x'] = jax.random.normal(jax.random.fold_in(jax.random.key(seed), 1), (4, 512, 128), dtype=_x0.dtype)
    del _x0
    return _d

def reference(L0_attn_a_x, L0_attn_a_w_qkv, L0_attn_a_w_proj, L0_attn_a_q_gamma, L0_attn_a_q_beta, L0_attn_a_k_gamma, L0_attn_a_k_beta, L0_attn_b_W_dq, L0_attn_b_W_uq, L0_attn_b_W_dkv, L0_attn_b_W_uk, L0_attn_b_W_uv, L0_attn_b_W_o, L0_ffn_Wqkv, L0_ffn_q_scale, L0_ffn_k_scale, L0_ffn_Wo, L0_ffn_ln_g, L0_ffn_ln_b, L0_ffn_W1, L0_ffn_b1, L0_ffn_W2, L0_ffn_b2, L1_attn_a_w_qkv, L1_attn_a_proj_matrix, L1_attn_a_w_out, L1_attn_a_b_out, L1_attn_b_w_qkv, L1_attn_b_w_o, L1_ffn_w_gate, L1_ffn_w_up, L1_ffn_w_down):

    def _L0_attn_a_ref(x, w_qkv, w_proj, q_gamma, q_beta, k_gamma, k_beta):
        import math
        import jax, jax.numpy as jnp
        import numpy as np
        D_MODEL = 128
        N_HEAD = 16
        HEAD_DIM = D_MODEL // N_HEAD
        T = 1.0
        EPS = 1e-05

        def _layernorm(t, gamma, beta):
            m = t.mean(axis=-1, keepdims=True)
            var = ((t - m) ** 2).mean(axis=-1, keepdims=True)
            return (t - m) * jax.lax.rsqrt(var + EPS) * gamma + beta
        B, S, C = x.shape
        H, Dh = (N_HEAD, HEAD_DIM)
        qkv = (x @ w_qkv).reshape(B, S, 3, H, Dh)
        qkv = jnp.transpose(qkv, (2, 0, 3, 1, 4))
        q, k, v = (qkv[0], qkv[1], qkv[2])
        q = _layernorm(q, q_gamma, q_beta)
        k = _layernorm(k, k_gamma, k_beta)
        logits = jnp.einsum('bhsd,bhtd->bhst', q, k) / (math.sqrt(Dh) * T)
        att = jax.nn.softmax(logits, axis=-1)
        out = jnp.einsum('bhst,bhtd->bhsd', att, v)
        out = jnp.transpose(out, (0, 2, 1, 3)).reshape(B, S, C)
        return out @ w_proj

    def _L0_attn_b_ref(x, W_dq, W_uq, W_dkv, W_uk, W_uv, W_o):
        import math
        import jax, jax.numpy as jnp
        import numpy as np
        D_MODEL = 128
        N_HEADS = 16
        D_K = D_MODEL // N_HEADS
        D_C = 32
        B, S = (2, 256)
        Bx, Sx, _ = x.shape
        c_q = x @ W_dq
        Q = (c_q @ W_uq).reshape(Bx, Sx, N_HEADS, D_K)
        c_kv = x @ W_dkv
        K = (c_kv @ W_uk).reshape(Bx, Sx, N_HEADS, D_K)
        V = (c_kv @ W_uv).reshape(Bx, Sx, N_HEADS, D_K)
        scores = jnp.einsum('bqhd,bkhd->bhqk', Q, K) / math.sqrt(D_K)
        causal = jnp.tril(jnp.ones((Sx, Sx), dtype=bool))
        scores = jnp.where(causal, scores, -jnp.inf)
        attn = jax.nn.softmax(scores, axis=-1)
        out = jnp.einsum('bhqk,bkhd->bqhd', attn, V).reshape(Bx, Sx, N_HEADS * D_K)
        return out @ W_o

    def _L0_ffn_ref(x, Wqkv, q_scale, k_scale, Wo, ln_g, ln_b, W1, b1, W2, b2):
        import jax, jax.numpy as jnp
        import numpy as np
        DIM = 128
        DEPTH = 6
        HEADS = 16
        DIM_HEAD = 64
        WINDOW = 32
        INNER = HEADS * DIM_HEAD
        DIM_INNER = int(DIM * 4 * 2 / 3)
        QK_SCALE = 8.0

        def shift_tokens(t):
            a, s = jnp.split(t, 2, -1)
            s = jnp.pad(s, ((0, 0), (1, 0), (0, 0)))[:, :-1]
            return jnp.concatenate([a, s], -1)

        def l2norm(t):
            return t / jnp.maximum(jnp.linalg.norm(t, axis=-1, keepdims=True), 1e-12)

        def rotate_half(x):
            x1, x2 = jnp.split(x, 2, -1)
            return jnp.concatenate([-x2, x1], -1)

        def rotary_tables(n):
            half = jnp.arange(0, DIM_HEAD, 2, dtype=jnp.float32)
            inv_freq = 1.0 / 10000.0 ** (half / DIM_HEAD)
            t = jnp.arange(n, dtype=jnp.float32)
            freqs = t[:, None] * inv_freq[None, :]
            freqs = jnp.concatenate([freqs, freqs], -1)
            base_scale = (half + 0.4 * DIM_HEAD) / (1.4 * DIM_HEAD)
            power = (t - n // 2) / (WINDOW // 2)
            scale = base_scale[None, :] ** power[:, None]
            scale = jnp.concatenate([scale, scale], -1)
            return (freqs, scale)

        def local_attention(q, k, v):
            b, h, n, d = q.shape
            w = WINDOW
            nw = n // w
            bq = q.reshape(b, h, nw, w, d)
            bk = k.reshape(b, h, nw, w, d)
            bv = v.reshape(b, h, nw, w, d)

            def look(t):
                p = jnp.pad(t, ((0, 0), (0, 0), (1, 0), (0, 0), (0, 0)))
                return jnp.concatenate([p[:, :, :nw], p[:, :, 1:]], axis=3)
            bk2, bv2 = (look(bk), look(bv))
            seq = jnp.arange(n).reshape(nw, w)
            seq_p = jnp.pad(seq, ((1, 0), (0, 0)), constant_values=-1)
            jt = jnp.concatenate([seq_p[:nw], seq_p[1:]], axis=1)
            it = seq[:, :, None]
            jb = jt[:, None, :]
            mask = (it < jb) | (it > jb + w) | (jb == -1)
            sim = jnp.einsum('bhwie,bhwje->bhwij', bq, bk2) * QK_SCALE
            sim = jnp.where(mask, -jnp.finfo(sim.dtype).max, sim)
            attn = jax.nn.softmax(sim, -1)
            out = jnp.einsum('bhwij,bhwje->bhwie', attn, bv2)
            return out.reshape(b, h, n, d)

        def attn_layer(x, Wqkv, qs, ksc, Wo):
            b, n, _ = x.shape
            qkv = x @ Wqkv
            q, k, v = jnp.split(qkv, 3, -1)
            sh = lambda t: t.reshape(b, n, HEADS, DIM_HEAD).transpose(0, 2, 1, 3)
            q, k, v = (sh(q), sh(k), sh(v))
            q = l2norm(q) * qs
            k = l2norm(k) * ksc
            freqs, scale = rotary_tables(n)
            cos, sin = (jnp.cos(freqs), jnp.sin(freqs))
            q = q * cos * scale + rotate_half(q) * sin * scale
            inv = 1.0 / scale
            k = k * cos * inv + rotate_half(k) * sin * inv
            out = local_attention(q, k, v)
            out = out.transpose(0, 2, 1, 3).reshape(b, n, INNER)
            return out @ Wo

        def ffn_layer(x, g, bln, W1, b1, W2, b2):
            mu = x.mean(-1, keepdims=True)
            var = ((x - mu) ** 2).mean(-1, keepdims=True)
            xn = (x - mu) / jnp.sqrt(var + 1e-05) * g + bln
            hg = xn @ W1 + b1
            a, gate = jnp.split(hg, 2, -1)
            return a * jax.nn.gelu(gate, approximate=False) @ W2 + b2
        for i in range(DEPTH):
            x = attn_layer(shift_tokens(x), Wqkv[i], q_scale[i], k_scale[i], Wo[i]) + x
            x = ffn_layer(shift_tokens(x), ln_g[i], ln_b[i], W1[i], b1[i], W2[i], b2[i]) + x
        return x

    def _L1_attn_a_ref(x, w_qkv, proj_matrix, w_out, b_out):
        import jax, jax.numpy as jnp
        import numpy as np
        DIM = 128
        HEADS = 16
        HEAD_DIM = DIM // HEADS
        FEAT = 32
        B, N = (4, 512)

        def _elu1(x):
            return jnp.where(x > 0, x + 1.0, jnp.exp(x))
        b, n, d = x.shape
        h, hd = (HEADS, HEAD_DIM)
        qkv = x @ w_qkv
        q, k, v = jnp.split(qkv, 3, axis=-1)
        to_heads = lambda t: t.reshape(b, n, h, hd).transpose(0, 2, 1, 3)
        q, k, v = (to_heads(q), to_heads(k), to_heads(v))
        q_proj = _elu1(jnp.einsum('bhnd,hdf->bhnf', q, proj_matrix))
        k_proj = _elu1(jnp.einsum('bhnd,hdf->bhnf', k, proj_matrix))
        kv = jnp.einsum('bhnf,bhnd->bhfd', k_proj, v)
        attn = jnp.einsum('bhnf,bhfd->bhnd', q_proj, kv)
        k_sum = k_proj.sum(axis=2)
        z = 1.0 / (jnp.einsum('bhnf,bhf->bhn', q_proj, k_sum) + 1e-08)
        attn = attn * z[..., None]
        out = attn.transpose(0, 2, 1, 3).reshape(b, n, d)
        return out @ w_out + b_out

    def _L1_attn_b_ref(x, w_qkv, w_o):
        import jax, jax.numpy as jnp
        import numpy as np
        D_MODEL = 128
        NUM_HEADS = 16
        D_K = D_MODEL // NUM_HEADS
        B, S = (4, 256)
        seq_len = x.shape[-2]
        d_k = w_qkv.shape[-2]
        qkv = jnp.einsum('bsm,qhkm->qbhsk', x, w_qkv)
        Q, K, V = (qkv[0], qkv[1], qkv[2])
        scores = jnp.einsum('bhsk,bhtk->bhst', Q, K) / jnp.sqrt(jnp.asarray(d_k, x.dtype))
        causal = jnp.tril(jnp.ones((seq_len, seq_len), dtype=bool))
        scores = jnp.where(causal, scores, -jnp.inf)
        probs = jax.nn.softmax(scores, axis=-1)
        attn = jnp.einsum('bhst,bhtk->bhsk', probs, V)
        b, h, s, k = attn.shape
        attn_cat = jnp.transpose(attn, (0, 2, 1, 3)).reshape(b, s, h * k)
        return jnp.einsum('bsd,md->bsm', attn_cat, w_o)

    def _L1_ffn_ref(x, w_gate, w_up, w_down):
        import jax, jax.numpy as jnp
        import numpy as np
        DIM = 128
        HIDDEN = 384
        SCALE = 1.0 / 127.0

        def _dequant(w_int, dtype):
            return w_int.astype(dtype) * jnp.asarray(SCALE, dtype)
        wg = _dequant(w_gate, x.dtype)
        wu = _dequant(w_up, x.dtype)
        wd = _dequant(w_down, x.dtype)
        gate = jnp.einsum('bsd,hd->bsh', x, wg)
        up = jnp.einsum('bsd,hd->bsh', x, wu)
        h = jax.nn.silu(gate) * up
        return jnp.einsum('bsh,dh->bsd', h, wd)
    x = L0_attn_a_x
    x = x + _L0_attn_a_ref(_layernorm(x, axis=-1), L0_attn_a_w_qkv, L0_attn_a_w_proj, L0_attn_a_q_gamma, L0_attn_a_q_beta, L0_attn_a_k_gamma, L0_attn_a_k_beta)
    x = x + _L0_ffn_ref(_layernorm(x, axis=-1), L0_ffn_Wqkv, L0_ffn_q_scale, L0_ffn_k_scale, L0_ffn_Wo, L0_ffn_ln_g, L0_ffn_ln_b, L0_ffn_W1, L0_ffn_b1, L0_ffn_W2, L0_ffn_b2)
    x = x + _L0_attn_b_ref(_layernorm(x, axis=-1), L0_attn_b_W_dq, L0_attn_b_W_uq, L0_attn_b_W_dkv, L0_attn_b_W_uk, L0_attn_b_W_uv, L0_attn_b_W_o)
    x = x + _L0_ffn_ref(_layernorm(x, axis=-1), L0_ffn_Wqkv, L0_ffn_q_scale, L0_ffn_k_scale, L0_ffn_Wo, L0_ffn_ln_g, L0_ffn_ln_b, L0_ffn_W1, L0_ffn_b1, L0_ffn_W2, L0_ffn_b2)
    x = x + _L1_attn_a_ref(_layernorm(x, axis=-1), L1_attn_a_w_qkv, L1_attn_a_proj_matrix, L1_attn_a_w_out, L1_attn_a_b_out)
    x = x + _L1_ffn_ref(_layernorm(x, axis=-1), L1_ffn_w_gate, L1_ffn_w_up, L1_ffn_w_down)
    x = x + _L1_attn_b_ref(_layernorm(x, axis=-1), L1_attn_b_w_qkv, L1_attn_b_w_o)
    x = x + _L1_ffn_ref(_layernorm(x, axis=-1), L1_ffn_w_gate, L1_ffn_w_up, L1_ffn_w_down)
    return x

_drawn_inputs = setup_inputs


def setup_inputs(seed=0):
    import zlib

    import numpy as np

    out = dict(_drawn_inputs(seed))
    spreads = {'L0_attn_a_q_gamma': (1.0, 0.2),
     'L0_attn_a_q_beta': (0.0, 0.1),
     'L0_attn_a_k_gamma': (1.0, 0.2),
     'L0_attn_a_k_beta': (0.0, 0.8),
     'L0_ffn_q_scale': (1.0, 0.6),
     'L0_ffn_k_scale': (1.0, 0.6),
     'L0_ffn_ln_g': (1.0, 0.6),
     'L0_ffn_ln_b': (0.0, 0.8),
     'L0_ffn_b1': (0.0, 0.33),
     'L0_ffn_b2': (0.0, 0.1)}
    factors = {'L0_attn_b_W_dq': 8.0,
     'L0_attn_b_W_uq': 8.0,
     'L0_attn_b_W_uk': 8.0,
     'L1_attn_a_proj_matrix': 7.796,
     'L1_attn_a_b_out': 8.0,
     'L1_attn_b_w_qkv': 8.0,
     'L1_attn_b_w_o': 8.0}
    for name, (base, spread) in spreads.items():
        noise = np.random.default_rng([zlib.crc32(name.encode()), seed]).standard_normal(out[name].shape)
        drawn = base * np.exp(spread * noise) if base else spread * noise
        out[name] = jnp.asarray(drawn.astype(out[name].dtype))
    for name, factor in factors.items():
        out[name] = (out[name] * factor).astype(out[name].dtype)
    return out
```

```python
import numpy as np
from contextlib import ExitStack

import concourse.bass as bass
from concourse import mybir
from concourse.alu_op_type import AluOpType as ALU

F32 = mybir.dt.float32
BF16 = mybir.dt.bfloat16
I32 = mybir.dt.int32
ACT = mybir.ActivationFunctionType
AX = mybir.AxisListType

P = 128
BATCH, SEQ = 4, 512
TOK = BATCH * SEQ
EPS = 1e-5

DEPTH, HEADS, HD, WIN = 6, 16, 64, 32
INNER = HEADS * HD
QKV = 3 * INNER
FF = int(P * 4 * 2 / 3)
FF_ROWS = [min(P, FF - P * j) for j in range(3)]
UNITS = 4
TB = SEQ // P
SLOTS = UNITS * TB
KEYS = WIN + P
NEG = -1e30

SH, SD = 16, 8
SG = SH // 4
FF_LOADS = 12
NORM_SCALE = 2.0 ** 16
AHEAD = 80


class Events:

    def __init__(self, ctx, nc, name):
        self.sem = ctx.enter_context(nc.semaphore(name))
        self.start = 0

    def at(self, n):
        return n + self.start

    def past(self, n):
        self.start += n


class Counts:

    def __init__(self, eng, turn, per_turn):
        self.eng, self.turn, self.per_turn, self.bases = eng, turn, per_turn, {}

    def wait(self, e, n):
        k = self.per_turn[e]
        if k not in self.bases:
            base = self.turn * k
            self.bases[k] = base if isinstance(base, int) else self.eng.snap(base)
        self.eng.wait_ge(e.sem, self.bases[k] + (e.start + n))


def constants():
    half = np.arange(0, HD, 2, dtype=np.float32)
    inv_freq = (1.0 / 10000.0 ** (half / HD)).astype(np.float32)
    pos = np.arange(SEQ, dtype=np.float32)
    freqs = pos[:, None] * inv_freq[None, :]
    cos, sin = np.cos(freqs), np.sin(freqs)
    base = (half + 0.4 * HD) / (1.4 * HD)
    scale = base[None, :] ** ((pos - SEQ // 2) / (WIN // 2))[:, None]
    straight = np.zeros((SEQ, 2, 2, HD // 2), np.float32)
    crossed = np.zeros((SEQ, 2, 2, HD // 2), np.float32)
    for s, f in enumerate((8.0 * scale, 1.0 / scale)):
        straight[:, s, 0] = straight[:, s, 1] = cos * f
        crossed[:, s, 0] = -sin * f
        crossed[:, s, 1] = sin * f
    lay = lambda a: np.ascontiguousarray(
        a.reshape(TB, P, 2 * HD).transpose(1, 0, 2).reshape(P, TB * 2 * HD), np.float32)
    p, c = np.arange(P)[:, None], np.arange(KEYS)[None, :]
    seen = (p <= c) & (c <= p + WIN)
    first = np.where(seen & (c >= WIN), 0.0, NEG)
    later = np.where(seen, 0.0, NEG)
    band = np.concatenate([first, first, later, later], 1).astype(np.float32)
    causal = np.where(np.arange(P)[None, :] <= p, 0.0, NEG).astype(np.float32)
    return {
        "rope_straight": lay(straight),
        "rope_crossed": lay(crossed),
        "band": band,
        "identity": np.eye(P, dtype=np.float32),
        "causal": causal,
        "head_of_channel": np.kron(np.eye(SH), np.ones((SD, 1))).astype(np.float32),
        "mean_of_8": np.kron(np.full((SD, SD), 1 / SD), np.eye(SH)).astype(np.float32),
        "sum_rows": np.kron(np.eye(4), np.outer(np.arange(32) == SD, np.ones(32))).astype(np.float32),
        "own_head": np.kron(np.eye(4), np.ones((32, 32))).astype(np.float32),
        "quadrant": np.kron(np.eye(TB), np.ones((WIN, 1))).astype(np.float32),
    }


class Core:

    def __init__(self, nc, ctx, d):
        self.nc, self.ctx, self.d = nc, ctx, d
        self.names = 0
        sb = self.sb
        self.x = sb(ctx, "x", [P, TOK])
        self.z = sb(ctx, "z", [P, TOK])
        self.ident = sb(ctx, "ident", [P, P])
        self.ident16 = sb(ctx, "ident16", [P, P], BF16)
        self.mean_w = sb(ctx, "mean_w", [P, P])
        self.small = sb(ctx, "small", [P, 8])
        self.ps = ctx.enter_context(nc.psum_tensor("ps", [P, 8, 512], F32))
        self.ev = {}

    def sb(self, ctx, name, shape, dt=F32):
        self.names += 1
        return ctx.enter_context(self.nc.sbuf_tensor(f"{name}_{self.names}", shape, dt))

    def events(self, *names):
        for n in names:
            if n not in self.ev:
                self.ev[n] = Events(self.ctx, self.nc, n)
        got = [self.ev[n] for n in names]
        return got[0] if len(got) == 1 else got


EPS_COL, LN_UP_COL = 0, 1


def load_and_transpose(core):
    nc, d = core.nc, core.d
    loaded, loaded_id, made, turned, moved = core.events("ld_x", "ld_ident", "consts_made", "x_turned", "x_moved")
    with ExitStack() as ctx:
        xt = core.sb(ctx, "xt", [P, TOK // P, P])
        block = ctx.enter_context(nc.Block())

        @block.sync
        def _(sp):
            sp.dma_start(core.ident[:, :], d["identity"]).then_inc(loaded_id.sem, 16)
            sp.dma_start(xt[:, :, :], d["L0_attn_a_x"].rearrange("b (t p) c -> p (b t) c", p=P)).then_inc(loaded.sem, 16)

        @block.gpsimd
        def _(pool):
            pool.memset(core.mean_w[:, :], 1.0 / P).then_inc(made.sem, 1)
            pool.memset(core.small[:, EPS_COL:EPS_COL + 1], EPS).then_inc(made.sem, 1)
            pool.memset(core.small[:, LN_UP_COL:LN_UP_COL + 1], float(8.0 * np.log(2.0))).then_inc(made.sem, 1)

        @block.tensor
        def _(pe):
            pe.wait_ge(loaded_id.sem, 16)
            pe.wait_ge(loaded.sem, 16)
            for k in range(TOK // P):
                bank = k // 4 % 4
                last = pe.transpose(core.ps[:, bank, k % 4 * P:k % 4 * P + P], xt[:, k, :], core.ident[:, :])
                if k % 4 == 3:
                    last.then_inc(turned.sem, 1)

        @block.vector
        def _(dve):
            dve.wait_ge(loaded_id.sem, 16)
            dve.tensor_copy(core.ident16[:, :], core.ident[:, :])
            for b in range(BATCH):
                dve.wait_ge(turned.sem, b + 1)
                dve.tensor_copy(core.x[:, b * SEQ:(b + 1) * SEQ], core.ps[:, b, :]).then_inc(moved.sem, 1)


def turn_and_store(core):
    nc, d = core.nc, core.d
    turned, moved, stored = core.events("y_turned", "y_moved", "y_stored")
    with ExitStack() as ctx:
        yt = core.sb(ctx, "yt", [P, TOK // P, P])
        block = ctx.enter_context(nc.Block())

        @block.tensor
        def _(pe):
            for k in range(TOK // P):
                last = pe.transpose(core.ps[:, k // 4, k % 4 * P:k % 4 * P + P], core.x[:, k * P:k * P + P], core.ident[:, :])
                if k % 4 == 3:
                    last.then_inc(turned.sem, 1)

        @block.vector
        def _(dve):
            for b in range(BATCH):
                dve.wait_ge(turned.sem, b + 1)
                dve.tensor_copy(yt[:, b * TB:b * TB + TB, :], core.ps[:, b, :].rearrange("p (t c) -> p t c", t=TB)).then_inc(moved.sem, 1)

        @block.sync
        def _(sp):
            for b in range(BATCH):
                sp.wait_ge(moved.sem, b + 1)
                sp.dma_start(d["out"][b].rearrange("(t p) c -> p t c", p=P), yt[:, b * TB:b * TB + TB, :]).then_inc(stored.sem, 16)
            sp.wait_ge(stored.sem, 16 * BATCH)


def normalise(core, add_z):
    nc, x, z, ps = core.nc, core.x, core.z, core.ps
    added, mean, centred, squared, var, ln, rstd, done = core.events(
        "n_added", "n_mean", "n_centred", "n_squared", "n_var", "n_ln", "n_rstd", "n_done")
    cols = [slice(b * SEQ, (b + 1) * SEQ) for b in range(BATCH)]
    with ExitStack() as ctx:
        c = core.sb(ctx, "centred", [P, TOK])
        q = core.sb(ctx, "squares", [P, TOK])
        r = core.sb(ctx, "rstd", [P, TOK])
        block = ctx.enter_context(nc.Block())

        @block.tensor
        def _(pe):
            for b in range(BATCH):
                if add_z:
                    pe.wait_ge(added.sem, added.at(b + 1))
                pe.matmul(ps[:, b, :], core.mean_w[:, :], x[:, cols[b]], start=True, stop=True).then_inc(mean.sem, 1)
            for b in range(BATCH):
                pe.wait_ge(squared.sem, squared.at(b + 1))
                pe.matmul(ps[:, 4 + b, :], core.mean_w[:, :], q[:, cols[b]], start=True, stop=True).then_inc(var.sem, 1)

        @block.vector
        def _(dve):
            if add_z:
                for b in range(BATCH):
                    dve.tensor_tensor(x[:, cols[b]], x[:, cols[b]], z[:, cols[b]], ALU.add).then_inc(added.sem, 1)
            for b in range(BATCH):
                if add_z:
                    dve.wait_ge(added.sem, added.at(b + 1))
                dve.wait_ge(mean.sem, mean.at(b + 1))
                dve.tensor_tensor(c[:, cols[b]], x[:, cols[b]], ps[:, b, :], ALU.subtract).then_inc(centred.sem, 1)
            for b in range(BATCH):
                dve.wait_ge(rstd.sem, rstd.at(b + 1))
                dve.tensor_tensor(z[:, cols[b]], c[:, cols[b]], r[:, cols[b]], ALU.mult).then_inc(done.sem, 1)

        @block.scalar
        def _(act):
            act.preload_act_table_set("natural_log_exp_and_others")
            for b in range(BATCH):
                act.wait_ge(centred.sem, centred.at(b + 1))
                act.activation(q[:, cols[b]], c[:, cols[b]], ACT.Square).then_inc(squared.sem, 1)
            for b in range(BATCH):
                act.wait_ge(var.sem, var.at(b + 1))
                act.activation(r[:, cols[b]], ps[:, 4 + b, :], ACT.Ln, bias=core.small[:, EPS_COL:EPS_COL + 1]).then_inc(ln.sem, 1)
            for b in range(BATCH):
                act.wait_ge(ln.sem, ln.at(b + 1))
                act.activation(r[:, cols[b]], r[:, cols[b]], ACT.Exp, scale=-0.5).then_inc(rstd.sem, 1)
    if add_z:
        added.past(BATCH)
    for e in (mean, centred, squared, var, ln, rstd, done):
        e.past(BATCH)


def add_z_to_x(core):
    nc, x, z = core.nc, core.x, core.z
    with nc.Block() as block:

        @block.vector
        def _(dve):
            dve.tensor_tensor(x[:, :], x[:, :], z[:, :], ALU.add)


def local_block(core):
    nc, d, x, z, ps = core.nc, core.d, core.x, core.z, core.ps
    ev = core.events
    qk_ready, v_ready, tr_ready, s_ready, pt_ready, pbt_ready, av_ready, wo_ready, ff_mm = ev(
        "qk_ready", "v_ready", "tr_ready", "s_ready", "pt_ready", "pbt_ready", "av_ready", "wo_ready", "ff_mm")
    sq_done, v_kept, q_kept, exp_done, ln_done, inv_done, o_kept, ff_act = ev(
        "sq_done", "v_kept", "q_kept", "exp_done", "ln_done", "inv_done", "o_kept", "ff_act")
    rope_done, ss_done, ssc_done, k_kept, max_done, recip_done, pt_kept, pbt_kept, z_added, ff_dve, tables_done, xs_done, fs_done, shift_done = ev(
        "rope_done", "ss_done", "ssc_done", "k_kept", "max_done", "recip_done", "pt_kept", "pbt_kept", "z_added", "ff_dve", "tables_done", "xs_done", "fs_done", "shift_done")
    sum_done, qkr_done, pn_done, cleared = ev("sum_done", "qkr_done", "pn_done", "cleared")
    ld_wq, ld_scales, ld_wo, ld_ff, ld_tables = ev("ld_wq", "ld_scales", "ld_wo", "ld_ff", "ld_tables")
    per_slot = [qk_ready, tr_ready, s_ready, pt_ready, av_ready, sq_done, q_kept, ln_done, inv_done,
                rope_done, ss_done, ssc_done, k_kept, max_done, recip_done, pt_kept, sum_done, qkr_done, pn_done]
    per_turn = {exp_done: 2 * SLOTS, v_ready: 3 * UNITS, v_kept: 3 * UNITS, pbt_ready: UNITS, wo_ready: UNITS, o_kept: UNITS,
                pbt_kept: UNITS, z_added: UNITS, ff_mm: 9, ff_act: 7, ff_dve: 6, xs_done: 1, fs_done: 1}
    for e in per_slot:
        per_turn[e] = SLOTS
    owner = {}
    for e in (qk_ready, v_ready, tr_ready, s_ready, pt_ready, pbt_ready, av_ready, wo_ready, ff_mm):
        owner[e] = "pe"
    for e in (sq_done, v_kept, q_kept, exp_done, ln_done, inv_done, o_kept, ff_act):
        owner[e] = "act"
    for e in (rope_done, ss_done, ssc_done, k_kept, max_done, recip_done, pt_kept, pbt_kept, z_added, ff_dve, xs_done, fs_done):
        owner[e] = "dve"
    for e in (sum_done, qkr_done, pn_done):
        owner[e] = "pool"
    for e in owner:
        e.past(AHEAD)

    PJ0, PJ1, TR0, TR1, SS, PO = ps[:, 0, :], ps[:, 1, :], ps[:, 2, :], ps[:, 3, :], (4, 5), (6, 7)

    def start_ahead(eng, who):
        for e, w in owner.items():
            if w == who:
                eng.sem_inc(e.sem, AHEAD)

    def Turn(eng, l, b):
        return Counts(eng, l * BATCH + b, per_turn)

    with ExitStack() as ctx:
        sb = lambda *a: core.sb(ctx, *a)
        wq = sb("wq", [P, 2, QKV])
        wo = sb("wo", [P, INNER // P, P])
        w1 = sb("w1", [P, 2 * FF])
        w2 = sb("w2", [P, 3, P])
        ffc = sb("ffc", [P, 16])
        scales = sb("scales", [P, 2, 2, 2, HD // 2])
        base = sb("base", [P, 2, TB, 2 * HD])
        rope = sb("rope", [P, 2, TB, 2 * HD])
        bandf = sb("bandf", [P, 4 * KEYS])
        band = sb("band", [P, 4 * KEYS], BF16)
        xs = sb("xs", [P, WIN + SEQ])
        xtail = sb("xtail", [P, TB, WIN])
        sq = sb("sq", [P, 2, 512])
        ra = sb("ra", [P, 2, 512])
        rb = sb("rb", [P, 2, 512])
        qkr = sb("qkr", [P, 2, 512])
        ssq = sb("ssq", [P, 2, 8])
        inv = sb("inv", [P, 2, 8])
        qt = sb("qt", [P, 2, 256])
        kz = sb("kz", [P, 4, WIN + SEQ])
        pr = sb("pr", [P, 2, 4, KEYS])
        neg = sb("neg", [P, 2, 4])
        den = sb("den", [P, 2, 4])
        rden = sb("rden", [P, 2, 4])
        pn = sb("pn", [P, 2, 4, P])
        pb = sb("pb", [P, 2, 4, TB, WIN])
        pt = sb("pt", [P, 2, 512])
        pbt = sb("pbt", [P, 4, TB, WIN])
        quad = sb("quad", [P, TB])
        vs = sb("vs", [P, UNITS, TB, 256])
        vc = sb("vc", [P, UNITS, 256])
        ot = sb("ot", [P, 2, 512])
        fs = sb("fs", [P, SEQ])
        fc = sb("fc", [P, SEQ])
        fq = sb("fq", [P, SEQ])
        fr = sb("fr", [P, SEQ])
        fx = sb("fx", [P, SEQ])
        fh = sb("fh", [P, SEQ])
        gl = sb("gl", [P, 3, SEQ])
        fm = sb("fm", [P, 3, SEQ])
        block = ctx.enter_context(nc.Block())

        @block.sync
        def _(sp):
            sp.dma_start(base[:, 0, :, :], d["rope_straight"].rearrange("p (t c) -> p t c", t=TB)).then_inc(ld_tables.sem, 16)
            sp.dma_start(base[:, 1, :, :], d["rope_crossed"].rearrange("p (t c) -> p t c", t=TB)).then_inc(ld_tables.sem, 16)
            sp.dma_start(bandf[:, :], d["band"]).then_inc(ld_tables.sem, 16)
            sp.dma_start(quad[:, :], d["quadrant"]).then_inc(ld_tables.sem, 16)
            with sp.Fori(0, DEPTH) as l:
                turn = Turn(sp, l, 0)
                sp.wait_ge(ld_wq.sem, l * 16 + 16 + ld_wq.start)
                turn.wait(v_ready, -3 * UNITS * BATCH)
                turn.wait(qk_ready, -SLOTS * BATCH)
                sp.dma_start(wq[:, bass.ds(l % 2, 1), :], d["L0_ffn_Wqkv"][bass.ds(l, 1), :, :].rearrange("l p c -> p l c")).then_inc(ld_wq.sem, 16)
                sp.wait_ge(tables_done.sem, l * 2 + (tables_done.start + 3))
                for s, name in enumerate(("L0_ffn_q_scale", "L0_ffn_k_scale")):
                    row = d[name][bass.ds(l, 1), :]
                    for e in range(2):
                        half = row[:, e * 32:e * 32 + 32].to_broadcast([P, 32])
                        sp.dma_start(scales[:, 0, s, e, :], half).then_inc(ld_scales.sem, 16)
                        sp.dma_start(scales[:, 1, s, 1 - e, :], half).then_inc(ld_scales.sem, 16)
                turn.wait(wo_ready, 0)
                sp.dma_start(wo[:, :, :], d["L0_ffn_Wo"][bass.ds(l, 1), :, :].rearrange("l (k p) c -> p (l k) c", p=P)).then_inc(ld_wo.sem, 16)
                turn.wait(ff_dve, 6)
                sp.dma_start(w1[:, :], d["L0_ffn_W1"][bass.ds(l, 1), :, :].rearrange("l p c -> p (l c)")).then_inc(ld_ff.sem, 16)
                w2d = d["L0_ffn_W2"][bass.ds(l, 1), :, :]
                sp.dma_start(w2[:, 0:2, :], w2d[:, 0:2 * P, :].rearrange("l (k p) c -> p (l k) c", p=P)).then_inc(ld_ff.sem, 16)
                sp.dma_start(w2[0:FF_ROWS[2], 2, :], w2d[:, 2 * P:FF, :].rearrange("l p c -> p (l c)")).then_inc(ld_ff.sem, 16)
                for col, name in enumerate(("L0_ffn_ln_g", "L0_ffn_ln_b", "L0_ffn_b2")):
                    sp.dma_start(ffc[:, col:col + 1], d[name][bass.ds(l, 1), :].rearrange("l p -> p l")).then_inc(ld_ff.sem, 16)
                for half in range(2):
                    for j in range(3):
                        rows = FF_ROWS[j]
                        at = half * FF + j * P
                        sp.dma_start(ffc[0:rows, 3 + 3 * half + j:4 + 3 * half + j],
                                     d["L0_ffn_b1"][bass.ds(l, 1), at:at + rows].rearrange("l p -> p l")).then_inc(ld_ff.sem, 16)

        @block.gpsimd
        def _(pool):
            start_ahead(pool, "pool")
            pool.sem_inc(ld_wq.sem, 16)
            pool.sem_inc(ld_ff.sem, 16)
            pool.memset(w1[:, :], 0.0).then_inc(cleared.sem, 1)
            pool.memset(w2[:, :, :], 0.0).then_inc(cleared.sem, 1)
            pool.memset(ffc[:, :], 0.0).then_inc(cleared.sem, 1)
            pool.memset(kz[:, :, :], 0.0).then_inc(cleared.sem, 1)
            pool.memset(xs[:, 0:WIN + 1], 0.0).then_inc(cleared.sem, 1)
            pool.memset(fs[:, 0:1], 0.0).then_inc(cleared.sem, 1)
            pool.wait_ge(cleared.sem, cleared.at(6))

            with pool.Fori(0, DEPTH) as l:
                with pool.Fori(0, BATCH) as b:
                    turn = Turn(pool, l, b)
                    for s in range(SLOTS + 8):
                        if 4 <= s < SLOTS + 4:
                            sc = s - 4
                            g, t = divmod(sc, TB)
                            turn.wait(recip_done, sc + 1)
                            turn.wait(exp_done, 2 * sc + 2)
                            turn.wait(pt_ready, sc - 1)
                            pool.tensor_tensor(pn[:, sc % 2, :, :], pr[:, sc % 2, :, 0:P],
                                               rden[:, sc % 2, :, None].to_broadcast([P, 4, P]), ALU.mult)
                            if t == 0:
                                turn.wait(pbt_ready, g - 1)
                            pool.tensor_tensor(pb[:, g % 2, :, t, :], pr[:, sc % 2, :, P:KEYS],
                                               rden[:, sc % 2, :, None].to_broadcast([P, 4, WIN]), ALU.mult).then_inc(pn_done.sem, 1)
                        if s < SLOTS:
                            turn.wait(rope_done, s + 1)
                            pool.tensor_tensor(ra[:, s % 2, :], ra[:, s % 2, :], rb[:, s % 2, :], ALU.add).then_inc(sum_done.sem, 1)
                            turn.wait(sum_done, s + 1)
                            turn.wait(inv_done, s + 1)
                            turn.wait(tr_ready, s - 1)
                            pool.tensor_tensor(qkr[:, s % 2, :].rearrange("p (h c) -> p h c", h=8),
                                               ra[:, s % 2, :].rearrange("p (h c) -> p h c", h=8),
                                               inv[:, s % 2, :, None].to_broadcast([P, 8, HD]), ALU.mult).then_inc(qkr_done.sem, 1)

        def ff_tensor(pe, turn, step, last_row=False):
            if step == 0:
                if not last_row:
                    turn.wait(sq_done, SLOTS)
                    turn.wait(rope_done, SLOTS)
                pe.wait_ge(ld_ff.sem, (turn.turn + (BATCH - 1)) // BATCH * (16 * FF_LOADS) + (ld_ff.start + 16))
                turn.wait(fs_done, 1)
                pe.matmul(PJ0, core.mean_w[:, :], fs[:, :], start=True, stop=True).then_inc(ff_mm.sem, 1)
            if step == 1:
                turn.wait(ff_dve, 1)
                turn.wait(ff_act, 1)
                pe.matmul(PJ0, core.mean_w[:, :], fq[:, :], start=True, stop=True).then_inc(ff_mm.sem, 1)
            if 2 <= step < 5:
                j = step - 2
                rows = FF_ROWS[j]
                turn.wait(ff_act, 4 + j)
                pe.matmul(PJ0[0:rows, :], w1[:, FF + j * P:FF + j * P + rows], fh[:, :], start=True, stop=True).then_inc(ff_mm.sem, 1)
                if j > 0:
                    turn.wait(ff_dve, 2 + j)
                pe.matmul(PJ1[0:rows, :], w1[:, j * P:j * P + rows], fh[:, :], start=True, stop=True).then_inc(ff_mm.sem, 1)
            if step == 5:
                turn.wait(ff_act, 7)
                for j in range(3):
                    turn.wait(ff_dve, 3 + j)
                    last = pe.matmul(PJ0, w2[0:FF_ROWS[j], j, :], fm[0:FF_ROWS[j], j, :], start=j == 0, stop=j == 2)
                last.then_inc(ff_mm.sem, 1)

        def ff_scalar(act, turn, step):
            if step == 0:
                turn.wait(ff_dve, 1)
                act.activation(fq[:, :], fc[:, :], ACT.Square).then_inc(ff_act.sem, 1)
                turn.wait(ff_mm, 2)
                act.activation(fr[:, :], PJ0, ACT.Ln, bias=core.small[:, EPS_COL:EPS_COL + 1]).then_inc(ff_act.sem, 1)
                turn.wait(ff_act, 2)
                act.activation(fr[:, :], fr[:, :], ACT.Exp, scale=-0.5).then_inc(ff_act.sem, 1)
            if step == 1:
                turn.wait(ff_dve, 2)
                act.activation(fh[:, :], fx[:, :], ACT.Identity, scale=ffc[:, 0:1], bias=ffc[:, 1:2]).then_inc(ff_act.sem, 1)
                for j in range(3):
                    turn.wait(ff_mm, 3 + 2 * j)
                    rows = FF_ROWS[j]
                    act.activation(gl[0:rows, j, :], PJ0[0:rows, :], ACT.Gelu, bias=ffc[0:rows, 6 + j:7 + j]).then_inc(ff_act.sem, 1)
                act.preload_act_table_set("natural_log_exp_and_others")

        def ff_vector(dve, turn, step, zcol):
            if step == 0:
                turn.wait(ff_mm, 1)
                dve.tensor_tensor(fc[:, :], fs[:, :], PJ0, ALU.subtract).then_inc(ff_dve.sem, 1)
            if step == 1:
                turn.wait(ff_act, 3)
                dve.tensor_tensor(fx[:, :], fc[:, :], fr[:, :], ALU.mult).then_inc(ff_dve.sem, 1)
            if 2 <= step < 5:
                j = step - 2
                rows = FF_ROWS[j]
                turn.wait(ff_mm, 4 + 2 * j)
                turn.wait(ff_act, 5 + j)
                dve.scalar_tensor_tensor(fm[0:rows, j, :], PJ1[0:rows, :], ffc[0:rows, 3 + j:4 + j], gl[0:rows, j, :], ALU.add, ALU.mult).then_inc(ff_dve.sem, 1)
            if step == 5:
                turn.wait(ff_mm, 9)
                dve.scalar_tensor_tensor(z[:, zcol], PJ0, ffc[:, 2:3], z[:, zcol], ALU.add, ALU.add).then_inc(ff_dve.sem, 1)

        @block.tensor
        def _(pe):
            start_ahead(pe, "pe")
            pe.wait_ge(cleared.sem, cleared.at(6))
            with pe.Fori(0, DEPTH) as l:
                with pe.Fori(0, BATCH) as b:
                    turn = Turn(pe, l, b)
                    lp = l % 2
                    for s in range(SLOTS + 8):
                        g, t = divmod(s, TB)
                        if s == 0:
                            turn.wait(xs_done, 1)
                            pe.wait_ge(ld_wq.sem, l * 16 + (ld_wq.start + 32))
                            turn.wait(ff_dve, 0)
                            turn.wait(z_added, 0)
                            pe.wait_ge(tables_done.sem, tables_done.at(3))
                        if s < SLOTS:
                            turn.wait(sq_done, s)
                            turn.wait(rope_done, s)
                            rhs = wq[:, bass.ds(lp, 1), 0:2 * INNER].rearrange("p l (s c) -> p (l s) c", s=2)[:, :, g * 256:g * 256 + 256]
                            pe.matmul(PJ0.rearrange("p (s c) -> p s c", s=2), xs[:, WIN + t * P:WIN + t * P + P], rhs, start=True, stop=True).then_inc(qk_ready.sem, 1)
                        if 3 <= s < SLOTS + 3:
                            ss = s - 3
                            st = ss % TB
                            turn.wait(q_kept, ss + 1)
                            turn.wait(k_kept, ss + 1)
                            for half in range(2):
                                bank = ps[:, SS[half], :]
                                turn.wait(exp_done, 2 * ss - 1 + half)
                                pe.matmul(bank[:, 0:2 * KEYS], core.ident16[:, :], band[:, 0 if st == 0 else 2 * KEYS:][:, 0:2 * KEYS], start=True, stop=False, skip_group_check=True)
                                for hh in range(2):
                                    last = pe.matmul(bank[:, hh * KEYS:hh * KEYS + KEYS], qt[:, ss % 2, half * P:half * P + P],
                                                     kz[:, 2 * half + hh, st * P:st * P + KEYS], start=False, stop=hh == 1, skip_group_check=True)
                            last.then_inc(s_ready.sem, 1)
                        if s >= 6 and s - 6 < SLOTS and (s - 6) % TB == 3:
                            gg = (s - 6) // TB
                            turn.wait(pn_done, s - 6 + 1)
                            turn.wait(q_kept, min(s - 2, SLOTS))
                            turn.wait(k_kept, min(s - 2, SLOTS))
                            for h in range(4):
                                last = pe.matmul(TR0[:, h * WIN:h * WIN + WIN], pb[96:P, gg % 2, h, :, :].rearrange("p t c -> p (t c)"), core.ident[96:P, 96:P], start=True, stop=True)
                            last.then_inc(pbt_ready.sem, 1)
                        if s < SLOTS and t < 3:
                            if g >= 3 and t == 0:
                                turn.wait(z_added, g - 2)
                            turn.wait(v_kept, 3 * g + t)
                            wv = wq[:, bass.ds(lp, 1), 2 * INNER + g * 256:2 * INNER + g * 256 + 256].rearrange("p l c -> p (l c)")
                            if t < 2:
                                for k in range(2):
                                    tt = 2 * t + k
                                    last = pe.matmul(PJ1[:, k * 256:k * 256 + 256], xs[:, tt * P:tt * P + P], wv, start=True, stop=True)
                            else:
                                last = pe.matmul(PJ1[:, 0:256], xtail[:, :, :].rearrange("p t c -> p (t c)"), wv, start=True, stop=True)
                            last.then_inc(v_ready.sem, 1)
                        if 5 <= s < SLOTS + 5:
                            sc = s - 5
                            turn.wait(pn_done, sc + 1)
                            turn.wait(pt_kept, sc)
                            for h in range(4):
                                last = pe.transpose(TR1[:, h * P:h * P + P], pn[:, sc % 2, h, :], core.ident[:, :])
                            last.then_inc(pt_ready.sem, 1)
                        if 2 <= s < SLOTS + 2:
                            sr = s - 2
                            turn.wait(qkr_done, sr + 1)
                            turn.wait(q_kept, sr)
                            turn.wait(k_kept, sr)
                            if s >= 6:
                                turn.wait(pbt_kept, (s - 6 + 1) // TB)
                            for j in range(4):
                                last = pe.transpose(TR0[:, j * P:j * P + P], qkr[:, sr % 2, j * P:j * P + P], core.ident[:, :])
                            last.then_inc(tr_ready.sem, 1)
                        if 6 <= s < SLOTS + 6:
                            sv = s - 6
                            gg, tt = divmod(sv, TB)
                            turn.wait(pt_kept, sv + 1)
                            turn.wait(v_kept, 3 * gg + (3 if tt == 3 else tt // 2 + 1))
                            if tt == 0:
                                turn.wait(o_kept, gg)
                            for h in range(4):
                                half = 64 * (h % 2)
                                last = pe.matmul(ps[half:half + 64, PO[h // 2], tt * P:tt * P + P], vs[:, gg, tt, h * HD:h * HD + HD],
                                                 pt[:, sv % 2, h * P:h * P + P], start=tt == 0, stop=False, skip_group_check=True)
                            if tt == 3:
                                turn.wait(pbt_kept, gg + 1)
                                for h in range(4):
                                    half = 64 * (h % 2)
                                    ends = ps[half:half + 64, PO[h // 2], :].rearrange("p (t c) -> p t c", t=TB)[:, :, P - WIN:]
                                    last = pe.matmul(ends, vc[:, gg, h * HD:h * HD + HD], pbt[:, h, :, :], start=False, stop=True, skip_group_check=True)
                            last.then_inc(av_ready.sem, 1)
                        if s >= 11 and (s - 11) % 4 == 0:
                            gg = (s - 11) // 4
                            turn.wait(o_kept, gg + 1)
                            if gg == 0:
                                pe.wait_ge(ld_wo.sem, l * 16 + (ld_wo.start + 16))
                            if s < SLOTS:
                                turn.wait(v_kept, 3 * g + 3)
                            else:
                                turn.wait(z_added, gg)
                                turn.wait(ff_dve, {19: 3, 23: 5}[s])
                            for k in range(2):
                                last = pe.matmul(PJ1, wo[:, 2 * gg + k, :], ot[:, k, :], start=k == 0, stop=k == 1)
                            last.then_inc(wo_ready.sem, 1)
                        if s == 16:
                            ff_tensor(pe, turn, 0)
                        if s == 17:
                            ff_tensor(pe, turn, 1)
                        if s in (18, 20, 21):
                            if s == 18:
                                turn.wait(z_added, 2)
                            if s == 20:
                                turn.wait(z_added, 3)
                            ff_tensor(pe, turn, {18: 2, 20: 3, 21: 4}[s])
                        if s == 22:
                            ff_tensor(pe, turn, 5)
            turn = Turn(pe, DEPTH, 0)
            turn.wait(z_added, 0)
            for step in range(6):
                ff_tensor(pe, turn, step, last_row=True)

        @block.scalar
        def _(act):
            start_ahead(act, "act")
            act.preload_act_table_set("natural_log_exp_and_others")
            with act.Fori(0, DEPTH) as l:
                with act.Fori(0, BATCH) as b:
                    turn = Turn(act, l, b)
                    for s in range(SLOTS + 8):
                        g, t = divmod(s, TB)
                        if s < SLOTS:
                            turn.wait(qk_ready, s + 1)
                            turn.wait(ss_done, s - 1)
                            act.activation(sq[:, s % 2, :], PJ0, ACT.Square).then_inc(sq_done.sem, 1)
                        if 3 <= s < SLOTS + 3:
                            ss = s - 3
                            turn.wait(max_done, ss + 1)
                            turn.wait(pn_done, ss - 1)
                            turn.wait(recip_done, ss - 1)
                            for h in range(4):
                                last = act.activation(pr[:, ss % 2, h, :], ps[:, SS[h // 2], (h % 2) * KEYS:(h % 2) * KEYS + KEYS], ACT.Exp,
                                                      bias=neg[:, ss % 2, h:h + 1], accum_out=den[:, ss % 2, h:h + 1])
                                if h % 2:
                                    last.then_inc(exp_done.sem, 1)
                        if s < SLOTS:
                            turn.wait(ssc_done, s + 1)
                            turn.wait(qkr_done, s - 1)
                            act.activation(inv[:, s % 2, :], ssq[:, s % 2, :], ACT.Ln, scale=NORM_SCALE).then_inc(ln_done.sem, 1)
                            turn.wait(ln_done, s + 1)
                            act.activation(inv[:, s % 2, :], inv[:, s % 2, :], ACT.Exp, scale=-0.5, bias=core.small[:, LN_UP_COL:LN_UP_COL + 1]).then_inc(inv_done.sem, 1)
                            if t < 3:
                                turn.wait(v_ready, 3 * g + t + 1)
                                if t < 2:
                                    act.activation(vs[:, g, 2 * t:2 * t + 2, :], PJ1.rearrange("p (t c) -> p t c", t=2), ACT.Copy).then_inc(v_kept.sem, 1)
                                else:
                                    act.activation(vc[:, g, :], PJ1[:, 0:256], ACT.Copy).then_inc(v_kept.sem, 1)
                        if 2 <= s < SLOTS + 2:
                            sr = s - 2
                            turn.wait(tr_ready, sr + 1)
                            turn.wait(s_ready, sr - 1)
                            act.activation(qt[:, sr % 2, :], TR0[:, 0:256], ACT.Copy).then_inc(q_kept.sem, 1)
                        if s >= 6 and s - 6 < SLOTS and (s - 6) % TB == 3:
                            gg = (s - 6) // TB
                            turn.wait(av_ready, s - 6 + 1)
                            turn.wait(wo_ready, gg)
                            act.activation(ot[:, :, :], ps[:, PO[0]:PO[1] + 1, :], ACT.Copy).then_inc(o_kept.sem, 1)
                        if s == 17:
                            ff_scalar(act, turn, 0)
                        if s == 19:
                            ff_scalar(act, turn, 1)
            turn = Turn(act, DEPTH, 0)
            ff_scalar(act, turn, 0)
            ff_scalar(act, turn, 1)

        def shifted(dve, to, at, row, sem):
            col = row * SEQ
            dve.tensor_scalar(to[0:64, at:at + SEQ], z[0:64, bass.ds(col, SEQ)], 1.0, None, ALU.mult)
            dve.tensor_scalar(to[64:P, at + 1:at + SEQ], z[64:P, bass.ds(col, SEQ - 1)], 1.0, None, ALU.mult).then_inc(sem, 1)

        def tails(dve):
            dve.tensor_copy(xtail[:, :, :], xs[:, WIN:].rearrange("p (t c) -> p t c", t=TB)[:, :, P - WIN:]).then_inc(xs_done.sem, 1)

        @block.vector
        def _(dve):
            start_ahead(dve, "dve")
            dve.wait_ge(cleared.sem, cleared.at(6))
            shifted(dve, xs, WIN, 0, shift_done.sem)
            dve.wait_ge(shift_done.sem, shift_done.at(1))
            tails(dve)
            dve.sem_inc(tables_done.sem, 2)
            dve.wait_ge(ld_tables.sem, ld_tables.at(64))
            dve.tensor_copy(band[:, :], bandf[:, :]).then_inc(tables_done.sem, 1)
            with dve.Fori(0, DEPTH) as l:
                dve.wait_ge(ld_scales.sem, l * 128 + (ld_scales.start + 128))
                for k in range(2):
                    dve.tensor_tensor(rope[:, k, :, :], base[:, k, :, :],
                                      scales[:, k, :, :, :].rearrange("p s e c -> p (s e c)")[:, None, :].to_broadcast([P, TB, 2 * HD]), ALU.mult).then_inc(tables_done.sem, 1)
                with dve.Fori(0, BATCH) as b:
                    turn = Turn(dve, l, b)
                    before = ((b + (BATCH - 1)) % BATCH) * SEQ
                    for s in range(SLOTS + 8):
                        g, t = divmod(s, TB)
                        if s == 0:
                            dve.wait_ge(tables_done.sem, l * 2 + (tables_done.start + 5))
                        if s < SLOTS:
                            turn.wait(sq_done, s + 1)
                            turn.wait(qkr_done, s - 1)
                            both = PJ0.rearrange("p (s h c) -> p s h c", s=2, h=4)
                            table = lambda k: rope[:, k, t, :].rearrange("p (s c) -> p s c", s=2)[:, :, None, :].to_broadcast([P, 2, 4, HD])
                            dve.tensor_tensor(ra[:, s % 2, :].rearrange("p (s h c) -> p s h c", s=2, h=4), both, table(0), ALU.mult)
                            halves = PJ0.rearrange("p (s h e c) -> p s h e c", s=2, h=4, e=2)[:, :, :, ::-1, :]
                            tableh = rope[:, 1, t, :].rearrange("p (s e c) -> p s e c", s=2, e=2)[:, :, None, :, :].to_broadcast([P, 2, 4, 2, HD // 2])
                            dve.tensor_tensor(rb[:, s % 2, :].rearrange("p (s h e c) -> p s h e c", s=2, h=4, e=2), halves, tableh, ALU.mult).then_inc(rope_done.sem, 1)
                            turn.wait(inv_done, s - 1)
                            dve.tensor_reduce(ssq[:, s % 2, :], sq[:, s % 2, :].rearrange("p (h c) -> p h c", h=8), AX.X, ALU.add).then_inc(ss_done.sem, 1)
                            turn.wait(ss_done, s + 1)
                            dve.tensor_scalar(ssq[:, s % 2, :], ssq[:, s % 2, :], 1e-24, None, ALU.max).then_inc(ssc_done.sem, 1)
                        if 3 <= s < SLOTS + 3:
                            ss = s - 3
                            turn.wait(s_ready, ss + 1)
                            turn.wait(exp_done, 2 * ss - 2)
                            scores = ps[:, SS[0]:SS[1] + 1, 0:2 * KEYS].rearrange("p a (h c) -> p a h c", h=2)
                            dve.tensor_reduce(neg[:, ss % 2, :].rearrange("p (a h) -> p a h", a=2), scores, AX.X, ALU.max, negate=True).then_inc(max_done.sem, 1)
                        if s >= 6 and s - 6 < SLOTS and (s - 6) % TB == 3:
                            gg = (s - 6) // TB
                            turn.wait(pbt_ready, gg + 1)
                            turn.wait(av_ready, 4 * gg)
                            dve.tensor_tensor(pbt[:, :, :, :], TR0[:, 0:4 * WIN].rearrange("p (h c) -> p h c", h=4)[:, :, None, :].to_broadcast([P, 4, TB, WIN]),
                                              quad[:, None, :, None].to_broadcast([P, 4, TB, WIN]), ALU.mult).then_inc(pbt_kept.sem, 1)
                        if 5 <= s < SLOTS + 5:
                            sc = s - 5
                            turn.wait(pt_ready, sc + 1)
                            turn.wait(av_ready, sc - 1)
                            dve.tensor_copy(pt[:, sc % 2, :], TR1).then_inc(pt_kept.sem, 1)
                        if 2 <= s < SLOTS + 2:
                            sr = s - 2
                            st = sr % TB
                            turn.wait(q_kept, sr + 1)
                            turn.wait(s_ready, sr - 2)
                            for e in range(2):
                                rows = slice(64 * e, 64 * e + 64)
                                last = dve.tensor_copy(kz[rows, e::2, WIN + st * P:WIN + st * P + P], TR0[rows, 256:512].rearrange("p (k c) -> p k c", k=2))
                            last.then_inc(k_kept.sem, 1)
                        if 3 <= s < SLOTS + 3:
                            turn.wait(exp_done, 2 * ss + 2)
                            turn.wait(pn_done, ss - 1)
                            dve.reciprocal(rden[:, ss % 2, :], den[:, ss % 2, :]).then_inc(recip_done.sem, 1)
                        if s >= 11 and (s - 11) % 4 == 0:
                            gg = (s - 11) // 4
                            turn.wait(z_added, gg)
                            turn.wait(wo_ready, gg + 1)
                            dve.tensor_tensor(z[:, bass.ds(b * SEQ, SEQ)], z[:, bass.ds(b * SEQ, SEQ)], PJ1, ALU.add).then_inc(z_added.sem, 1)
                        if s == 12:
                            turn.wait(z_added, 0)
                            turn.wait(ff_mm, 0)
                            shifted(dve, fs, 0, (b + (BATCH - 1)) % BATCH, fs_done.sem)
                        if s == 17:
                            turn.wait(v_ready, 3 * UNITS)
                            turn.wait(qk_ready, SLOTS)
                            shifted(dve, xs, WIN, (b + 1) % BATCH, shift_done.sem)
                            dve.wait_ge(shift_done.sem, turn.turn + (shift_done.start + 2))
                            tails(dve)
                        if s == 16:
                            ff_vector(dve, turn, 0, None)
                        if s == 17:
                            ff_vector(dve, turn, 1, None)
                        if s in (18, 20, 21):
                            ff_vector(dve, turn, {18: 2, 20: 3, 21: 4}[s], None)
                        if s == 22:
                            ff_vector(dve, turn, 5, bass.ds(before, SEQ))
            turn = Turn(dve, DEPTH, 0)
            turn.wait(z_added, 0)
            shifted(dve, fs, 0, BATCH - 1, fs_done.sem)
            for step in range(6):
                ff_vector(dve, turn, step, slice((BATCH - 1) * SEQ, BATCH * SEQ))

    turns = DEPTH * BATCH
    for e, k in per_turn.items():
        e.past(turns * k + (k if e in (ff_mm, ff_act, ff_dve, xs_done, fs_done) else 0))
    shift_done.past(1 + turns)
    tables_done.past(3 + 2 * DEPTH)
    cleared.past(6)
    ld_wq.past(16 + 16 * DEPTH)
    ld_scales.past(128 * DEPTH)
    ld_wo.past(16 * DEPTH)
    ld_ff.past(16 + 16 * FF_LOADS * DEPTH)
    ld_tables.past(64)


def swiglu(core, first):
    nc, d, x, z, ps = core.nc, core.d, core.x, core.z, core.ps
    ld_w, floated, scaled, turned, kept = core.events("sw_ld", "sw_floated", "sw_scaled", "sw_turned", "sw_kept")
    gate_mm, up_mm, y_mm, silu_done, h_done, added = core.events("sw_gate", "sw_up", "sw_y", "sw_silu", "sw_h", "sw_added")
    T = 3
    per_turn = {gate_mm: T, up_mm: T, silu_done: T, h_done: T, y_mm: 1, added: 1}
    if first:
        core.sw = core.sb(core.ctx, "sw", [P, 3, T, P])
    w = core.sw
    if first:
        with ExitStack() as ctx:
            wi = core.sb(ctx, "wi", [P, 3, T, P], I32)
            wf = core.sb(ctx, "wf", [P, 3, T, P])
            block = ctx.enter_context(nc.Block())

            @block.sync
            def _(sp):
                sp.dma_start(wi[:, 0, :, :], d["L1_ffn_w_gate"].rearrange("(t p) c -> p t c", p=P)).then_inc(ld_w.sem, 16)
                sp.dma_start(wi[:, 1, :, :], d["L1_ffn_w_up"].rearrange("(t p) c -> p t c", p=P)).then_inc(ld_w.sem, 16)
                sp.dma_start(wi[:, 2, :, :], d["L1_ffn_w_down"].rearrange("p (t c) -> p t c", c=P)).then_inc(ld_w.sem, 16)

            @block.vector
            def _(dve):
                dve.wait_ge(ld_w.sem, 48)
                dve.tensor_copy(wf[:, :, :, :], wi[:, :, :, :]).then_inc(floated.sem, 1)
                dve.wait_ge(floated.sem, 1)
                dve.tensor_scalar(wf[:, :, :, :], wf[:, :, :, :], float(np.float32(1.0 / 127.0)), None, ALU.mult).then_inc(scaled.sem, 1)
                for k in range(3):
                    dve.wait_ge(turned.sem, k + 1)
                    dve.tensor_copy(w[:, k, :, :], ps[:, k, 0:T * P].rearrange("p (t c) -> p t c", t=T)).then_inc(kept.sem, 1)

            @block.tensor
            def _(pe):
                pe.wait_ge(scaled.sem, 1)
                for k in range(3):
                    for t in range(T):
                        last = pe.transpose(ps[:, k, t * P:t * P + P], wf[:, k, t, :], core.ident[:, :])
                    last.then_inc(turned.sem, 1)

    for e in per_turn:
        e.past(AHEAD)
    with ExitStack() as ctx:
        sg = core.sb(ctx, "sg", [P, T, SEQ])
        sh = core.sb(ctx, "sh", [P, T, SEQ])
        block = ctx.enter_context(nc.Block())

        @block.tensor
        def _(pe):
            for e in (gate_mm, up_mm, y_mm):
                pe.sem_inc(e.sem, AHEAD)
            with pe.Fori(0, BATCH) as b:
                turn = Counts(pe, b, per_turn)
                zb = z[:, bass.ds(b * SEQ, SEQ)]
                for t in range(T):
                    turn.wait(silu_done, t + 1 - T)
                    pe.matmul(ps[:, t, :], w[:, 0, t, :], zb, start=True, stop=True).then_inc(gate_mm.sem, 1)
                    turn.wait(h_done, t + 1 - T)
                    pe.matmul(ps[:, T + t, :], w[:, 1, t, :], zb, start=True, stop=True).then_inc(up_mm.sem, 1)
                turn.wait(added, 0)
                for t in range(T):
                    turn.wait(h_done, t + 1)
                    last = pe.matmul(ps[:, 2 * T, :], w[:, 2, t, :], sh[:, t, :], start=t == 0, stop=t == T - 1)
                last.then_inc(y_mm.sem, 1)

        @block.scalar
        def _(act):
            act.sem_inc(silu_done.sem, AHEAD)
            act.preload_act_table(ACT.Silu)
            with act.Fori(0, BATCH) as b:
                turn = Counts(act, b, per_turn)
                for t in range(T):
                    turn.wait(gate_mm, t + 1)
                    turn.wait(h_done, t + 1 - T)
                    act.activation(sg[:, t, :], ps[:, t, :], ACT.Silu).then_inc(silu_done.sem, 1)

        @block.vector
        def _(dve):
            dve.sem_inc(h_done.sem, AHEAD)
            dve.sem_inc(added.sem, AHEAD)
            with dve.Fori(0, BATCH) as b:
                turn = Counts(dve, b, per_turn)
                for t in range(T):
                    turn.wait(y_mm, 0)
                    turn.wait(up_mm, t + 1)
                    turn.wait(silu_done, t + 1)
                    dve.tensor_tensor(sh[:, t, :], sg[:, t, :], ps[:, T + t, :], ALU.mult).then_inc(h_done.sem, 1)
                turn.wait(y_mm, 1)
                xb = x[:, bass.ds(b * SEQ, SEQ)]
                dve.tensor_tensor(xb, xb, ps[:, 2 * T, :], ALU.add).then_inc(added.sem, 1)
    for e, k in per_turn.items():
        e.past(BATCH * k)


PARTS = 3
STACK = PARTS * PARTS * SD
M_ROW = 96


def load_output_weights(core, sp, wp, w, sem):
    rows = w.rearrange("(g j c) m -> j c g m", g=SG, j=4)
    for j in range(4):
        sp.dma_start(wp[32 * j:32 * j + SD, :, :], rows[j]).then_inc(sem, 16)


def small_attention(core, kind):
    nc, d, x, z, ps = core.nc, core.d, core.x, core.z, core.ps
    causal = kind != "norm"
    ev = core.events
    scale = float(SD) ** -0.5
    n = "L0_attn_a" if kind == "norm" else "L0_attn_b" if kind == "latent" else "L1_attn_b"
    if causal:
        part = {j: (off, SEQ - P * j) for j, off in enumerate((0, 512, 1024, 896))}
        halves = [((0, 0, 0), (1, 1, 0), (3, 1, 384)), ((2, 2, 0),)]
        spans = [(0, 2, 0, 1024), (2, 1, 1024, 256)]
    else:
        part = {j: (512 * j, SEQ) for j in range(TB)}
        halves = [((0, 0, 0), (1, 1, 0)), ((2, 2, 0), (3, 3, 0))]
        spans = [(0, 2, 0, 1024), (2, 2, 1024, 1024)]
    width = 1280 if causal else 2048

    ld_w, prep_dve, prep_pe, prep_pool = ev("sa_ld_w", "sa_prep_dve", "sa_prep_pe", "sa_prep_pool")
    proj_mm, s_mm, mt_mm, st_mm, av_mm, sum_mm, y_mm = ev(
        "sa_proj_mm", "sa_s_mm", "sa_mt_mm", "sa_st_mm", "sa_av_mm", "sa_sum_mm", "sa_y_mm")
    proj_act, exp_done, out_kept, ln_done, recip_done = ev(
        "sa_proj_act", "sa_exp_done", "sa_out_kept", "sa_ln_done", "sa_recip_done")
    row_kept, v_kept, qk_normed, cut_done, max_done, mcut_done, out_normed, added = ev(
        "sa_row_kept", "sa_v_kept", "sa_qk_normed", "sa_cut_done", "sa_max_done", "sa_mcut_done", "sa_out_normed", "sa_added")
    ld_stack, ld_m = ev("sa_ld_stack", "sa_ld_m")
    n_mm = {"norm": 2, "latent": 2, "plain": 1}[kind]
    n_act = {"norm": 4, "latent": 2, "plain": 1}[kind]
    owner = {
        "pe": {proj_mm: n_mm, s_mm: SH, mt_mm: 1, st_mm: 2 * SH, av_mm: SG, sum_mm: SG, y_mm: 1},
        "act": {proj_act: n_act, exp_done: 2 * SH, out_kept: SG, ln_done: SG, recip_done: SG},
        "dve": {row_kept: 1, v_kept: 1, qk_normed: 1, cut_done: 5, max_done: SH, mcut_done: 6, out_normed: SG, added: 1},
    }
    if kind != "norm":
        del owner["dve"][qk_normed]
    per_turn = {e: k for es in owner.values() for e, k in es.items()}
    for e in per_turn:
        e.past(AHEAD)
    loads = 2 * PARTS * PARTS
    per_turn[ld_stack] = 16 * loads
    per_turn[ld_m] = 16 * PARTS

    with ExitStack() as ctx:
        sb = lambda *a: core.sb(ctx, *a)
        w = sb("w", [P, 3, P])
        wp = sb("wp", [P, SG, P])
        gb = sb("gb", [P, 4])
        sums = sb("sums", [P, P])
        mean8 = sb("mean8", [P, P])
        cmask = sb("cmask", [P, P], BF16)
        qs = sb("qs", [P, SH, SEQ], BF16)
        ks = sb("ks", [P, SH, SEQ], BF16)
        va = sb("va", [P, TB, SH, 32])
        hb = sb("hb", [P, SEQ])
        xf = sb("xf", [P, 2, SEQ])
        x1 = sb("x1", [P, 2, SEQ])
        cut = sb("cut", [P, PARTS, 2, SEQ], BF16)
        nm = sb("nm", [P, SH, TB])
        mf = sb("mf", [64, P])
        m1 = sb("m1", [64, P])
        mcut = sb("mcut", [64, PARTS, P], BF16)
        pt = sb("pt", [P, 2, 4, width])
        ou = sb("ou", [P, 2, SEQ])
        rr = sb("rr", [P, 2, SEQ])
        on = sb("on", [P, 2, SEQ])

        with ExitStack() as prep:
            tmp = core.sb(prep, "tmp", [P, 4, P])
            mean = core.sb(prep, "mean", [P, 2, SH])
            block = prep.enter_context(nc.Block())
            @block.gpsimd
            def _(pool):
                pool.memset(wp[:, :, :], 0.0).then_inc(prep_pool.sem, 1)
                pool.memset(va[:, :, :, :], 0.0).then_inc(prep_pool.sem, 1)
                pool.memset(qs[:, :, :], 0.0).then_inc(prep_pool.sem, 1)
                pool.memset(ks[:, :, :], 1.0).then_inc(prep_pool.sem, 1)
                pool.memset(tmp[:, 3, :], 0.0).then_inc(prep_pool.sem, 1)
                pool.wait_ge(prep_pool.sem, prep_pool.at(5))
                pool.memset(va[:, :, :, SD:SD + 1], 1.0).then_inc(prep_pool.sem, 1)

            @block.sync
            def _(sp):
                sp.dma_start(sums[:, :], d["sum_rows"]).then_inc(ld_w.sem, 16)
                if kind == "norm":
                    sp.dma_start(mean8[:, :], d["mean_of_8"]).then_inc(ld_w.sem, 16)
                    sp.dma_start(tmp[:, 0:3, :], d[f"{n}_w_qkv"].rearrange("p (s c) -> p s c", s=3)).then_inc(ld_w.sem, 16)
                    for col, name in enumerate(("q_gamma", "q_beta", "k_gamma", "k_beta")):
                        for c in range(SD):
                            sp.dma_start(gb[SH * c:SH * c + SH, col:col + 1], d[f"{n}_{name}"][c:c + 1].rearrange("(a c) -> a c", a=1).to_broadcast([SH, 1])).then_inc(ld_w.sem, 16)
                elif kind == "latent":
                    sp.dma_start(tmp[:, 0, :], d["causal"]).then_inc(ld_w.sem, 16)
                    sp.dma_start(w[:, 0, 0:32], d[f"{n}_W_dq"]).then_inc(ld_w.sem, 16)
                    sp.dma_start(w[:, 0, 32:64], d[f"{n}_W_dkv"]).then_inc(ld_w.sem, 16)
                    sp.dma_start(tmp[0:32, 1, :], d[f"{n}_W_uq"]).then_inc(ld_w.sem, 16)
                    sp.dma_start(tmp[0:32, 2, :], d[f"{n}_W_uk"]).then_inc(ld_w.sem, 16)
                    sp.dma_start(mean8[0:32, :], d[f"{n}_W_uv"]).then_inc(ld_w.sem, 16)
                else:
                    sp.dma_start(mean8[:, :], d["causal"]).then_inc(ld_w.sem, 16)
                    sp.dma_start(tmp[:, 0:3, :], d[f"{n}_w_qkv"].rearrange("s h c m -> (h c) s m")).then_inc(ld_w.sem, 16)
                    sp.dma_start(rr[:, 0, 0:P], d[f"{n}_w_o"]).then_inc(ld_w.sem, 16)
                sp.wait_ge(prep_pool.sem, prep_pool.at(1))
                if kind != "plain":
                    load_output_weights(core, sp, wp, d[f"{n}_w_proj" if kind == "norm" else f"{n}_W_o"], ld_w.sem)

            by_channel = lambda a: a.rearrange("p s (c h) -> p s h c", h=SH)
            n_ld = {"norm": 3 + 4 * SD + 4, "latent": 7 + 4, "plain": 4}[kind]

            @block.vector
            def _(dve):
                dve.wait_ge(ld_w.sem, ld_w.at(16 * n_ld))
                if kind == "norm":
                    heads = tmp[:, 0:2, :].rearrange("p s (h c) -> p s h c", c=SD)
                    dve.tensor_reduce(mean[:, :, :], heads, AX.X, ALU.add).then_inc(prep_dve.sem, 1)
                    dve.wait_ge(prep_dve.sem, prep_dve.at(1))
                    dve.tensor_scalar(mean[:, :, :], mean[:, :, :], 1.0 / SD, None, ALU.mult).then_inc(prep_dve.sem, 1)
                    dve.wait_ge(prep_dve.sem, prep_dve.at(2))
                    dve.tensor_tensor(by_channel(w[:, 0:2, :]), heads, mean[:, :, :, None].to_broadcast([P, 2, SH, SD]), ALU.subtract).then_inc(prep_dve.sem, 1)
                    dve.tensor_copy(w[:, 2, :], tmp[:, 2, :])
                    dve.tensor_scalar(gb[:, 0:2], gb[:, 0:2], scale, None, ALU.mult).then_inc(prep_dve.sem, 1)
                elif kind == "latent":
                    dve.tensor_copy(by_channel(w[0:32, 1:3, :]), tmp[0:32, 1:3, :].rearrange("p s (h c) -> p s h c", c=SD))
                    dve.tensor_copy(cmask[:, :], tmp[:, 0, :]).then_inc(prep_dve.sem, 1)
                else:
                    dve.tensor_copy(cmask[:, :], mean8[:, :]).then_inc(prep_dve.sem, 1)
                    dve.wait_ge(prep_pool.sem, prep_pool.at(5))
                    for g in range(SG):
                        if g:
                            dve.wait_ge(prep_pe.sem, prep_pe.at(1 + g))
                        dve.tensor_copy(tmp[:, 3, :].rearrange("p (j c) -> p j c", j=4)[:, :, 0:SD],
                                        rr[:, 0, g * 32:g * 32 + 32].rearrange("p (j c) -> p j c", j=4)).then_inc(prep_dve.sem, 1)
                    dve.wait_ge(prep_pe.sem, prep_pe.at(5))
                    dve.tensor_copy(by_channel(w[:, 0:2, :]), ps[:, 0, 0:2 * P].rearrange("p (s h c) -> p s h c", s=2, c=SD))
                    dve.tensor_copy(w[:, 2, :], ps[:, 0, 2 * P:3 * P])
                    dve.tensor_copy(wp[:, :, :], ps[:, 1, :].rearrange("p (g c) -> p g c", g=SG)).then_inc(prep_dve.sem, 1)

            if kind == "plain":
                @block.tensor
                def _(pe):
                    pe.wait_ge(ld_w.sem, ld_w.at(16 * n_ld))
                    for s in range(3):
                        last = pe.transpose(ps[:, 0, s * P:s * P + P], tmp[:, s, :], core.ident[:, :])
                    last.then_inc(prep_pe.sem, 1)
                    for g in range(SG):
                        pe.wait_ge(prep_dve.sem, prep_dve.at(2 + g))
                        pe.transpose(ps[:, 1, g * P:g * P + P], tmp[:, 3, :], core.ident[:, :]).then_inc(prep_pe.sem, 1)
            ld_w.past(16 * n_ld)
            prep_dve.past({"norm": 4, "latent": 1, "plain": 6}[kind])
            prep_pe.past(5 if kind == "plain" else 0)
            prep_pool.past(6)

        block = ctx.enter_context(nc.Block())

        @block.sync
        def _(sp):
            with sp.Fori(0, BATCH) as b:
                turn = Counts(sp, b, per_turn)
                turn.wait(cut_done, 5)
                turn.wait(st_mm, 0)
                for c in range(PARTS * PARTS):
                    rows = slice(SD * c, SD * c + SD)
                    for to, s, p in ((qs, 0, c // PARTS), (ks, 1, c % PARTS)):
                        sp.dma_start(to[rows, :, :], cut[:, p, s, :]).then_inc(ld_stack.sem, 16)
                turn.wait(mcut_done, 6)
                for c in range(PARTS):
                    sp.dma_start(qs[M_ROW + c:M_ROW + c + 1, :, :].rearrange("o h (i t) -> o (h i) t", i=TB), mcut[:, c, :]).then_inc(ld_m.sem, 16)

        @block.tensor
        def _(pe):
            for e in owner["pe"]:
                pe.sem_inc(e.sem, AHEAD)
            with pe.Fori(0, BATCH) as b:
                turn = Counts(pe, b, per_turn)
                turn.wait(added, 0)
                turn.wait(row_kept, 1)
                if kind == "latent":
                    pe.matmul(ps[0:32, 0, :], w[:, 0, 0:32], hb[:, :], start=True, stop=True)
                    pe.matmul(ps[0:32, 1, :], w[:, 0, 32:64], hb[:, :], start=True, stop=True).then_inc(proj_mm.sem, 1)
                    turn.wait(proj_act, 1)
                    pe.matmul(ps[:, 4, :], w[0:32, 1, :], xf[0:32, 0, :], start=True, stop=True)
                    pe.matmul(ps[:, 5, :], w[0:32, 2, :], xf[0:32, 1, :], start=True, stop=True)
                    for t in range(TB):
                        last = pe.matmul(ps[:, 3, t * P:t * P + P], xf[0:32, 1, t * P:t * P + P], mean8[0:32, :], start=True, stop=True)
                    last.then_inc(proj_mm.sem, 1)
                else:
                    for s in range(2):
                        pe.matmul(ps[:, s, :], w[:, s, :], hb[:, :], start=True, stop=True)
                    for t in range(TB):
                        last = pe.matmul(ps[:, 3, t * P:t * P + P], hb[:, t * P:t * P + P], w[:, 2, :], start=True, stop=True)
                    last.then_inc(proj_mm.sem, 1)
                if kind == "norm":
                    turn.wait(proj_act, 1)
                    for s in range(2):
                        last = pe.matmul(ps[:, 4 + s, :], mean8[:, :], x1[:, s, :], start=True, stop=True)
                    last.then_inc(proj_mm.sem, 1)
                turn.wait(v_kept, 1)
                turn.wait(ld_stack, 16 * loads)
                for h in range(SH):
                    turn.wait(max_done, h - 1)
                    for i in range(TB):
                        bank = ps[:, 4 * (h % 2) + i, :]
                        keys = P * (i + 1) if causal else SEQ
                        if causal:
                            pe.matmul(bank[:, i * P:i * P + P], core.ident16[:, :], cmask[:, :], start=True, stop=False, skip_group_check=True)
                        last = pe.matmul(bank[:, 0:keys], qs[0:STACK, h, i * P:i * P + P], ks[0:STACK, h, 0:keys],
                                         start=not causal, stop=True, skip_group_check=True)
                    last.then_inc(s_mm.sem, 1)
                turn.wait(max_done, SH)
                pe.matmul(ps[0:64, 0, 0:P], nm[:, :, :].rearrange("p h i -> p (h i)"), core.ident[:, :], start=True, stop=True).then_inc(mt_mm.sem, 1)
                turn.wait(ld_m, 16 * PARTS)
                turn.wait(mcut_done, 1)
                for g in range(SG + 3):
                    if g < SG:
                        for h in range(4 * g, 4 * g + 4):
                            for half in range(2):
                                turn.wait(exp_done, 2 * h + half - 1)
                                for j, bank, col in halves[half]:
                                    q0 = P * j if causal else 0
                                    cols = part[j][1]
                                    if causal:
                                        pe.matmul(ps[:, bank, col:col + P], cmask[:, :], core.ident16[:, :], start=True, stop=False, skip_group_check=True)
                                    last = pe.matmul(ps[:, bank, col:col + cols], ks[0:M_ROW + PARTS, h, j * P:j * P + P],
                                                     qs[0:M_ROW + PARTS, h, q0:SEQ], start=not causal, stop=True, skip_group_check=True)
                                last.then_inc(st_mm.sem, 1)
                    if 1 <= g < SG + 1:
                        gg = g - 1
                        turn.wait(exp_done, 8 * gg + 8)
                        turn.wait(out_kept, gg - 1)
                        for j in range(TB):
                            off, cols = part[j]
                            for hh in range(4):
                                last = pe.matmul(ps[32 * hh:32 * hh + 32, 4 + gg % 2, SEQ - cols:SEQ], va[:, j, 4 * gg + hh, :],
                                                 pt[:, gg % 2, hh, off:off + cols], start=j == 0, stop=j == TB - 1, skip_group_check=True)
                        last.then_inc(av_mm.sem, 1)
                    if 2 <= g < SG + 2:
                        gg = g - 2
                        turn.wait(out_kept, gg + 1)
                        turn.wait(ln_done, gg)
                        pe.matmul(ps[:, 6, :], sums[:, :], ou[:, gg % 2, :], start=True, stop=True).then_inc(sum_mm.sem, 1)
                    if 3 <= g:
                        gg = g - 3
                        turn.wait(out_normed, gg + 1)
                        last = pe.matmul(ps[:, 7, :], wp[:, gg, :], on[:, gg % 2, :], start=gg == 0, stop=gg == SG - 1)
                last.then_inc(y_mm.sem, 1)

        @block.scalar
        def _(act):
            for e in owner["act"]:
                act.sem_inc(e.sem, AHEAD)
            act.preload_act_table_set("natural_log_exp_and_others")
            with act.Fori(0, BATCH) as b:
                turn = Counts(act, b, per_turn)
                if kind == "norm":
                    turn.wait(proj_mm, 1)
                    turn.wait(cut_done, 0)
                    act.activation(x1[:, :, :], ps[:, 0:2, :], ACT.Square).then_inc(proj_act.sem, 1)
                    turn.wait(proj_mm, 2)
                    act.activation(xf[:, :, :], ps[:, 4:6, :], ACT.Ln, bias=core.small[:, EPS_COL:EPS_COL + 1]).then_inc(proj_act.sem, 1)
                    turn.wait(proj_act, 2)
                    act.activation(xf[:, :, :], xf[:, :, :], ACT.Exp, scale=-0.5).then_inc(proj_act.sem, 1)
                    turn.wait(qk_normed, 1)
                    for s in range(2):
                        last = act.activation(xf[:, s, :], x1[:, s, :], ACT.Identity, scale=gb[:, 2 * s:2 * s + 1], bias=gb[:, 2 * s + 1:2 * s + 2])
                    last.then_inc(proj_act.sem, 1)
                if kind == "latent":
                    turn.wait(proj_mm, 1)
                    turn.wait(cut_done, 0)
                    act.activation(xf[0:32, :, :], ps[0:32, 0:2, :], ACT.Copy).then_inc(proj_act.sem, 1)
                if kind != "norm":
                    b0 = 4 if kind == "latent" else 0
                    turn.wait(proj_mm, n_mm)
                    turn.wait(cut_done, 0)
                    act.activation(xf[:, 0, :], ps[:, b0, :], ACT.Copy, scale=scale)
                    act.activation(xf[:, 1, :], ps[:, b0 + 1, :], ACT.Copy).then_inc(proj_act.sem, 1)
                for g in range(SG + 2):
                    if g < SG:
                        turn.wait(av_mm, g - 1)
                        for h in range(4 * g, 4 * g + 4):
                            for half, (bank, banks, col, cols) in enumerate(spans):
                                turn.wait(st_mm, 2 * h + half + 1)
                                src = ps[:, bank:bank + banks, :] if banks > 1 else ps[:, bank, 0:cols]
                                act.activation(pt[:, g % 2, h % 4, col:col + cols], src, ACT.Exp).then_inc(exp_done.sem, 1)
                    if 1 <= g < SG + 1:
                        gg = g - 1
                        turn.wait(av_mm, gg + 1)
                        turn.wait(out_normed, gg - 1)
                        act.activation(ou[:, gg % 2, :], ps[:, 4 + gg % 2, :], ACT.Copy).then_inc(out_kept.sem, 1)
                    if 2 <= g:
                        gg = g - 2
                        turn.wait(sum_mm, gg + 1)
                        act.activation(rr[:, gg % 2, :], ps[:, 6, :], ACT.Ln).then_inc(ln_done.sem, 1)
                        turn.wait(ln_done, gg + 1)
                        act.activation(rr[:, gg % 2, :], rr[:, gg % 2, :], ACT.Exp, scale=-1.0).then_inc(recip_done.sem, 1)

        @block.vector
        def _(dve):
            for e in owner["dve"]:
                dve.sem_inc(e.sem, AHEAD)
            with dve.Fori(0, BATCH) as b:
                turn = Counts(dve, b, per_turn)
                turn.wait(proj_mm, 0)
                dve.tensor_scalar(hb[:, :], z[:, bass.ds(b * SEQ, SEQ)], 1.0, None, ALU.mult).then_inc(row_kept.sem, 1)
                turn.wait(proj_mm, n_mm)
                turn.wait(av_mm, 0)
                dve.tensor_copy(va[:, :, :, 0:SD], ps[:, 3, :].rearrange("p (t h c) -> p t h c", t=TB, h=SH)).then_inc(v_kept.sem, 1)
                if kind == "norm":
                    turn.wait(proj_act, 3)
                    dve.tensor_tensor(x1[:, :, :], ps[:, 0:2, :], xf[:, :, :], ALU.mult).then_inc(qk_normed.sem, 1)
                turn.wait(proj_act, n_act)
                turn.wait(ld_stack, 0)
                dve.tensor_copy(cut[:, 0, :, :], xf[:, :, :]).then_inc(cut_done.sem, 1)
                turn.wait(cut_done, 1)
                dve.tensor_tensor(x1[:, :, :], xf[:, :, :], cut[:, 0, :, :], ALU.subtract).then_inc(cut_done.sem, 1)
                turn.wait(cut_done, 2)
                dve.tensor_copy(cut[:, 1, :, :], x1[:, :, :]).then_inc(cut_done.sem, 1)
                turn.wait(cut_done, 3)
                dve.tensor_tensor(x1[:, :, :], x1[:, :, :], cut[:, 1, :, :], ALU.subtract).then_inc(cut_done.sem, 1)
                turn.wait(cut_done, 4)
                dve.tensor_copy(cut[:, 2, :, :], x1[:, :, :]).then_inc(cut_done.sem, 1)
                turn.wait(mt_mm, 0)
                for h in range(SH):
                    turn.wait(s_mm, h + 1)
                    banks = 4 * (h % 2)
                    if causal:
                        for i in range(TB):
                            last = dve.tensor_reduce(nm[:, h, i:i + 1], ps[:, banks + i, 0:P * (i + 1)], AX.X, ALU.max, negate=True)
                        last.then_inc(max_done.sem, 1)
                    else:
                        dve.tensor_reduce(nm[:, h, :], ps[:, banks:banks + 4, :], AX.X, ALU.max, negate=True).then_inc(max_done.sem, 1)
                turn.wait(mt_mm, 1)
                turn.wait(ld_m, 0)
                dve.tensor_copy(mf[:, :], ps[0:64, 0, 0:P]).then_inc(mcut_done.sem, 1)
                turn.wait(mcut_done, 1)
                dve.tensor_copy(mcut[:, 0, :], mf[:, :]).then_inc(mcut_done.sem, 1)
                turn.wait(mcut_done, 2)
                dve.tensor_tensor(m1[:, :], mf[:, :], mcut[:, 0, :], ALU.subtract).then_inc(mcut_done.sem, 1)
                turn.wait(mcut_done, 3)
                dve.tensor_copy(mcut[:, 1, :], m1[:, :]).then_inc(mcut_done.sem, 1)
                turn.wait(mcut_done, 4)
                dve.tensor_tensor(m1[:, :], m1[:, :], mcut[:, 1, :], ALU.subtract).then_inc(mcut_done.sem, 1)
                turn.wait(mcut_done, 5)
                dve.tensor_copy(mcut[:, 2, :], m1[:, :]).then_inc(mcut_done.sem, 1)
                for gg in range(SG):
                    turn.wait(recip_done, gg + 1)
                    dve.tensor_tensor(on[:, gg % 2, :], ou[:, gg % 2, :], rr[:, gg % 2, :], ALU.mult).then_inc(out_normed.sem, 1)
                turn.wait(y_mm, 1)
                xb = x[:, bass.ds(b * SEQ, SEQ)]
                dve.tensor_tensor(xb, xb, ps[:, 7, :], ALU.add).then_inc(added.sem, 1)
    for e, k in per_turn.items():
        e.past(BATCH * k)


def linear_attention(core):
    nc, d, x, z, ps = core.nc, core.d, core.x, core.z, core.ps
    ev = core.events
    ld_w, prep_pool, prep_dve = ev("la_ld_w", "la_prep_pool", "la_prep_dve")
    proj_mm, feat_mm, kv_mm, out_mm, sum_mm, y_mm = ev("la_proj_mm", "la_feat_mm", "la_kv_mm", "la_out_mm", "la_sum_mm", "la_y_mm")
    qk_kept, exp_done, out_kept, ln_done, recip_done = ev("la_qk_kept", "la_exp_done", "la_out_kept", "la_ln_done", "la_recip_done")
    row_kept, v_kept, feat_done, kv_kept, out_normed, added = ev(
        "la_row_kept", "la_v_kept", "la_feat_done", "la_kv_kept", "la_out_normed", "la_added")
    TILES = TB + SG
    owner = {
        "pe": {proj_mm: 2, feat_mm: TILES, kv_mm: 1, out_mm: SG, sum_mm: SG, y_mm: 1},
        "act": {qk_kept: 1, exp_done: TILES, out_kept: SG, ln_done: SG, recip_done: SG},
        "dve": {row_kept: 1, v_kept: 1, feat_done: TILES, kv_kept: 1, out_normed: SG, added: 1},
    }
    per_turn = {e: k for es in owner.values() for e, k in es.items()}
    for e in per_turn:
        e.past(AHEAD)
    KV_BANK, SUM_BANK = 2, 3

    with ExitStack() as ctx:
        sb = lambda *a: core.sb(ctx, *a)
        w = sb("w", [P, 3, P])
        wp = sb("wp", [P, SG, P])
        feat_w = sb("feat_w", [P, SH, 32])
        hoc = sb("hoc", [P, SH])
        pm = sb("pm", [P, 32])
        own = sb("own", [P, P])
        sums = sb("sums", [P, P])
        cols = sb("cols", [P, 2])
        hb = sb("hb", [P, SEQ])
        qk = sb("qk", [P, 2, SEQ])
        va = sb("va", [P, TB, SH, 32])
        fe = sb("fe", [P, 2, SEQ])
        fr = sb("fr", [P, 2, SEQ])
        feats = sb("feats", [P, TILES, SEQ])
        kv = sb("kv", [P, SG, P])
        ou = sb("ou", [P, 2, SEQ])
        rr = sb("rr", [P, 2, SEQ])
        on = sb("on", [P, 2, SEQ])
        block = ctx.enter_context(nc.Block())

        @block.gpsimd
        def _(pool):
            pool.memset(wp[:, :, :], 0.0).then_inc(prep_pool.sem, 1)
            pool.memset(cols[:, 1:2], 1e-8).then_inc(prep_pool.sem, 1)
            pool.memset(va[:, :, :, :], 0.0).then_inc(prep_pool.sem, 1)
            pool.wait_ge(prep_pool.sem, prep_pool.at(3))
            pool.memset(va[:, :, :, SD:SD + 1], 1.0).then_inc(prep_pool.sem, 1)

        @block.sync
        def _(sp):
            sp.dma_start(w[:, :, :], d["L1_attn_a_w_qkv"].rearrange("p (s c) -> p s c", s=3)).then_inc(ld_w.sem, 16)
            sp.dma_start(pm[:, :], d["L1_attn_a_proj_matrix"].rearrange("h c f -> (h c) f")).then_inc(ld_w.sem, 16)
            sp.dma_start(hoc[:, :], d["head_of_channel"]).then_inc(ld_w.sem, 16)
            sp.dma_start(own[:, :], d["own_head"]).then_inc(ld_w.sem, 16)
            sp.dma_start(sums[:, :], d["sum_rows"]).then_inc(ld_w.sem, 16)
            sp.dma_start(cols[:, 0:1], d["L1_attn_a_b_out"].rearrange("(c a) -> c a", a=1)).then_inc(ld_w.sem, 16)
            sp.wait_ge(prep_pool.sem, prep_pool.at(1))
            load_output_weights(core, sp, wp, d["L1_attn_a_w_out"], ld_w.sem)

        @block.tensor
        def _(pe):
            for e in owner["pe"]:
                pe.sem_inc(e.sem, AHEAD)
            pe.wait_ge(ld_w.sem, ld_w.at(160))
            pe.wait_ge(prep_dve.sem, prep_dve.at(1))
            with pe.Fori(0, BATCH) as b:
                turn = Counts(pe, b, per_turn)
                turn.wait(row_kept, 1)
                turn.wait(out_kept, 0)
                for s in range(2):
                    last = pe.matmul(ps[:, s, :], w[:, s, :], hb[:, :], start=True, stop=True)
                last.then_inc(proj_mm.sem, 1)
                turn.wait(ln_done, 0)
                for t in range(TB):
                    last = pe.matmul(ps[:, SUM_BANK, t * P:t * P + P], hb[:, t * P:t * P + P], w[:, 2, :], start=True, stop=True)
                last.then_inc(proj_mm.sem, 1)
                turn.wait(qk_kept, 1)
                for i in range(TILES):
                    turn.wait(exp_done, i - 3)
                    if i < TB:
                        pe.matmul(ps[:, 4 + i % 4, :], qk[:, 1, i * P:i * P + P], feat_w[:, :, :].rearrange("p h f -> p (h f)"),
                                  start=True, stop=True).then_inc(feat_mm.sem, 1)
                    else:
                        g = i - TB
                        pe.matmul(ps[:, 4 + i % 4, :], feat_w[:, 4 * g:4 * g + 4, :].rearrange("p h f -> p (h f)"), qk[:, 0, :],
                                  start=True, stop=True).then_inc(feat_mm.sem, 1)
                turn.wait(v_kept, 1)
                turn.wait(added, 0)
                turn.wait(feat_done, TB)
                for g in range(SG):
                    for t in range(TB):
                        last = pe.matmul(ps[:, KV_BANK, g * P:g * P + P], feats[:, t, g * P:g * P + P],
                                         va[:, t, 4 * g:4 * g + 4, :].rearrange("p h c -> p (h c)"), start=t == 0, stop=t == TB - 1)
                last.then_inc(kv_mm.sem, 1)
                turn.wait(kv_kept, 1)
                for g in range(SG + 2):
                    if g < SG:
                        turn.wait(feat_done, TB + g + 1)
                        turn.wait(out_kept, g - 1)
                        pe.matmul(ps[:, g % 2, :], kv[:, g, :], feats[:, TB + g, :], start=True, stop=True).then_inc(out_mm.sem, 1)
                    if 1 <= g < SG + 1:
                        turn.wait(out_kept, g)
                        turn.wait(ln_done, g - 1)
                        pe.matmul(ps[:, SUM_BANK, :], sums[:, :], ou[:, (g - 1) % 2, :], start=True, stop=True).then_inc(sum_mm.sem, 1)
                    if g >= 2:
                        turn.wait(out_normed, g - 1)
                        last = pe.matmul(ps[:, KV_BANK, :], wp[:, g - 2, :], on[:, g % 2, :], start=g == 2, stop=g == SG + 1)
                last.then_inc(y_mm.sem, 1)

        @block.scalar
        def _(act):
            for e in owner["act"]:
                act.sem_inc(e.sem, AHEAD)
            act.preload_act_table_set("natural_log_exp_and_others")
            act.wait_ge(prep_pool.sem, prep_pool.at(2))
            with act.Fori(0, BATCH) as b:
                turn = Counts(act, b, per_turn)
                turn.wait(proj_mm, 1)
                turn.wait(feat_mm, 0)
                act.activation(qk[:, :, :], ps[:, 0:2, :], ACT.Copy).then_inc(qk_kept.sem, 1)
                for i in range(TILES):
                    turn.wait(feat_mm, i + 1)
                    turn.wait(feat_done, i - 1)
                    act.activation(fe[:, i % 2, :], ps[:, 4 + i % 4, :], ACT.Exp)
                    act.activation(fr[:, i % 2, :], ps[:, 4 + i % 4, :], ACT.Relu).then_inc(exp_done.sem, 1)
                for g in range(SG + 1):
                    if g < SG:
                        turn.wait(out_mm, g + 1)
                        turn.wait(out_normed, g - 1)
                        act.activation(ou[:, g % 2, :], ps[:, g % 2, :], ACT.Copy).then_inc(out_kept.sem, 1)
                    if g >= 1:
                        turn.wait(sum_mm, g)
                        act.activation(rr[:, (g - 1) % 2, :], ps[:, SUM_BANK, :], ACT.Ln, bias=cols[:, 1:2]).then_inc(ln_done.sem, 1)
                        turn.wait(ln_done, g)
                        act.activation(rr[:, (g - 1) % 2, :], rr[:, (g - 1) % 2, :], ACT.Exp, scale=-1.0).then_inc(recip_done.sem, 1)

        @block.vector
        def _(dve):
            for e in owner["dve"]:
                dve.sem_inc(e.sem, AHEAD)
            dve.wait_ge(ld_w.sem, ld_w.at(160))
            dve.wait_ge(prep_pool.sem, prep_pool.at(4))
            dve.tensor_tensor(feat_w[:, :, :], pm[:, None, :].to_broadcast([P, SH, 32]),
                              hoc[:, :, None].to_broadcast([P, SH, 32]), ALU.mult).then_inc(prep_dve.sem, 1)
            with dve.Fori(0, BATCH) as b:
                turn = Counts(dve, b, per_turn)
                turn.wait(proj_mm, 0)
                dve.tensor_scalar(hb[:, :], z[:, bass.ds(b * SEQ, SEQ)], 1.0, None, ALU.mult).then_inc(row_kept.sem, 1)
                turn.wait(proj_mm, 2)
                turn.wait(kv_mm, 0)
                dve.tensor_copy(va[:, :, :, 0:SD], ps[:, SUM_BANK, :].rearrange("p (t h c) -> p t h c", t=TB, h=SH)).then_inc(v_kept.sem, 1)
                for i in range(TILES):
                    turn.wait(exp_done, i + 1)
                    turn.wait(kv_mm, 0)
                    if i >= TB:
                        turn.wait(out_mm, i - TB + 1 - SG)
                    dve.scalar_tensor_tensor(feats[:, i, :], fe[:, i % 2, :], 1.0, fr[:, i % 2, :], ALU.min, ALU.add).then_inc(feat_done.sem, 1)
                turn.wait(kv_mm, 1)
                turn.wait(out_mm, 0)
                dve.tensor_tensor(kv[:, :, :], ps[:, KV_BANK, :].rearrange("p (g c) -> p g c", g=SG),
                                  own[:, None, :].to_broadcast([P, SG, P]), ALU.mult).then_inc(kv_kept.sem, 1)
                for g in range(SG):
                    turn.wait(recip_done, g + 1)
                    dve.tensor_tensor(on[:, g % 2, :], ou[:, g % 2, :], rr[:, g % 2, :], ALU.mult).then_inc(out_normed.sem, 1)
                turn.wait(y_mm, 1)
                xb = x[:, bass.ds(b * SEQ, SEQ)]
                dve.scalar_tensor_tensor(xb, ps[:, KV_BANK, :], cols[:, 0:1], xb, ALU.add, ALU.add).then_inc(added.sem, 1)
    for e, k in per_turn.items():
        e.past(BATCH * k)
    ld_w.past(160)
    prep_pool.past(4)
    prep_dve.past(1)


_INS = ["L0_attn_a_x", "L0_attn_a_w_qkv", "L0_attn_a_w_proj", "L0_attn_a_q_gamma", "L0_attn_a_q_beta",
        "L0_attn_a_k_gamma", "L0_attn_a_k_beta", "L0_attn_b_W_dq", "L0_attn_b_W_uq", "L0_attn_b_W_dkv",
        "L0_attn_b_W_uk", "L0_attn_b_W_uv", "L0_attn_b_W_o", "L0_ffn_Wqkv", "L0_ffn_q_scale", "L0_ffn_k_scale",
        "L0_ffn_Wo", "L0_ffn_ln_g", "L0_ffn_ln_b", "L0_ffn_W1", "L0_ffn_b1", "L0_ffn_W2", "L0_ffn_b2",
        "L1_attn_a_w_qkv", "L1_attn_a_proj_matrix", "L1_attn_a_w_out", "L1_attn_a_b_out",
        "L1_attn_b_w_qkv", "L1_attn_b_w_o", "L1_ffn_w_gate", "L1_ffn_w_up", "L1_ffn_w_down"]


def build(nc, d):
    with ExitStack() as ctx:
        core = Core(nc, ctx, d)
        load_and_transpose(core)
        normalise(core, False)
        small_attention(core, "norm")
        normalise(core, False)
        local_block(core)
        normalise(core, True)
        small_attention(core, "latent")
        normalise(core, False)
        local_block(core)
        normalise(core, True)
        linear_attention(core)
        normalise(core, False)
        swiglu(core, True)
        normalise(core, False)
        small_attention(core, "plain")
        normalise(core, False)
        swiglu(core, False)
        turn_and_store(core)


def kernel(**inputs):
    import numpy as _np
    import concourse.bacc as _bacc
    from concourse import mybir as _mybir
    from concourse.bass_utils import run_bass_kernel_spmd as _run

    nc = _bacc.Bacc("TRN2", target_bir_lowering=False, num_devices=1)
    laid = {name: _np.ascontiguousarray(inputs[name]) for name in _INS}
    laid.update(constants())
    arrays, d = {}, {}
    for name, a in laid.items():
        arrays[f"in_{name}"] = a
        d[name] = nc.dram_tensor(f"in_{name}", a.shape, _mybir.dt.from_np(a.dtype), kind="ExternalInput").ap()
    d["out"] = nc.dram_tensor("out", (BATCH, SEQ, P), _mybir.dt.float32, kind="ExternalOutput").ap()
    build(nc, d)
    r = _run(nc, [arrays], core_ids=[0])
    return r.results[0]["out"]
```

```python
import numpy as np
from contextlib import ExitStack

import concourse.bass as bass
from concourse import mybir
from concourse.alu_op_type import AluOpType as ALU

F32 = mybir.dt.float32
BF16 = mybir.dt.bfloat16
I32 = mybir.dt.int32
ACT = mybir.ActivationFunctionType
AX = mybir.AxisListType

P = 128
BATCH, SEQ = 4, 512
TOK = BATCH * SEQ
EPS = 1e-5

DEPTH, HEADS, HD, WIN = 6, 16, 64, 32
INNER = HEADS * HD
QKV = 3 * INNER
FF = int(P * 4 * 2 / 3)
FF_ROWS = [min(P, FF - P * j) for j in range(3)]
UNITS = 4
TB = SEQ // P
SLOTS = UNITS * TB
KEYS = 2 * WIN
NEG = -1e30

SH, SD = 16, 8
SG = SH // 4
FF_LOADS = 12
NORM_SCALE = 2.0 ** 16
AHEAD = 80


class Events:

    def __init__(self, ctx, nc, name):
        self.sem = ctx.enter_context(nc.semaphore(name))
        self.start = 0

    def at(self, n):
        return n + self.start

    def past(self, n):
        self.start += n


class Counts:

    def __init__(self, eng, turn, per_turn):
        self.eng, self.turn, self.per_turn, self.bases, self.ahead = eng, turn, per_turn, {}, 0

    def next(self):
        after = Counts(self.eng, self.turn, self.per_turn)
        after.bases, after.ahead = self.bases, self.ahead + 1
        return after

    def wait(self, e, n):
        k = self.per_turn[e]
        if k not in self.bases:
            base = self.turn * k
            self.bases[k] = base if isinstance(base, int) else self.eng.snap(base)
        self.eng.wait_ge(e.sem, self.bases[k] + (e.start + n + self.ahead * k))


def constants():
    half = np.arange(0, HD, 2, dtype=np.float32)
    inv_freq = (1.0 / 10000.0 ** (half / HD)).astype(np.float32)
    pos = np.arange(SEQ, dtype=np.float32)
    freqs = pos[:, None] * inv_freq[None, :]
    cos, sin = np.cos(freqs), np.sin(freqs)
    base = (half + 0.4 * HD) / (1.4 * HD)
    scale = base[None, :] ** ((pos - SEQ // 2) / (WIN // 2))[:, None]
    straight = np.zeros((SEQ, 2, 2, HD // 2), np.float32)
    crossed = np.zeros((SEQ, 2, 2, HD // 2), np.float32)
    for s, f in enumerate((8.0 * scale, 1.0 / scale)):
        straight[:, s, 0] = straight[:, s, 1] = cos * f
        crossed[:, s, 0] = -sin * f
        crossed[:, s, 1] = sin * f
    lay = lambda a: np.ascontiguousarray(
        a.reshape(TB, P, 2 * HD).transpose(1, 0, 2).reshape(P, TB * 2 * HD), np.float32)
    p, c = np.arange(P)[:, None], np.arange(2 * WIN)[None, :]
    seen = (p % WIN <= c) & (c <= p % WIN + WIN)
    first = np.where(seen & ((p >= WIN) | (c >= WIN)), 0.0, NEG)
    later = np.where(seen, 0.0, NEG)
    band = np.concatenate([first] * 4 + [later] * 4, 1).astype(np.float32)
    causal = np.where(np.arange(P)[None, :] <= p, 0.0, NEG).astype(np.float32)
    return {
        "rope_straight": lay(straight),
        "rope_crossed": lay(crossed),
        "band": band,
        "identity": np.eye(P, dtype=np.float32),
        "causal": causal,
        "head_of_channel": np.kron(np.eye(SH), np.ones((SD, 1))).astype(np.float32),
        "mean_of_8": np.kron(np.full((SD, SD), 1 / SD), np.eye(SH)).astype(np.float32),
        "sum_rows": np.kron(np.eye(4), np.outer(np.arange(32) == SD, np.ones(32))).astype(np.float32),
        "own_head": np.kron(np.eye(4), np.ones((32, 32))).astype(np.float32),
        "quadrant": np.kron(np.eye(TB), np.ones((WIN, 1))).astype(np.float32),
    }


class Core:

    def __init__(self, nc, ctx, d):
        self.nc, self.ctx, self.d = nc, ctx, d
        self.names = 0
        sb = self.sb
        self.x = sb(ctx, "x", [P, TOK])
        self.z = sb(ctx, "z", [P, TOK])
        self.ident = sb(ctx, "ident", [P, P])
        self.ident16 = sb(ctx, "ident16", [P, P], BF16)
        self.mean_w = sb(ctx, "mean_w", [P, P])
        self.small = sb(ctx, "small", [P, 8])
        self.ps = ctx.enter_context(nc.psum_tensor("ps", [P, 8, 512], F32))
        self.ev = {}

    def sb(self, ctx, name, shape, dt=F32):
        self.names += 1
        return ctx.enter_context(self.nc.sbuf_tensor(f"{name}_{self.names}", shape, dt))

    def events(self, *names):
        for n in names:
            if n not in self.ev:
                self.ev[n] = Events(self.ctx, self.nc, n)
        got = [self.ev[n] for n in names]
        return got[0] if len(got) == 1 else got


EPS_COL, LN_UP_COL = 0, 1


def load_and_transpose(core):
    nc, d = core.nc, core.d
    loaded, loaded_id, made, turned, moved = core.events("ld_x", "ld_ident", "consts_made", "x_turned", "x_moved")
    with ExitStack() as ctx:
        xt = core.sb(ctx, "xt", [P, TOK // P, P])
        block = ctx.enter_context(nc.Block())

        @block.sync
        def _(sp):
            sp.dma_start(core.ident[:, :], d["identity"]).then_inc(loaded_id.sem, 16)
            sp.dma_start(xt[:, :, :], d["L0_attn_a_x"].rearrange("b (t p) c -> p (b t) c", p=P)).then_inc(loaded.sem, 16)

        @block.gpsimd
        def _(pool):
            pool.memset(core.mean_w[:, :], 1.0 / P).then_inc(made.sem, 1)
            pool.memset(core.small[:, EPS_COL:EPS_COL + 1], EPS).then_inc(made.sem, 1)
            pool.memset(core.small[:, LN_UP_COL:LN_UP_COL + 1], float(8.0 * np.log(2.0))).then_inc(made.sem, 1)

        @block.tensor
        def _(pe):
            pe.wait_ge(loaded_id.sem, 16)
            pe.wait_ge(loaded.sem, 16)
            for k in range(TOK // P):
                bank = k // 4 % 4
                last = pe.transpose(core.ps[:, bank, k % 4 * P:k % 4 * P + P], xt[:, k, :], core.ident[:, :])
                if k % 4 == 3:
                    last.then_inc(turned.sem, 1)

        @block.vector
        def _(dve):
            dve.wait_ge(loaded_id.sem, 16)
            dve.tensor_copy(core.ident16[:, :], core.ident[:, :])
            for b in range(BATCH):
                dve.wait_ge(turned.sem, b + 1)
                dve.tensor_copy(core.x[:, b * SEQ:(b + 1) * SEQ], core.ps[:, b, :]).then_inc(moved.sem, 1)


def turn_and_store(core):
    nc, d = core.nc, core.d
    turned, moved, stored = core.events("y_turned", "y_moved", "y_stored")
    with ExitStack() as ctx:
        yt = core.sb(ctx, "yt", [P, TOK // P, P])
        block = ctx.enter_context(nc.Block())

        @block.tensor
        def _(pe):
            for k in range(TOK // P):
                last = pe.transpose(core.ps[:, k // 4, k % 4 * P:k % 4 * P + P], core.x[:, k * P:k * P + P], core.ident[:, :])
                if k % 4 == 3:
                    last.then_inc(turned.sem, 1)

        @block.vector
        def _(dve):
            for b in range(BATCH):
                dve.wait_ge(turned.sem, b + 1)
                dve.tensor_copy(yt[:, b * TB:b * TB + TB, :], core.ps[:, b, :].rearrange("p (t c) -> p t c", t=TB)).then_inc(moved.sem, 1)

        @block.sync
        def _(sp):
            for b in range(BATCH):
                sp.wait_ge(moved.sem, b + 1)
                sp.dma_start(d["out"][b].rearrange("(t p) c -> p t c", p=P), yt[:, b * TB:b * TB + TB, :]).then_inc(stored.sem, 16)
            sp.wait_ge(stored.sem, 16 * BATCH)


def normalise(core, add_z):
    nc, x, z, ps = core.nc, core.x, core.z, core.ps
    added, mean, centred, squared, var, ln, rstd, done = core.events(
        "n_added", "n_mean", "n_centred", "n_squared", "n_var", "n_ln", "n_rstd", "n_done")
    cols = [slice(b * SEQ, (b + 1) * SEQ) for b in range(BATCH)]
    with ExitStack() as ctx:
        c = core.sb(ctx, "centred", [P, TOK])
        q = core.sb(ctx, "squares", [P, TOK])
        r = core.sb(ctx, "rstd", [P, TOK])
        block = ctx.enter_context(nc.Block())

        @block.tensor
        def _(pe):
            for b in range(BATCH):
                if add_z:
                    pe.wait_ge(added.sem, added.at(b + 1))
                pe.matmul(ps[:, b, :], core.mean_w[:, :], x[:, cols[b]], start=True, stop=True).then_inc(mean.sem, 1)
            for b in range(BATCH):
                pe.wait_ge(squared.sem, squared.at(b + 1))
                pe.matmul(ps[:, 4 + b, :], core.mean_w[:, :], q[:, cols[b]], start=True, stop=True).then_inc(var.sem, 1)

        @block.vector
        def _(dve):
            if add_z:
                for b in range(BATCH):
                    dve.tensor_tensor(x[:, cols[b]], x[:, cols[b]], z[:, cols[b]], ALU.add).then_inc(added.sem, 1)
            for b in range(BATCH):
                if add_z:
                    dve.wait_ge(added.sem, added.at(b + 1))
                dve.wait_ge(mean.sem, mean.at(b + 1))
                dve.tensor_tensor(c[:, cols[b]], x[:, cols[b]], ps[:, b, :], ALU.subtract).then_inc(centred.sem, 1)
            for b in range(BATCH):
                dve.wait_ge(rstd.sem, rstd.at(b + 1))
                dve.tensor_tensor(z[:, cols[b]], c[:, cols[b]], r[:, cols[b]], ALU.mult).then_inc(done.sem, 1)

        @block.scalar
        def _(act):
            act.preload_act_table_set("natural_log_exp_and_others")
            for b in range(BATCH):
                act.wait_ge(centred.sem, centred.at(b + 1))
                act.activation(q[:, cols[b]], c[:, cols[b]], ACT.Square).then_inc(squared.sem, 1)
            for b in range(BATCH):
                act.wait_ge(var.sem, var.at(b + 1))
                act.activation(r[:, cols[b]], ps[:, 4 + b, :], ACT.Ln, bias=core.small[:, EPS_COL:EPS_COL + 1]).then_inc(ln.sem, 1)
            for b in range(BATCH):
                act.wait_ge(ln.sem, ln.at(b + 1))
                act.activation(r[:, cols[b]], r[:, cols[b]], ACT.Exp, scale=-0.5).then_inc(rstd.sem, 1)
    if add_z:
        added.past(BATCH)
    for e in (mean, centred, squared, var, ln, rstd, done):
        e.past(BATCH)


def add_z_to_x(core):
    nc, x, z = core.nc, core.x, core.z
    with nc.Block() as block:

        @block.vector
        def _(dve):
            dve.tensor_tensor(x[:, :], x[:, :], z[:, :], ALU.add)


def local_block(core):
    nc, d, x, z, ps = core.nc, core.d, core.x, core.z, core.ps
    ev = core.events
    qk_ready, v_ready, tr_ready, s_ready, pt_ready, pbt_ready, av_ready, wo_ready, ff_mm = ev(
        "qk_ready", "v_ready", "tr_ready", "s_ready", "pt_ready", "pbt_ready", "av_ready", "wo_ready", "ff_mm")
    sq_done, v_kept, q_kept, exp_done, ln_done, inv_done, o_kept, ff_act = ev(
        "sq_done", "v_kept", "q_kept", "exp_done", "ln_done", "inv_done", "o_kept", "ff_act")
    pnd_done = ev("pnd_done")
    rope_done, ss_done, ssc_done, k_kept, max_done, recip_done, pt_kept, pbt_kept, z_added, ff_dve, tables_done, xs_done, fs_done, shift_done = ev(
        "rope_done", "ss_done", "ssc_done", "k_kept", "max_done", "recip_done", "pt_kept", "pbt_kept", "z_added", "ff_dve", "tables_done", "xs_done", "fs_done", "shift_done")
    sum_done, qkr_done, pn_done, cleared = ev("sum_done", "qkr_done", "pn_done", "cleared")
    ld_wq, ld_scales, ld_wo, ld_ff, ld_tables = ev("ld_wq", "ld_scales", "ld_wo", "ld_ff", "ld_tables")
    per_slot = [qk_ready, tr_ready, s_ready, pt_ready, av_ready, sq_done, q_kept, ln_done, inv_done,
                rope_done, ss_done, ssc_done, k_kept, max_done, recip_done, pt_kept, sum_done, qkr_done, pn_done]
    per_turn = {exp_done: SLOTS, pnd_done: SLOTS, v_ready: 3 * UNITS, v_kept: 3 * UNITS, pbt_ready: UNITS, wo_ready: UNITS, o_kept: UNITS,
                pbt_kept: UNITS, z_added: UNITS, ff_mm: 9, ff_act: 7, ff_dve: 8, xs_done: 1, fs_done: 1}
    for e in per_slot:
        per_turn[e] = SLOTS
    owner = {}
    for e in (qk_ready, v_ready, tr_ready, s_ready, pt_ready, pbt_ready, av_ready, wo_ready, ff_mm):
        owner[e] = "pe"
    for e in (sq_done, v_kept, q_kept, exp_done, ln_done, inv_done, o_kept, ff_act):
        owner[e] = "act"
    for e in (pnd_done, rope_done, ss_done, ssc_done, k_kept, max_done, recip_done, pt_kept, pbt_kept, z_added, ff_dve, xs_done, fs_done):
        owner[e] = "dve"
    for e in (sum_done, qkr_done, pn_done):
        owner[e] = "pool"
    for e in owner:
        e.past(AHEAD)

    TURN_SLOTS = SLOTS + 2
    CLEARED = 7 + 12
    LAG_TR, LAG_KEEP, LAG_S, LAG_PT, LAG_AV = 1, 2, 3, 4, 5
    O_GROUP = {9: 0, 13: 1, 17: 2, 4: -1}
    WO_GROUP = {11: 0, 15: 1, 3: -2, 7: -1}
    behind = {s_ready: 1, max_done: 1, exp_done: 1, recip_done: 1, pn_done: 2, pnd_done: 2, pt_ready: 2, pt_kept: 3,
              av_ready: 3, pbt_ready: 1, pbt_kept: 1, o_kept: 1, wo_ready: 2, z_added: 2}

    def item(s, lag, whole, rest=True):
        k = s - lag
        if 0 <= k < SLOTS:
            return k if whole else None
        if rest and k < 0 and k + TURN_SLOTS < SLOTS:
            return k + TURN_SLOTS - SLOTS
        return None

    PJ0, PJ1, TR0, TR1, SS, PO = ps[:, 0, :], ps[:, 1, :], ps[:, 2, :], ps[:, 3, :], (4, 5), (6, 7)

    def start_ahead(eng, who):
        for e, w in owner.items():
            if w == who:
                eng.sem_inc(e.sem, AHEAD - (behind[e] if e in behind else 0))

    def Turn(eng, l, b):
        return Counts(eng, l * BATCH + b, per_turn)

    def ff_weights(eng, turn):
        eng.wait_ge(ld_ff.sem, (turn.turn + (BATCH - 2)) // BATCH * (16 * FF_LOADS) + (ld_ff.start + 16))

    def over_sum(eng, w, sc):
        rows = slice(WIN * w, WIN * w + WIN)
        return eng.tensor_tensor(pn[rows, sc % 2, :, WIN * w:WIN * w + KEYS], pr[rows, sc % 2, :, :],
                                 rden[rows, sc % 2, :, None].to_broadcast([WIN, 4, KEYS]), ALU.mult)

    with ExitStack() as ctx:
        sb = lambda *a: core.sb(ctx, *a)
        wq = sb("wq", [P, 2, QKV])
        wo = sb("wo", [P, INNER // P, P])
        w1 = sb("w1", [P, 2 * FF])
        w2 = sb("w2", [P, 3, P])
        ffc = sb("ffc", [P, 16])
        scales = sb("scales", [P, 2, 2, 2, HD // 2])
        base = sb("base", [P, 2, TB, 2 * HD])
        rope = sb("rope", [P, 2, TB, 2 * HD])
        bandf = sb("bandf", [P, 8 * KEYS])
        band = sb("band", [P, 8 * KEYS], BF16)
        xs = sb("xs", [P, WIN + SEQ])
        xtail = sb("xtail", [P, TB, WIN])
        sq = sb("sq", [P, 2, 512])
        ra = sb("ra", [P, 2, 512])
        rb = sb("rb", [P, 2, 512])
        qkr = sb("qkr", [P, 2, 512])
        ssq = sb("ssq", [P, 2, 8])
        inv = sb("inv", [P, 2, 8])
        qt = sb("qt", [P, 2, 256])
        kz = sb("kz", [P, 4, WIN + SEQ])
        pr = sb("pr", [P, 2, 4, KEYS])
        neg = sb("neg", [P, 2, 4])
        den = sb("den", [P, 2, 4])
        rden = sb("rden", [P, 2, 4])
        pn = sb("pn", [P, 2, 4, P])
        pb = sb("pb", [P, 2, 4, TB, WIN])
        pt = sb("pt", [P, 2, 512])
        pbt = sb("pbt", [P, 4, TB, WIN])
        quad = sb("quad", [P, TB])
        vs = sb("vs", [P, UNITS, TB, 256])
        vc = sb("vc", [P, UNITS, 256])
        ot = sb("ot", [P, 2, 512])
        fs = sb("fs", [P, SEQ])
        fc = sb("fc", [P, SEQ])
        fq = sb("fq", [P, SEQ])
        fr = sb("fr", [P, SEQ])
        fx = sb("fx", [P, SEQ])
        fh = sb("fh", [P, SEQ])
        third = sb("third", [FF_ROWS[2], 2, SEQ])
        gl = sb("gl", [P, 3, SEQ])
        fm = sb("fm", [P, 3, SEQ])
        block = ctx.enter_context(nc.Block())

        @block.sync
        def _(sp):
            sp.dma_start(base[:, 0, :, :], d["rope_straight"].rearrange("p (t c) -> p t c", t=TB)).then_inc(ld_tables.sem, 16)
            sp.dma_start(base[:, 1, :, :], d["rope_crossed"].rearrange("p (t c) -> p t c", t=TB)).then_inc(ld_tables.sem, 16)
            sp.dma_start(bandf[:, :], d["band"]).then_inc(ld_tables.sem, 16)
            sp.dma_start(quad[:, :], d["quadrant"]).then_inc(ld_tables.sem, 16)
            with sp.Fori(0, DEPTH) as l:
                turn = Turn(sp, l, 0)
                sp.wait_ge(ld_wq.sem, l * 16 + 16 + ld_wq.start)
                turn.wait(v_ready, -3 * UNITS * BATCH)
                turn.wait(qk_ready, -SLOTS * BATCH)
                sp.dma_start(wq[:, bass.ds(l % 2, 1), :], d["L0_ffn_Wqkv"][bass.ds(l, 1), :, :].rearrange("l p c -> p l c")).then_inc(ld_wq.sem, 16)
                sp.wait_ge(tables_done.sem, l * 2 + (tables_done.start + 3))
                for s, name in enumerate(("L0_ffn_q_scale", "L0_ffn_k_scale")):
                    row = d[name][bass.ds(l, 1), :]
                    for e in range(2):
                        half = row[:, e * 32:e * 32 + 32].to_broadcast([P, 32])
                        sp.dma_start(scales[:, 0, s, e, :], half).then_inc(ld_scales.sem, 16)
                        sp.dma_start(scales[:, 1, s, 1 - e, :], half).then_inc(ld_scales.sem, 16)
                turn.wait(wo_ready, 0)
                sp.dma_start(wo[:, :, :], d["L0_ffn_Wo"][bass.ds(l, 1), :, :].rearrange("l (k p) c -> p (l k) c", p=P)).then_inc(ld_wo.sem, 16)
                turn.wait(ff_dve, 16)
                sp.dma_start(w1[:, :], d["L0_ffn_W1"][bass.ds(l, 1), :, :].rearrange("l p c -> p (l c)")).then_inc(ld_ff.sem, 16)
                w2d = d["L0_ffn_W2"][bass.ds(l, 1), :, :]
                sp.dma_start(w2[:, 0:2, :], w2d[:, 0:2 * P, :].rearrange("l (k p) c -> p (l k) c", p=P)).then_inc(ld_ff.sem, 16)
                sp.dma_start(w2[0:FF_ROWS[2], 2, :], w2d[:, 2 * P:FF, :].rearrange("l p c -> p (l c)")).then_inc(ld_ff.sem, 16)
                for col, name in enumerate(("L0_ffn_ln_g", "L0_ffn_ln_b", "L0_ffn_b2")):
                    sp.dma_start(ffc[:, col:col + 1], d[name][bass.ds(l, 1), :].rearrange("l p -> p l")).then_inc(ld_ff.sem, 16)
                for half in range(2):
                    for j in range(3):
                        rows = FF_ROWS[j]
                        at = half * FF + j * P
                        sp.dma_start(ffc[0:rows, 3 + 3 * half + j:4 + 3 * half + j],
                                     d["L0_ffn_b1"][bass.ds(l, 1), at:at + rows].rearrange("l p -> p l")).then_inc(ld_ff.sem, 16)

        @block.gpsimd
        def _(pool):
            start_ahead(pool, "pool")
            pool.sem_inc(ld_wq.sem, 16)
            pool.sem_inc(ld_ff.sem, 16)
            pool.memset(w1[:, :], 0.0).then_inc(cleared.sem, 1)
            pool.memset(w2[:, :, :], 0.0).then_inc(cleared.sem, 1)
            pool.memset(ffc[:, :], 0.0).then_inc(cleared.sem, 1)
            pool.memset(kz[:, :, :], 0.0).then_inc(cleared.sem, 1)
            pool.memset(xs[:, 0:WIN + 1], 0.0).then_inc(cleared.sem, 1)
            pool.memset(fs[:, 0:1], 0.0).then_inc(cleared.sem, 1)
            pool.memset(wo[:, :, :], 0.0).then_inc(cleared.sem, 1)
            pool.wait_ge(cleared.sem, cleared.at(CLEARED))

            def slot(turn, s, whole):
                sr = item(s, 1, whole)
                if sr is not None:
                    turn.wait(sum_done, sr + 1)
                    turn.wait(inv_done, sr + 1)
                    turn.wait(tr_ready, sr - 1)
                    pool.tensor_tensor(qkr[:, sr % 2, :].rearrange("p (h c) -> p h c", h=8),
                                       ra[:, sr % 2, :].rearrange("p (h c) -> p h c", h=8),
                                       inv[:, sr % 2, :, None].to_broadcast([P, 8, HD]), ALU.mult).then_inc(qkr_done.sem, 1)
                sc = item(s, LAG_PT, whole)
                if sc is not None:
                    g, t = divmod(sc, TB)
                    turn.wait(recip_done, sc + 1)
                    turn.wait(exp_done, sc + 1)
                    turn.wait(pt_ready, sc - 1)
                    if sr is not None:
                        turn.wait(qkr_done, sr + 1)
                    over_sum(pool, 2, sc)
                    rows = slice(3 * WIN, P)
                    over = rden[rows, sc % 2, :, None].to_broadcast([WIN, 4, WIN])
                    pool.tensor_tensor(pn[rows, sc % 2, :, 3 * WIN:P], pr[rows, sc % 2, :, 0:WIN], over, ALU.mult)
                    if t == 0:
                        turn.wait(pbt_ready, g - 1)
                    pool.tensor_tensor(pb[rows, g % 2, :, t, :], pr[rows, sc % 2, :, WIN:KEYS], over, ALU.mult).then_inc(pn_done.sem, 1)
                if whole and s < SLOTS:
                    turn.wait(rope_done, s + 1)
                    if sc is not None:
                        turn.wait(pn_done, sc + 1)
                    pool.tensor_tensor(ra[:, s % 2, :], ra[:, s % 2, :], rb[:, s % 2, :], ALU.add).then_inc(sum_done.sem, 1)

            with pool.Fori(0, DEPTH) as l:
                with pool.Fori(0, BATCH) as b:
                    turn = Turn(pool, l, b)
                    for s in range(TURN_SLOTS):
                        slot(turn, s, True)
            turn = Turn(pool, DEPTH, 0)
            for s in range(TURN_SLOTS):
                slot(turn, s, False)

        @block.tensor
        def _(pe):
            start_ahead(pe, "pe")
            pe.wait_ge(cleared.sem, cleared.at(CLEARED))
            pe.wait_ge(tables_done.sem, tables_done.at(3))

            def slot(turn, s, whole, stats, l, lp):
                def made(e, n):
                    turn.wait(e, n if whole else 0 if stats else -per_turn[e])

                g, t = divmod(s, TB)
                fresh = whole and s < SLOTS
                ss = item(s, LAG_S, whole, stats)
                if ss is not None:
                    st = ss % TB
                    turn.wait(q_kept, ss + 1)
                    turn.wait(k_kept, ss + 1)
                    turn.wait(exp_done, ss - 1)
                    bank = ps[:, SS[ss % 2], 0:4 * KEYS]
                    pe.matmul(bank, core.ident16[:, :], band[:, 0 if st == 0 else 4 * KEYS:][:, 0:4 * KEYS], start=True, stop=False, skip_group_check=True)
                    for h in range(4):
                        for w in range(TB):
                            last = pe.matmul(ps[WIN * w:WIN * w + WIN, SS[ss % 2], h * KEYS:h * KEYS + KEYS],
                                             qt[:, ss % 2, h // 2 * P + WIN * w:h // 2 * P + WIN * w + WIN],
                                             kz[:, h, st * P + WIN * w:st * P + WIN * w + KEYS], start=False, stop=h == 3, skip_group_check=True)
                    last.then_inc(s_ready.sem, 1)
                if fresh and s == 0:
                    turn.wait(xs_done, 1)
                    pe.wait_ge(ld_wq.sem, l * 16 + (ld_wq.start + 32))
                    turn.wait(ff_dve, -1)
                if fresh:
                    turn.wait(sq_done, s)
                    turn.wait(rope_done, s)
                    rhs = wq[:, bass.ds(lp, 1), 0:2 * INNER].rearrange("p l (s c) -> p (l s) c", s=2)[:, :, g * 256:g * 256 + 256]
                    pe.matmul(PJ0.rearrange("p (s c) -> p s c", s=2), xs[:, WIN + t * P:WIN + t * P + P], rhs, start=True, stop=True).then_inc(qk_ready.sem, 1)
                sv = item(s, LAG_AV, whole, stats)
                if sv is not None and sv % TB == 3:
                    gg = sv // TB
                    turn.wait(pn_done, sv + 1)
                    made(q_kept, s - 1)
                    made(k_kept, s - 1)
                    for h in range(4):
                        last = pe.matmul(TR0[:, h * WIN:h * WIN + WIN], pb[96:P, gg % 2, h, :, :].rearrange("p t c -> p (t c)"), core.ident[96:P, 96:P], start=True, stop=True)
                    last.then_inc(pbt_ready.sem, 1)
                if s == TURN_SLOTS - 2:
                    ff_weights(pe, turn)
                    turn.wait(ff_act, 1)
                    made(sq_done, SLOTS)
                    made(rope_done, SLOTS)
                    for j in range(2):
                        if j == 1:
                            turn.wait(ff_act, 3)
                            turn.wait(ff_dve, 4)
                        pe.matmul((PJ0, PJ1)[j], w1[:, FF + j * P:FF + j * P + P], fh[:, :], start=True, stop=True).then_inc(ff_mm.sem, 1)
                if fresh and t < 3:
                    if t == 0:
                        turn.wait(z_added, g - 2)
                        turn.wait(ff_dve, (0, 2, 3, 4)[g])
                    turn.wait(v_kept, 3 * g + t)
                    wv = wq[:, bass.ds(lp, 1), 2 * INNER + g * 256:2 * INNER + g * 256 + 256].rearrange("p l c -> p (l c)")
                    if t < 2:
                        for k in range(2):
                            tt = 2 * t + k
                            last = pe.matmul(PJ1[:, k * 256:k * 256 + 256], xs[:, tt * P:tt * P + P], wv, start=True, stop=True)
                    else:
                        last = pe.matmul(PJ1[:, 0:256], xtail[:, :, :].rearrange("p t c -> p (t c)"), wv, start=True, stop=True)
                    last.then_inc(v_ready.sem, 1)
                if s in WO_GROUP and (whole or stats and WO_GROUP[s] < 0):
                    gg = WO_GROUP[s]
                    turn.wait(o_kept, gg + 1)
                    if gg == 0:
                        pe.wait_ge(ld_wo.sem, l * 16 + (ld_wo.start + 16))
                    if whole:
                        turn.wait(v_kept, 3 * g + 3)
                    if s < 8:
                        turn.wait(ff_dve, 0 if s == 3 else 2)
                    turn.wait(z_added, gg)
                    for k in range(2):
                        last = pe.matmul(PJ1, wo[:, 2 * (gg % UNITS) + k, :], ot[:, k, :], start=k == 0, stop=k == 1)
                    last.then_inc(wo_ready.sem, 1)
                sr = item(s, LAG_TR, whole, stats)
                if sr is not None:
                    turn.wait(qkr_done, sr + 1)
                    turn.wait(q_kept, sr)
                    turn.wait(k_kept, sr)
                    if sv is not None and sv % TB == 3:
                        turn.wait(pbt_kept, sv // TB + 1)
                    for j in range(4):
                        last = pe.transpose(TR0[:, j * P:j * P + P], qkr[:, sr % 2, j * P:j * P + P], core.ident[:, :])
                    last.then_inc(tr_ready.sem, 1)
                if s == TURN_SLOTS - 1:
                    for j in range(2):
                        turn.wait(ff_act, 5 + j)
                        pe.matmul((PJ0, PJ1)[j], w1[:, j * P:j * P + P], fh[:, :], start=True, stop=True).then_inc(ff_mm.sem, 1)
                if sv is not None:
                    gg, tt = divmod(sv, TB)
                    turn.wait(pt_kept, sv + 1)
                    turn.wait(v_kept, 3 * gg + (3 if tt == 3 else tt // 2 + 1))
                    if tt == 0:
                        turn.wait(o_kept, gg)
                    for h in range(4):
                        half = 64 * (h % 2)
                        last = pe.matmul(ps[half:half + 64, PO[h // 2], tt * P:tt * P + P], vs[:, gg % UNITS, tt, h * HD:h * HD + HD],
                                         pt[:, sv % 2, h * P:h * P + P], start=tt == 0, stop=False, skip_group_check=True)
                    if tt == 3:
                        turn.wait(pbt_kept, gg + 1)
                        for h in range(4):
                            half = 64 * (h % 2)
                            ends = ps[half:half + 64, PO[h // 2], :].rearrange("p (t c) -> p t c", t=TB)[:, :, P - WIN:]
                            last = pe.matmul(ends, vc[:, gg % UNITS, h * HD:h * HD + HD], pbt[:, h, :, :], start=False, stop=True, skip_group_check=True)
                    last.then_inc(av_ready.sem, 1)
                sc = item(s, LAG_PT, whole, stats)
                if sc is not None:
                    turn.wait(pn_done, sc + 1)
                    turn.wait(pnd_done, sc + 1)
                    turn.wait(pt_kept, sc)
                    for h in range(4):
                        last = pe.transpose(TR1[:, h * P:h * P + P], pn[:, sc % 2, h, :], core.ident[:, :])
                    last.then_inc(pt_ready.sem, 1)
                if s in (3, 7):
                    ff_weights(pe, turn)
                    turn.wait(ff_act, 1)
                    turn.wait(ff_dve, 0 if s == 3 else 2)
                    turn.wait(z_added, (-1 if s == 3 else 0) - (0 if stats else UNITS))
                    at = 2 * P + (FF if s == 3 else 0)
                    pe.matmul(PJ1[0:FF_ROWS[2], :], w1[:, at:at + FF_ROWS[2]], fh[:, :], start=True, stop=True).then_inc(ff_mm.sem, 1)
                if s == 11 and stats:
                    made(z_added, 1)
                    turn.wait(ff_dve, 3)
                    turn.wait(fs_done, 1)
                    pe.matmul(PJ1, core.mean_w[:, :], fs[:, :], start=True, stop=True).then_inc(ff_mm.sem, 1)
                if s == 15 and stats:
                    made(z_added, 2)
                    turn.wait(ff_act, 2)
                    pe.matmul(PJ1, core.mean_w[:, :], fq[:, :], start=True, stop=True).then_inc(ff_mm.sem, 1)
                if s == TURN_SLOTS - 1:
                    turn.wait(ff_dve, 7)
                    for j in range(3):
                        last = pe.matmul(PJ1, w2[0:FF_ROWS[j], j, :], fm[0:FF_ROWS[j], j, :], start=j == 0, stop=j == 2)
                    last.then_inc(ff_mm.sem, 1)

            with pe.Fori(0, DEPTH) as l:
                with pe.Fori(0, BATCH) as b:
                    turn = Turn(pe, l, b)
                    lp = l % 2
                    for s in range(TURN_SLOTS):
                        slot(turn, s, True, True, l, lp)
            turn = Turn(pe, DEPTH, 0)
            for s in range(TURN_SLOTS):
                slot(turn, s, False, True, None, None)
            turn = Turn(pe, DEPTH, 1)
            for s in (3, 7):
                slot(turn, s, False, False, None, None)
            turn.wait(ff_mm, 2)
            pe.sem_inc(ff_mm.sem, 2)
            for s in range(TURN_SLOTS - 2, TURN_SLOTS):
                slot(turn, s, False, False, None, None)

        @block.scalar
        def _(act):
            start_ahead(act, "act")
            act.preload_act_table_set("natural_log_exp_and_others")
            act.wait_ge(cleared.sem, cleared.at(CLEARED))

            def slot(turn, s, whole, stats):
                sr = item(s, LAG_KEEP, whole, stats)
                if sr is not None:
                    turn.wait(tr_ready, sr + 1)
                    turn.wait(s_ready, sr - 1)
                    act.activation(qt[:, sr % 2, :], TR0[:, 0:256], ACT.Copy).then_inc(q_kept.sem, 1)
                if s == TURN_SLOTS - 2 and stats:
                    turn.wait(ff_mm, 4)
                    turn.wait(ff_dve, 4)
                    act.activation(fr[:, :], PJ1, ACT.Ln, bias=core.small[:, EPS_COL:EPS_COL + 1]).then_inc(ff_act.sem, 1)
                    turn.wait(ff_act, 3)
                    act.activation(fr[:, :], fr[:, :], ACT.Exp, scale=-0.5).then_inc(ff_act.sem, 1)
                sr = item(s, 1, whole, stats)
                if sr is not None:
                    turn.wait(ssc_done, sr + 1)
                    turn.wait(qkr_done, sr - 1)
                    act.activation(inv[:, sr % 2, :], ssq[:, sr % 2, :], ACT.Ln, scale=NORM_SCALE).then_inc(ln_done.sem, 1)
                    turn.wait(ln_done, sr + 1)
                    act.activation(inv[:, sr % 2, :], inv[:, sr % 2, :], ACT.Exp, scale=-0.5, bias=core.small[:, LN_UP_COL:LN_UP_COL + 1]).then_inc(inv_done.sem, 1)
                    gv, tv = divmod(sr, TB)
                    if tv < 3:
                        turn.wait(v_ready, 3 * gv + tv + 1)
                        if tv < 2:
                            act.activation(vs[:, gv, 2 * tv:2 * tv + 2, :], PJ1.rearrange("p (t c) -> p t c", t=2), ACT.Copy).then_inc(v_kept.sem, 1)
                        else:
                            act.activation(vc[:, gv, :], PJ1[:, 0:256], ACT.Copy).then_inc(v_kept.sem, 1)
                sc = item(s, LAG_AV, whole, stats)
                if sc is not None:
                    turn.wait(pt_ready, sc + 1)
                    turn.wait(av_ready, sc - 1)
                    act.activation(pt[:, sc % 2, :], TR1, ACT.Copy).then_inc(pt_kept.sem, 1)
                if s in O_GROUP and (whole or O_GROUP[s] < 0):
                    gg = O_GROUP[s]
                    turn.wait(av_ready, 4 * gg + 4)
                    turn.wait(wo_ready, gg)
                    act.activation(ot[:, :, :], ps[:, PO[0]:PO[1] + 1, :], ACT.Copy).then_inc(o_kept.sem, 1)
                if whole and s < SLOTS:
                    turn.wait(qk_ready, s + 1)
                    turn.wait(ss_done, s - 1)
                    act.activation(sq[:, s % 2, :], PJ0, ACT.Square).then_inc(sq_done.sem, 1)
                ss = item(s, LAG_S, whole, stats)
                if ss is not None:
                    turn.wait(max_done, ss + 1)
                    turn.wait(pn_done, ss - 1)
                    turn.wait(recip_done, ss - 1)
                    turn.wait(pnd_done, ss - 1)
                    for h in range(4):
                        last = act.activation(pr[:, ss % 2, h, :], ps[:, SS[ss % 2], h * KEYS:h * KEYS + KEYS], ACT.Exp,
                                              bias=neg[:, ss % 2, h:h + 1], accum_out=den[:, ss % 2, h:h + 1])
                    last.then_inc(exp_done.sem, 1)
                if s == 13 and stats:
                    turn.wait(ff_dve, 4)
                    act.activation(fq[:, :], fc[:, :], ACT.Square).then_inc(ff_act.sem, 1)
                if s == 2:
                    turn.wait(ff_dve, 1)
                    turn.wait(ff_mm, 0)
                    ff_weights(act, turn)
                    act.activation(fh[:, :], fx[:, :], ACT.Identity, scale=ffc[:, 0:1], bias=ffc[:, 1:2]).then_inc(ff_act.sem, 1)
                if s == TURN_SLOTS - 2:
                    for j in range(3):
                        rows = FF_ROWS[j]
                        if j < 2:
                            turn.wait(ff_mm, 5 + j)
                        else:
                            turn.wait(ff_dve, 2)
                        gate = (PJ0, PJ1, third[:, 0, :])[j]
                        act.activation(gl[0:rows, j, :], gate[0:rows, :], ACT.Gelu, bias=ffc[0:rows, 6 + j:7 + j]).then_inc(ff_act.sem, 1)
                    act.preload_act_table_set("natural_log_exp_and_others")

            with act.Fori(0, DEPTH) as l:
                with act.Fori(0, BATCH) as b:
                    turn = Turn(act, l, b)
                    for s in range(TURN_SLOTS):
                        slot(turn, s, True, True)
            turn = Turn(act, DEPTH, 0)
            for s in range(TURN_SLOTS):
                slot(turn, s, False, True)
            turn = Turn(act, DEPTH, 1)
            slot(turn, 2, False, False)
            turn.wait(ff_act, 1)
            act.sem_inc(ff_act.sem, 3)
            slot(turn, TURN_SLOTS - 2, False, False)

        def shifted(dve, to, at, row, sem):
            col = row * SEQ
            dve.tensor_scalar(to[0:64, at:at + SEQ], z[0:64, bass.ds(col, SEQ)], 1.0, None, ALU.mult)
            dve.tensor_scalar(to[64:P, at + 1:at + SEQ], z[64:P, bass.ds(col, SEQ - 1)], 1.0, None, ALU.mult).then_inc(sem, 1)

        def tails(dve):
            dve.tensor_copy(xtail[:, :, :], xs[:, WIN:].rearrange("p (t c) -> p t c", t=TB)[:, :, P - WIN:]).then_inc(xs_done.sem, 1)

        @block.vector
        def _(dve):
            start_ahead(dve, "dve")
            for nought in (ps[:, 3, :], ps[:, PO[0]:PO[1] + 1, :], vs[:, UNITS - 1, :, :], vc[:, UNITS - 1, :], qt[:, 1, :],
                           fc[:, :], fr[:, :], pr[:, 0, :, :], rden[:, 0, :], pb[:, 1, :, :, :], pn[:, :, :, :], ot[:, :, :]):
                dve.memset(nought, 0.0).then_inc(cleared.sem, 1)
            dve.wait_ge(cleared.sem, cleared.at(CLEARED))
            shifted(dve, xs, WIN, 0, shift_done.sem)
            dve.wait_ge(shift_done.sem, shift_done.at(1))
            tails(dve)
            dve.sem_inc(tables_done.sem, 2)
            dve.wait_ge(ld_tables.sem, ld_tables.at(64))
            dve.tensor_copy(band[:, :], bandf[:, :]).then_inc(tables_done.sem, 1)

            def product(turn, j):
                rows = FF_ROWS[j]
                turn.wait(ff_act, 5 + j)
                if j < 2:
                    turn.wait(ff_mm, 7 + j)
                value = (PJ0, PJ1, third[:, 1, :])[j]
                dve.scalar_tensor_tensor(fm[0:rows, j, :], value[0:rows, :], ffc[0:rows, 3 + j:4 + j], gl[0:rows, j, :], ALU.add, ALU.mult).then_inc(ff_dve.sem, 1)

            def slot(turn, s, whole, stats, b, before, two_before):
                t = s % TB
                if s == TURN_SLOTS - 1:
                    product(turn, 2)
                sr = item(s, LAG_KEEP, whole, stats)
                if sr is not None:
                    st = sr % TB
                    turn.wait(q_kept, sr + 1)
                    turn.wait(s_ready, sr - 2)
                    for e in range(2):
                        rows = slice(64 * e, 64 * e + 64)
                        last = dve.tensor_copy(kz[rows, e::2, WIN + st * P:WIN + st * P + P], TR0[rows, 256:512].rearrange("p (k c) -> p k c", k=2))
                    last.then_inc(k_kept.sem, 1)
                ss = item(s, LAG_S, whole, stats)
                if ss is not None:
                    turn.wait(s_ready, ss + 1)
                    turn.wait(exp_done, ss - 1)
                    scores = ps[:, SS[ss % 2], 0:4 * KEYS].rearrange("p (h c) -> p h c", h=4)
                    dve.tensor_reduce(neg[:, ss % 2, :], scores, AX.X, ALU.max, negate=True).then_inc(max_done.sem, 1)
                sc = item(s, LAG_PT, whole, stats)
                if sc is not None:
                    turn.wait(recip_done, sc + 1)
                    turn.wait(pt_ready, sc - 1)
                    over_sum(dve, 0, sc)
                    over_sum(dve, 1, sc).then_inc(pnd_done.sem, 1)
                if s == TURN_SLOTS - 1:
                    product(turn, 0)
                    product(turn, 1)
                if s == 1:
                    turn.wait(ff_act, 0)
                    dve.tensor_tensor(fx[:, :], fc[:, :], fr[:, :], ALU.mult).then_inc(ff_dve.sem, 1)
                if s in (4, 8):
                    turn.wait(ff_mm, s // 4)
                    turn.wait(ff_act, 0)
                    dve.tensor_copy(third[:, s // 4 - 1, :], PJ1[0:FF_ROWS[2], :]).then_inc(ff_dve.sem, 1)
                if s == 12 and stats:
                    turn.wait(ff_mm, 3)
                    dve.tensor_tensor(fc[:, :], fs[:, :], PJ1, ALU.subtract).then_inc(ff_dve.sem, 1)
                sv = item(s, LAG_AV, whole, stats)
                if sv is not None and sv % TB == 3:
                    gg = sv // TB
                    turn.wait(pbt_ready, gg + 1)
                    turn.wait(av_ready, 4 * gg)
                    dve.tensor_tensor(pbt[:, :, :, :], TR0[:, 0:4 * WIN].rearrange("p (h c) -> p h c", h=4)[:, :, None, :].to_broadcast([P, 4, TB, WIN]),
                                      quad[:, None, :, None].to_broadcast([P, 4, TB, WIN]), ALU.mult).then_inc(pbt_kept.sem, 1)
                if whole and s < SLOTS:
                    turn.wait(sq_done, s + 1)
                    turn.wait(qkr_done, s - 1)
                    both = PJ0.rearrange("p (s h c) -> p s h c", s=2, h=4)
                    table = rope[:, 0, t, :].rearrange("p (s c) -> p s c", s=2)[:, :, None, :].to_broadcast([P, 2, 4, HD])
                    dve.tensor_tensor(ra[:, s % 2, :].rearrange("p (s h c) -> p s h c", s=2, h=4), both, table, ALU.mult)
                    halves = PJ0.rearrange("p (s h e c) -> p s h e c", s=2, h=4, e=2)[:, :, :, ::-1, :]
                    tableh = rope[:, 1, t, :].rearrange("p (s e c) -> p s e c", s=2, e=2)[:, :, None, :, :].to_broadcast([P, 2, 4, 2, HD // 2])
                    dve.tensor_tensor(rb[:, s % 2, :].rearrange("p (s h e c) -> p s h e c", s=2, h=4, e=2), halves, tableh, ALU.mult).then_inc(rope_done.sem, 1)
                if s in WO_GROUP and (whole or stats and WO_GROUP[s] < 0):
                    gg = WO_GROUP[s]
                    turn.wait(z_added, gg)
                    turn.wait(wo_ready, gg + 1)
                    row = bass.ds(before if gg < 0 else b * SEQ, SEQ)
                    dve.tensor_tensor(z[:, row], z[:, row], PJ1, ALU.add).then_inc(z_added.sem, 1)
                if whole and s < SLOTS:
                    turn.wait(inv_done, s - 1)
                    dve.tensor_reduce(ssq[:, s % 2, :], sq[:, s % 2, :].rearrange("p (h c) -> p h c", h=8), AX.X, ALU.add).then_inc(ss_done.sem, 1)
                    turn.wait(ss_done, s + 1)
                    dve.tensor_scalar(ssq[:, s % 2, :], ssq[:, s % 2, :], 1e-24, None, ALU.max).then_inc(ssc_done.sem, 1)
                if ss is not None:
                    turn.wait(exp_done, ss + 1)
                    turn.wait(pn_done, ss - 1)
                    dve.reciprocal(rden[:, ss % 2, :], den[:, ss % 2, :]).then_inc(recip_done.sem, 1)
                if s == 8 and stats:
                    turn.wait(z_added, 0)
                    shifted(dve, fs, 0, (b + (BATCH - 1)) % BATCH if whole else BATCH - 1, fs_done.sem)
                if s == TURN_SLOTS - 2:
                    if whole:
                        turn.wait(v_ready, 3 * UNITS)
                        turn.wait(qk_ready, SLOTS)
                        shifted(dve, xs, WIN, (b + 1) % BATCH, shift_done.sem)
                        dve.wait_ge(shift_done.sem, turn.turn + (shift_done.start + 2))
                        tails(dve)
                if s == TURN_SLOTS - 1:
                    turn.wait(ff_mm, 9)
                    row = bass.ds(two_before, SEQ)
                    dve.scalar_tensor_tensor(z[:, row], PJ1, ffc[:, 2:3], z[:, row], ALU.add, ALU.add).then_inc(ff_dve.sem, 1)

            with dve.Fori(0, DEPTH) as l:
                dve.wait_ge(ld_scales.sem, l * 128 + (ld_scales.start + 128))
                for k in range(2):
                    dve.tensor_tensor(rope[:, k, :, :], base[:, k, :, :],
                                      scales[:, k, :, :, :].rearrange("p s e c -> p (s e c)")[:, None, :].to_broadcast([P, TB, 2 * HD]), ALU.mult).then_inc(tables_done.sem, 1)
                with dve.Fori(0, BATCH) as b:
                    turn = Turn(dve, l, b)
                    before = ((b + (BATCH - 1)) % BATCH) * SEQ
                    two_before = ((b + (BATCH - 2)) % BATCH) * SEQ
                    for s in range(TURN_SLOTS):
                        if s == 0:
                            dve.wait_ge(tables_done.sem, l * 2 + (tables_done.start + 5))
                        slot(turn, s, True, True, b, before, two_before)
            turn = Turn(dve, DEPTH, 0)
            for s in range(TURN_SLOTS):
                slot(turn, s, False, True, None, (BATCH - 1) * SEQ, (BATCH - 2) * SEQ)
            turn = Turn(dve, DEPTH, 1)
            for s in (1, 4, 8):
                slot(turn, s, False, False, None, None, (BATCH - 1) * SEQ)
            turn.wait(ff_dve, 3)
            dve.sem_inc(ff_dve.sem, 1)
            slot(turn, TURN_SLOTS - 1, False, False, None, None, (BATCH - 1) * SEQ)

    turns = DEPTH * BATCH
    for e, k in per_turn.items():
        e.past(turns * k + (k if e in (xs_done, fs_done) else 2 * k if e in (ff_mm, ff_act, ff_dve) else 0))
    shift_done.past(1 + turns)
    tables_done.past(3 + 2 * DEPTH)
    cleared.past(CLEARED)
    ld_wq.past(16 + 16 * DEPTH)
    ld_scales.past(128 * DEPTH)
    ld_wo.past(16 * DEPTH)
    ld_ff.past(16 + 16 * FF_LOADS * DEPTH)
    ld_tables.past(64)


def swiglu(core, first):
    nc, d, x, z, ps = core.nc, core.d, core.x, core.z, core.ps
    ld_w, floated, scaled, turned, kept = core.events("sw_ld", "sw_floated", "sw_scaled", "sw_turned", "sw_kept")
    gate_mm, up_mm, y_mm, silu_done, h_done, added = core.events("sw_gate", "sw_up", "sw_y", "sw_silu", "sw_h", "sw_added")
    T = 3
    per_turn = {gate_mm: T, up_mm: T, silu_done: T, h_done: T, y_mm: 1, added: 1}
    if first:
        core.sw = core.sb(core.ctx, "sw", [P, 3, T, P])
    w = core.sw
    if first:
        with ExitStack() as ctx:
            wi = core.sb(ctx, "wi", [P, 3, T, P], I32)
            wf = core.sb(ctx, "wf", [P, 3, T, P])
            block = ctx.enter_context(nc.Block())

            @block.sync
            def _(sp):
                sp.dma_start(wi[:, 0, :, :], d["L1_ffn_w_gate"].rearrange("(t p) c -> p t c", p=P)).then_inc(ld_w.sem, 16)
                sp.dma_start(wi[:, 1, :, :], d["L1_ffn_w_up"].rearrange("(t p) c -> p t c", p=P)).then_inc(ld_w.sem, 16)
                sp.dma_start(wi[:, 2, :, :], d["L1_ffn_w_down"].rearrange("p (t c) -> p t c", c=P)).then_inc(ld_w.sem, 16)

            @block.vector
            def _(dve):
                dve.wait_ge(ld_w.sem, 48)
                dve.tensor_copy(wf[:, :, :, :], wi[:, :, :, :]).then_inc(floated.sem, 1)
                dve.wait_ge(floated.sem, 1)
                dve.tensor_scalar(wf[:, :, :, :], wf[:, :, :, :], float(np.float32(1.0 / 127.0)), None, ALU.mult).then_inc(scaled.sem, 1)
                for k in range(3):
                    dve.wait_ge(turned.sem, k + 1)
                    dve.tensor_copy(w[:, k, :, :], ps[:, k, 0:T * P].rearrange("p (t c) -> p t c", t=T)).then_inc(kept.sem, 1)

            @block.tensor
            def _(pe):
                pe.wait_ge(scaled.sem, 1)
                for k in range(3):
                    for t in range(T):
                        last = pe.transpose(ps[:, k, t * P:t * P + P], wf[:, k, t, :], core.ident[:, :])
                    last.then_inc(turned.sem, 1)

    for e in per_turn:
        e.past(AHEAD)
    with ExitStack() as ctx:
        sg = core.sb(ctx, "sg", [P, T, SEQ])
        sh = core.sb(ctx, "sh", [P, T, SEQ])
        block = ctx.enter_context(nc.Block())

        @block.tensor
        def _(pe):
            for e in (gate_mm, up_mm, y_mm):
                pe.sem_inc(e.sem, AHEAD)
            with pe.Fori(0, BATCH) as b:
                turn = Counts(pe, b, per_turn)
                zb = z[:, bass.ds(b * SEQ, SEQ)]
                for t in range(T):
                    turn.wait(silu_done, t + 1 - T)
                    pe.matmul(ps[:, t, :], w[:, 0, t, :], zb, start=True, stop=True).then_inc(gate_mm.sem, 1)
                    turn.wait(h_done, t + 1 - T)
                    pe.matmul(ps[:, T + t, :], w[:, 1, t, :], zb, start=True, stop=True).then_inc(up_mm.sem, 1)
                turn.wait(added, 0)
                for t in range(T):
                    turn.wait(h_done, t + 1)
                    last = pe.matmul(ps[:, 2 * T, :], w[:, 2, t, :], sh[:, t, :], start=t == 0, stop=t == T - 1)
                last.then_inc(y_mm.sem, 1)

        @block.scalar
        def _(act):
            act.sem_inc(silu_done.sem, AHEAD)
            act.preload_act_table(ACT.Silu)
            with act.Fori(0, BATCH) as b:
                turn = Counts(act, b, per_turn)
                for t in range(T):
                    turn.wait(gate_mm, t + 1)
                    turn.wait(h_done, t + 1 - T)
                    act.activation(sg[:, t, :], ps[:, t, :], ACT.Silu).then_inc(silu_done.sem, 1)

        @block.vector
        def _(dve):
            dve.sem_inc(h_done.sem, AHEAD)
            dve.sem_inc(added.sem, AHEAD)
            with dve.Fori(0, BATCH) as b:
                turn = Counts(dve, b, per_turn)
                for t in range(T):
                    turn.wait(y_mm, 0)
                    turn.wait(up_mm, t + 1)
                    turn.wait(silu_done, t + 1)
                    dve.tensor_tensor(sh[:, t, :], sg[:, t, :], ps[:, T + t, :], ALU.mult).then_inc(h_done.sem, 1)
                turn.wait(y_mm, 1)
                xb = x[:, bass.ds(b * SEQ, SEQ)]
                dve.tensor_tensor(xb, xb, ps[:, 2 * T, :], ALU.add).then_inc(added.sem, 1)
    for e, k in per_turn.items():
        e.past(BATCH * k)


PARTS = 3
STACK = PARTS * PARTS * SD
M_ROW = STACK


def load_output_weights(core, sp, wp, w, sem):
    rows = w.rearrange("(g j c) m -> j c g m", g=SG, j=4)
    for j in range(4):
        sp.dma_start(wp[32 * j:32 * j + SD, :, :], rows[j]).then_inc(sem, 16)


def small_attention(core, kind):
    nc, d, x, z, ps = core.nc, core.d, core.x, core.z, core.ps
    causal = kind != "norm"
    ev = core.events
    scale = float(SD) ** -0.5
    n = "L0_attn_a" if kind == "norm" else "L0_attn_b" if kind == "latent" else "L1_attn_b"
    if causal:
        q_pieces = [[(3, 0)], [(0, 0), (2, P)], [(1, 0)]]
        k_pieces = [[(0, 0)], [(1, 0), (3, 3 * P)], [(2, 0)]]
        part = {j: (off, SEQ - P * j) for j, off in enumerate((0, 512, 1024, 896))}
    else:
        q_pieces = [[(i, 0)] for i in range(TB)]
        k_pieces = [[(j, 0)] for j in range(TB)]
        part = {j: (512 * j, SEQ) for j in range(TB)}
    width = 1280 if causal else 2048
    NP = len(q_pieces)
    order = [(p, n) for n in range(NP) for p in "qk"] if not causal else [(p, n) for p in "qk" for n in range(NP)]
    Q_BANKS, K_BANKS, AV_BANK, MISC_BANK = (0, 1, 2), (3, 4, 5), 6, 7
    LAG = 7
    RING = 8 if causal else 6
    V_BANK = 1 if kind == "latent" else 2
    STEPS = SH + LAG + 2

    ld_w, prep_dve, prep_pe, prep_pool = ev("sa_ld_w", "sa_prep_dve", "sa_prep_pe", "sa_prep_pool")
    proj_mm, s_mm, mt_mm, st_mm, av_mm, sum_mm, y_mm = ev(
        "sa_proj_mm", "sa_s_mm", "sa_mt_mm", "sa_st_mm", "sa_av_mm", "sa_sum_mm", "sa_y_mm")
    proj_act, exp_done, out_kept, ln_done, recip_done = ev(
        "sa_proj_act", "sa_exp_done", "sa_out_kept", "sa_ln_done", "sa_recip_done")
    v_early = ev("sa_v_early")
    row_kept, v_kept, qk_normed, cut_done, max_done, mcut_done, out_normed, added = ev(
        "sa_row_kept", "sa_v_kept", "sa_qk_normed", "sa_cut_done", "sa_max_done", "sa_mcut_done", "sa_out_normed", "sa_added")
    ld_stack, *ld_m = ev("sa_ld_stack", "sa_ld_m_even", "sa_ld_m_odd")
    n_mm = {"norm": 4, "latent": 2, "plain": 1}[kind]
    n_act = {"norm": 5, "latent": 2, "plain": 1}[kind]
    owner = {
        "pe": {proj_mm: n_mm, s_mm: NP * SH, mt_mm: SG, st_mm: NP * SH, av_mm: SG, sum_mm: SG, y_mm: 1},
        "act": {proj_act: n_act, exp_done: NP * SH, out_kept: SG, ln_done: SG, recip_done: SG},
        "dve": {row_kept: 1, v_early: 1, v_kept: 1, qk_normed: 1, cut_done: 5, max_done: NP * SH, mcut_done: 6 * SG, out_normed: SG, added: 1},
    }
    if kind != "norm":
        del owner["dve"][qk_normed]
    per_turn = {e: k for es in owner.values() for e, k in es.items()}
    for e in per_turn:
        e.past(AHEAD)
    loads = 2 * PARTS * PARTS
    LOOK_BACK = 2 * 16 * PARTS
    for e in (ld_stack, *ld_m):
        e.past(LOOK_BACK)
    per_turn[ld_stack] = 16 * loads
    for e in ld_m:
        per_turn[e] = 16 * PARTS * SG // 2

    with ExitStack() as ctx:
        sb = lambda *a: core.sb(ctx, *a)
        w = sb("w", [P, 3, P])
        wp = sb("wp", [P, SG, P])
        gb = sb("gb", [P, 4])
        sums = sb("sums", [P, P])
        mean8 = sb("mean8", [P, P])
        cmask = sb("cmask", [P, P], BF16)
        qs = sb("qs", [P, 2, SH, SEQ], BF16)
        ks = sb("ks", [P, 2, SH, SEQ], BF16)
        vt = sb("vt", [P, SEQ])
        va = sb("va", [P, TB, SH, 32])
        hb = sb("hb", [P, SEQ])
        xf = sb("xf", [P, 2, SEQ])
        x1 = sb("x1", [P, 2, SEQ])
        cut = sb("cut", [P, PARTS, 2, SEQ], BF16)
        nm = sb("nm", [P, SH, TB])
        mf = sb("mf", [4 * TB, P])
        m1 = sb("m1", [4 * TB, P])
        mcut = sb("mcut", [4 * TB, 2, PARTS, P], BF16)
        pt = sb("pt", [P, RING, width])
        ou = sb("ou", [P, 2, SEQ])
        rr = sb("rr", [P, 2, SEQ])
        on = sb("on", [P, SG, SEQ])

        with ExitStack() as prep:
            tmp = core.sb(prep, "tmp", [P, 4, P])
            mean = core.sb(prep, "mean", [P, 2, SH])
            block = prep.enter_context(nc.Block())
            @block.gpsimd
            def _(pool):
                pool.memset(wp[:, :, :], 0.0).then_inc(prep_pool.sem, 1)
                pool.memset(va[:, :, :, :], 0.0).then_inc(prep_pool.sem, 1)
                pool.memset(tmp[:, 3, :], 0.0).then_inc(prep_pool.sem, 1)
                pool.wait_ge(prep_pool.sem, prep_pool.at(3))
                pool.memset(va[:, :, :, SD:SD + 1], 1.0).then_inc(prep_pool.sem, 1)

            @block.sync
            def _(sp):
                sp.dma_start(sums[:, :], d["sum_rows"]).then_inc(ld_w.sem, 16)
                if kind == "norm":
                    sp.dma_start(mean8[:, :], d["mean_of_8"]).then_inc(ld_w.sem, 16)
                    sp.dma_start(tmp[:, 0:3, :], d[f"{n}_w_qkv"].rearrange("p (s c) -> p s c", s=3)).then_inc(ld_w.sem, 16)
                    for col, name in enumerate(("q_gamma", "q_beta", "k_gamma", "k_beta")):
                        for c in range(SD):
                            sp.dma_start(gb[SH * c:SH * c + SH, col:col + 1], d[f"{n}_{name}"][c:c + 1].rearrange("(a c) -> a c", a=1).to_broadcast([SH, 1])).then_inc(ld_w.sem, 16)
                elif kind == "latent":
                    sp.dma_start(tmp[:, 0, :], d["causal"]).then_inc(ld_w.sem, 16)
                    sp.dma_start(w[:, 0, 0:32], d[f"{n}_W_dq"]).then_inc(ld_w.sem, 16)
                    sp.dma_start(w[:, 0, 32:64], d[f"{n}_W_dkv"]).then_inc(ld_w.sem, 16)
                    sp.dma_start(tmp[0:32, 1, :], d[f"{n}_W_uq"]).then_inc(ld_w.sem, 16)
                    sp.dma_start(tmp[0:32, 2, :], d[f"{n}_W_uk"]).then_inc(ld_w.sem, 16)
                    sp.dma_start(mean8[0:32, :], d[f"{n}_W_uv"]).then_inc(ld_w.sem, 16)
                else:
                    sp.dma_start(mean8[:, :], d["causal"]).then_inc(ld_w.sem, 16)
                    sp.dma_start(tmp[:, 0:3, :], d[f"{n}_w_qkv"].rearrange("s h c m -> (h c) s m")).then_inc(ld_w.sem, 16)
                    sp.dma_start(rr[:, 0, 0:P], d[f"{n}_w_o"]).then_inc(ld_w.sem, 16)
                sp.wait_ge(prep_pool.sem, prep_pool.at(1))
                if kind != "plain":
                    load_output_weights(core, sp, wp, d[f"{n}_w_proj" if kind == "norm" else f"{n}_W_o"], ld_w.sem)

            by_channel = lambda a: a.rearrange("p s (c h) -> p s h c", h=SH)
            n_ld = {"norm": 3 + 4 * SD + 4, "latent": 7 + 4, "plain": 4}[kind]

            @block.vector
            def _(dve):
                dve.memset(ks[64:96, :, :, :], 1.0)
                dve.wait_ge(ld_w.sem, ld_w.at(16 * n_ld))
                if kind == "norm":
                    heads = tmp[:, 0:2, :].rearrange("p s (h c) -> p s h c", c=SD)
                    dve.tensor_reduce(mean[:, :, :], heads, AX.X, ALU.add).then_inc(prep_dve.sem, 1)
                    dve.wait_ge(prep_dve.sem, prep_dve.at(1))
                    dve.tensor_scalar(mean[:, :, :], mean[:, :, :], 1.0 / SD, None, ALU.mult).then_inc(prep_dve.sem, 1)
                    dve.wait_ge(prep_dve.sem, prep_dve.at(2))
                    dve.tensor_tensor(by_channel(w[:, 0:2, :]), heads, mean[:, :, :, None].to_broadcast([P, 2, SH, SD]), ALU.subtract).then_inc(prep_dve.sem, 1)
                    dve.tensor_copy(w[:, 2, :], tmp[:, 2, :])
                    dve.tensor_scalar(gb[:, 0:2], gb[:, 0:2], scale, None, ALU.mult).then_inc(prep_dve.sem, 1)
                elif kind == "latent":
                    dve.tensor_copy(by_channel(w[0:32, 1:3, :]), tmp[0:32, 1:3, :].rearrange("p s (h c) -> p s h c", c=SD))
                    dve.tensor_copy(cmask[:, :], tmp[:, 0, :]).then_inc(prep_dve.sem, 1)
                else:
                    dve.tensor_copy(cmask[:, :], mean8[:, :]).then_inc(prep_dve.sem, 1)
                    dve.wait_ge(prep_pool.sem, prep_pool.at(3))
                    for g in range(SG):
                        if g:
                            dve.wait_ge(prep_pe.sem, prep_pe.at(1 + g))
                        dve.tensor_copy(tmp[:, 3, :].rearrange("p (j c) -> p j c", j=4)[:, :, 0:SD],
                                        rr[:, 0, g * 32:g * 32 + 32].rearrange("p (j c) -> p j c", j=4)).then_inc(prep_dve.sem, 1)
                    dve.wait_ge(prep_pe.sem, prep_pe.at(5))
                    dve.tensor_copy(by_channel(w[:, 0:2, :]), ps[:, 0, 0:2 * P].rearrange("p (s h c) -> p s h c", s=2, c=SD))
                    dve.tensor_copy(w[:, 2, :], ps[:, 0, 2 * P:3 * P])
                    dve.tensor_copy(wp[:, :, :], ps[:, 1, :].rearrange("p (g c) -> p g c", g=SG)).then_inc(prep_dve.sem, 1)

            if kind == "plain":
                @block.tensor
                def _(pe):
                    pe.wait_ge(ld_w.sem, ld_w.at(16 * n_ld))
                    for s in range(3):
                        last = pe.transpose(ps[:, 0, s * P:s * P + P], tmp[:, s, :], core.ident[:, :])
                    last.then_inc(prep_pe.sem, 1)
                    for g in range(SG):
                        pe.wait_ge(prep_dve.sem, prep_dve.at(2 + g))
                        pe.transpose(ps[:, 1, g * P:g * P + P], tmp[:, 3, :], core.ident[:, :]).then_inc(prep_pe.sem, 1)
            ld_w.past(16 * n_ld)
            prep_dve.past({"norm": 4, "latent": 1, "plain": 6}[kind])
            prep_pe.past(5 if kind == "plain" else 0)
            prep_pool.past(4)

        block = ctx.enter_context(nc.Block())

        def sums_by(k):
            return len([kk for kk in range(k) if kk - LAG >= 5 and (kk - LAG) % 4 == 1])

        def sum_of(pe, turn, gg, k):
            turn.wait(out_kept, gg + 1)
            turn.wait(mcut_done, 6 * min(k // 4, SG) - 5)
            turn.wait(ln_done, gg)
            pe.matmul(ps[:, MISC_BANK, :], sums[:, :], ou[:, gg % 2, :], start=True, stop=True).then_inc(sum_mm.sem, 1)

        @block.sync
        def _(sp):
            def stacks(nxt, row):
                nxt.wait(st_mm, -NP * SH)
                for part_ in range(PARTS):
                    nxt.wait(cut_done, 2 * part_ + 1)
                    for to, s, p, c in [(qs, 0, c // PARTS, c) for c in range(PARTS * PARTS)] + [(ks, 1, c % PARTS, c) for c in range(PARTS * PARTS)]:
                        if p != part_:
                            continue
                        rows = slice(SD * c, SD * c + SD)
                        sp.dma_start(to[rows, row % 2, :, :], cut[:, p, s, :]).then_inc(ld_stack.sem, 16)

            def maxima(turn, row):
                for g in range(SG):
                    turn.wait(mcut_done, 6 * g + 6)
                    for c in range(PARTS):
                        sp.dma_start(qs[M_ROW + c:M_ROW + c + 1, row % 2, 4 * g:4 * g + 4, :].rearrange("o h (i t) -> o (h i) t", i=TB), mcut[:, g % 2, c, :]).then_inc(ld_m[g % 2].sem, 16)

            for e in (ld_stack, *ld_m):
                sp.sem_inc(e.sem, LOOK_BACK)
            stacks(Counts(sp, 0, per_turn), 0)
            for b in range(BATCH - 1):
                turn = Counts(sp, b, per_turn)
                maxima(turn, b)
                stacks(turn.next(), b + 1)
            maxima(Counts(sp, BATCH - 1, per_turn), BATCH - 1)

        @block.tensor
        def _(pe):
            for e in owner["pe"]:
                pe.sem_inc(e.sem, AHEAD)

            def prepare(nxt, step):
                if step == 0:
                    nxt.wait(max_done, 0)
                    nxt.wait(row_kept, 1)
                    if kind == "latent":
                        pe.matmul(ps[0:32, 0, :], w[:, 0, 0:32], hb[:, :], start=True, stop=True)
                        pe.matmul(ps[0:32, 1, :], w[:, 0, 32:64], hb[:, :], start=True, stop=True).then_inc(proj_mm.sem, 1)
                    else:
                        for s in range(2):
                            last = pe.matmul(ps[:, s, :], w[:, s, :], hb[:, :], start=True, stop=True)
                        if kind == "norm":
                            last.then_inc(proj_mm.sem, 1)
                        else:
                            values(hb, w[:, 2, :])
                if step == 1 and kind == "latent":
                    nxt.wait(proj_act, 1)
                    pe.matmul(ps[:, 2, :], w[0:32, 1, :], xf[0:32, 0, :], start=True, stop=True)
                    pe.matmul(ps[:, 0, :], w[0:32, 2, :], xf[0:32, 1, :], start=True, stop=True)
                    values(xf[0:32, 1, :], mean8[0:32, :])
                if step in (1, 2) and kind == "norm":
                    nxt.wait(proj_act, step)
                    pe.matmul(ps[:, 2, :], mean8[:, :], x1[:, step - 1, :], start=True, stop=True).then_inc(proj_mm.sem, 1)
                if step == 3 and kind == "norm":
                    nxt.wait(proj_act, 3)
                    values(hb, w[:, 2, :])

            def values(rows, weights):
                for t in range(TB):
                    last = pe.matmul(ps[:, V_BANK, t * P:t * P + P], rows[:, t * P:t * P + P], weights, start=True, stop=True)
                last.then_inc(proj_mm.sem, 1)

            def row(turn, nxt, b):
                qsr = qs[:, b % 2, :, :]
                ksr = ks[:, b % 2, :, :]
                turn.wait(v_early, 1)
                turn.wait(ld_stack, 16 * loads)
                for k in range(STEPS):
                    h = k - LAG
                    for which, n_ in order:
                        if which == "q" and k < SH:
                            n = NP * k + n_
                            turn.wait(max_done, max(n - 2, 0))
                            bank = ps[:, Q_BANKS[n % 3], :]
                            for i, col in q_pieces[n_]:
                                keys = P * (i + 1) if causal else SEQ
                                if causal:
                                    pe.matmul(bank[:, col + i * P:col + i * P + P], core.ident16[:, :], cmask[:, :], start=True, stop=False, skip_group_check=True)
                                last = pe.matmul(bank[:, col:col + keys], qsr[0:STACK, k, i * P:i * P + P], ksr[0:STACK, k, 0:keys],
                                                 start=not causal, stop=True, skip_group_check=True)
                            last.then_inc(s_mm.sem, 1)
                        if which == "k" and n_ == 0 and k % 4 == 0 and 0 < k <= SH:
                            g = k // 4 - 1
                            turn.wait(max_done, NP * k)
                            if g == 0:
                                turn.wait(added, 0)
                            turn.wait(ln_done, sums_by(k))
                            pe.matmul(ps[0:4 * TB, MISC_BANK, 0:P], nm[:, 4 * g:4 * g + 4, :].rearrange("p h i -> p (h i)"), core.ident[:, :], start=True, stop=True).then_inc(mt_mm.sem, 1)
                        if which == "k" and 0 <= h < SH:
                            if n_ == 0 and h % 4 == 0:
                                turn.wait(ld_m[h // 4 % 2], 16 * PARTS * (h // 8 + 1))
                            n = NP * h + n_
                            turn.wait(exp_done, max(n - 2, 0))
                            bank = ps[:, K_BANKS[n % 3], :]
                            for j, col in k_pieces[n_]:
                                q0 = P * j if causal else 0
                                cols = part[j][1]
                                if causal:
                                    pe.matmul(bank[:, col:col + P], cmask[:, :], core.ident16[:, :], start=True, stop=False, skip_group_check=True)
                                last = pe.matmul(bank[:, col:col + cols], ksr[0:M_ROW + PARTS, h, j * P:j * P + P],
                                                 qsr[0:M_ROW + PARTS, h, q0:SEQ], start=not causal, stop=True, skip_group_check=True)
                            last.then_inc(st_mm.sem, 1)
                    if h >= 4 and h % 4 == 0:
                        gg = h // 4 - 1
                        turn.wait(exp_done, 4 * NP * (gg + 1))
                        turn.wait(out_kept, gg)
                        turn.wait(v_kept, 1)
                        for j in range(TB):
                            off, cols = part[j]
                            for hh in range(4):
                                last = pe.matmul(ps[32 * hh:32 * hh + 32, AV_BANK, SEQ - cols:SEQ], va[:, j, 4 * gg + hh, :],
                                                 pt[:, (4 * gg + hh) % RING, off:off + cols], start=j == 0, stop=j == TB - 1, skip_group_check=True)
                        last.then_inc(av_mm.sem, 1)
                    if h >= 5 and h % 4 == 1:
                        sum_of(pe, turn, h // 4 - 1, k)
                    if nxt is not None and k > SH:
                        prepare(nxt, k - SH - 1)
                turn.wait(out_normed, SG)
                turn.wait(ln_done, SG)
                for gg in range(SG):
                    last = pe.matmul(ps[:, MISC_BANK, :], wp[:, gg, :], on[:, gg, :], start=gg == 0, stop=gg == SG - 1)
                last.then_inc(y_mm.sem, 1)

            first = Counts(pe, 0, per_turn)
            for step in range(4):
                prepare(first, step)
            for b in range(BATCH - 1):
                turn = Counts(pe, b, per_turn)
                row(turn, turn.next(), b)
            row(Counts(pe, BATCH - 1, per_turn), None, BATCH - 1)

        @block.scalar
        def _(act):
            for e in owner["act"]:
                act.sem_inc(e.sem, AHEAD)
            act.preload_act_table_set("natural_log_exp_and_others")

            def keep_out(turn, gg):
                turn.wait(av_mm, gg + 1)
                turn.wait(out_normed, gg - 1)
                act.activation(ou[:, gg % 2, :], ps[:, AV_BANK, :], ACT.Copy).then_inc(out_kept.sem, 1)

            def over_sum(turn, gg):
                turn.wait(sum_mm, gg + 1)
                act.activation(rr[:, gg % 2, :], ps[:, MISC_BANK, :], ACT.Ln).then_inc(ln_done.sem, 1)
                turn.wait(ln_done, gg + 1)
                act.activation(rr[:, gg % 2, :], rr[:, gg % 2, :], ACT.Exp, scale=-1.0).then_inc(recip_done.sem, 1)

            def prepare(nxt, step):
                if kind == "norm":
                    if step == 0:
                        nxt.wait(proj_mm, 1)
                        nxt.wait(cut_done, 0)
                        act.activation(x1[:, :, :], ps[:, 0:2, :], ACT.Square).then_inc(proj_act.sem, 1)
                    if step in (1, 2):
                        nxt.wait(proj_mm, step + 1)
                        act.activation(xf[:, step - 1, :], ps[:, 2, :], ACT.Ln, bias=core.small[:, EPS_COL:EPS_COL + 1]).then_inc(proj_act.sem, 1)
                    if step == 2:
                        nxt.wait(proj_act, 3)
                        act.activation(xf[:, :, :], xf[:, :, :], ACT.Exp, scale=-0.5).then_inc(proj_act.sem, 1)
                    if step == 3:
                        nxt.wait(qk_normed, 1)
                        for s in range(2):
                            last = act.activation(xf[:, s, :], x1[:, s, :], ACT.Identity, scale=gb[:, 2 * s:2 * s + 1], bias=gb[:, 2 * s + 1:2 * s + 2])
                        last.then_inc(proj_act.sem, 1)
                if kind == "latent" and step == 0:
                    nxt.wait(proj_mm, 1)
                    nxt.wait(cut_done, 0)
                    act.activation(xf[0:32, :, :], ps[0:32, 0:2, :], ACT.Copy).then_inc(proj_act.sem, 1)
                if kind != "norm" and step == 1:
                    nxt.wait(proj_mm, n_mm)
                    nxt.wait(cut_done, 0)
                    q_bank, k_bank = (2, 0) if kind == "latent" else (0, 1)
                    act.activation(xf[:, 0, :], ps[:, q_bank, :], ACT.Copy, scale=scale)
                    act.activation(xf[:, 1, :], ps[:, k_bank, :], ACT.Copy).then_inc(proj_act.sem, 1)

            def row(turn, nxt):
                for h in range(SH + 2):
                    if h < SH:
                        if h == 0:
                            turn.wait(av_mm, 0)
                        if h >= RING:
                            turn.wait(av_mm, (h - RING) // 4 + 1)
                        for n_, piece in enumerate(k_pieces):
                            n = NP * h + n_
                            col = part[piece[0][0]][0]
                            cols = sum(part[j][1] for j, _ in piece)
                            turn.wait(st_mm, n + 1)
                            act.activation(pt[:, h % RING, col:col + cols], ps[:, K_BANKS[n % 3], 0:cols], ACT.Exp).then_inc(exp_done.sem, 1)
                    if h >= 4 and h % 4 == 0:
                        keep_out(turn, h // 4 - 1)
                    if h >= 5 and h % 4 == 1:
                        over_sum(turn, h // 4 - 1)
                    if nxt is not None and 10 <= h < 14:
                        prepare(nxt, h - 10)

            first = Counts(act, 0, per_turn)
            for step in range(4):
                prepare(first, step)
            for b in range(BATCH - 1):
                turn = Counts(act, b, per_turn)
                row(turn, turn.next())
            row(Counts(act, BATCH - 1, per_turn), None)

        @block.vector
        def _(dve):
            for e in owner["dve"]:
                dve.sem_inc(e.sem, AHEAD)
            def keep_row(nxt, b):
                nxt.wait(proj_mm, 0)
                dve.tensor_scalar(hb[:, :], z[:, bass.ds(b * SEQ, SEQ)], 1.0, None, ALU.mult).then_inc(row_kept.sem, 1)

            def prepare(nxt):
                if kind == "norm":
                    nxt.wait(proj_act, 4)
                    dve.tensor_tensor(x1[:, :, :], ps[:, 0:2, :], xf[:, :, :], ALU.mult).then_inc(qk_normed.sem, 1)
                nxt.wait(proj_mm, n_mm)
                nxt.wait(v_kept, 0)
                if kind == "plain":
                    nxt.wait(proj_act, 1)
                dve.tensor_copy(vt[:, :], ps[:, V_BANK, :]).then_inc(v_early.sem, 1)
                nxt.wait(proj_act, n_act)
                nxt.wait(ld_stack, 0)
                dve.tensor_copy(cut[:, 0, :, :], xf[:, :, :]).then_inc(cut_done.sem, 1)
                nxt.wait(cut_done, 1)
                dve.tensor_tensor(x1[:, :, :], xf[:, :, :], cut[:, 0, :, :], ALU.subtract).then_inc(cut_done.sem, 1)
                nxt.wait(cut_done, 2)
                dve.tensor_copy(cut[:, 1, :, :], x1[:, :, :]).then_inc(cut_done.sem, 1)
                nxt.wait(cut_done, 3)
                dve.tensor_tensor(x1[:, :, :], x1[:, :, :], cut[:, 1, :, :], ALU.subtract).then_inc(cut_done.sem, 1)
                nxt.wait(cut_done, 4)
                dve.tensor_copy(cut[:, 2, :, :], x1[:, :, :]).then_inc(cut_done.sem, 1)

            def normed(turn, gg):
                turn.wait(recip_done, gg + 1)
                dve.tensor_tensor(on[:, gg, :], ou[:, gg % 2, :], rr[:, gg % 2, :], ALU.mult).then_inc(out_normed.sem, 1)

            def row(turn, nxt, b):
                turn.wait(v_early, 1)
                turn.wait(av_mm, 0)
                dve.tensor_copy(va[:, :, :, 0:SD], vt[:, :].rearrange("p (t h c) -> p t h c", t=TB, h=SH)).then_inc(v_kept.sem, 1)
                turn.wait(mt_mm, 0)
                for k in range(SH + 1):
                    if k < SH:
                        for n_, piece in enumerate(q_pieces):
                            n = NP * k + n_
                            turn.wait(s_mm, n + 1)
                            for i, col in piece:
                                keys = P * (i + 1) if causal else SEQ
                                last = dve.tensor_reduce(nm[:, k, i:i + 1], ps[:, Q_BANKS[n % 3], col:col + keys], AX.X, ALU.max, negate=True)
                            last.then_inc(max_done.sem, 1)
                    if k % 4 == 0 and k > 0:
                        g = k // 4 - 1
                        turn.wait(mt_mm, g + 1)
                        turn.wait(ld_m[g % 2], 16 * PARTS * (g // 2))
                        mc = mcut[:, g % 2, :, :]
                        dve.tensor_copy(mf[:, :], ps[0:4 * TB, MISC_BANK, 0:P]).then_inc(mcut_done.sem, 1)
                        turn.wait(mcut_done, 6 * g + 1)
                        dve.tensor_copy(mc[:, 0, :], mf[:, :]).then_inc(mcut_done.sem, 1)
                        turn.wait(mcut_done, 6 * g + 2)
                        dve.tensor_tensor(m1[:, :], mf[:, :], mc[:, 0, :], ALU.subtract).then_inc(mcut_done.sem, 1)
                        turn.wait(mcut_done, 6 * g + 3)
                        dve.tensor_copy(mc[:, 1, :], m1[:, :]).then_inc(mcut_done.sem, 1)
                        turn.wait(mcut_done, 6 * g + 4)
                        dve.tensor_tensor(m1[:, :], m1[:, :], mc[:, 1, :], ALU.subtract).then_inc(mcut_done.sem, 1)
                        turn.wait(mcut_done, 6 * g + 5)
                        dve.tensor_copy(mc[:, 2, :], m1[:, :]).then_inc(mcut_done.sem, 1)
                if nxt is not None:
                    keep_row(nxt, b + 1)
                normed(turn, 0)
                normed(turn, 1)
                if nxt is not None:
                    prepare(nxt)
                normed(turn, 2)
                normed(turn, 3)
                turn.wait(y_mm, 1)
                xb = x[:, bass.ds(b * SEQ, SEQ)]
                dve.tensor_tensor(xb, xb, ps[:, MISC_BANK, :], ALU.add).then_inc(added.sem, 1)

            first = Counts(dve, 0, per_turn)
            keep_row(first, 0)
            prepare(first)
            for b in range(BATCH - 1):
                turn = Counts(dve, b, per_turn)
                row(turn, turn.next(), b)
            row(Counts(dve, BATCH - 1, per_turn), None, BATCH - 1)
    for e, k in per_turn.items():
        e.past(BATCH * k)


def linear_attention(core):
    nc, d, x, z, ps = core.nc, core.d, core.x, core.z, core.ps
    ev = core.events
    ld_w, prep_pool, prep_dve = ev("la_ld_w", "la_prep_pool", "la_prep_dve")
    proj_mm, feat_mm, kv_mm, out_mm, sum_mm, y_mm = ev("la_proj_mm", "la_feat_mm", "la_kv_mm", "la_out_mm", "la_sum_mm", "la_y_mm")
    qk_kept, exp_done, out_kept, ln_done, recip_done = ev("la_qk_kept", "la_exp_done", "la_out_kept", "la_ln_done", "la_recip_done")
    row_kept, v_kept, feat_done, kv_kept, out_normed, added = ev(
        "la_row_kept", "la_v_kept", "la_feat_done", "la_kv_kept", "la_out_normed", "la_added")
    TILES = TB + SG
    owner = {
        "pe": {proj_mm: 2, feat_mm: TILES, kv_mm: 1, out_mm: SG, sum_mm: SG, y_mm: 1},
        "act": {qk_kept: 1, exp_done: TILES, out_kept: SG, ln_done: SG, recip_done: SG},
        "dve": {row_kept: 1, v_kept: 1, feat_done: TILES, kv_kept: 1, out_normed: SG, added: 1},
    }
    per_turn = {e: k for es in owner.values() for e, k in es.items()}
    for e in per_turn:
        e.past(AHEAD)
    KV_BANK, SUM_BANK = 2, 3

    with ExitStack() as ctx:
        sb = lambda *a: core.sb(ctx, *a)
        w = sb("w", [P, 3, P])
        wp = sb("wp", [P, SG, P])
        feat_w = sb("feat_w", [P, SH, 32])
        hoc = sb("hoc", [P, SH])
        pm = sb("pm", [P, 32])
        own = sb("own", [P, P])
        sums = sb("sums", [P, P])
        cols = sb("cols", [P, 2])
        hb = sb("hb", [P, SEQ])
        qk = sb("qk", [P, 2, SEQ])
        va = sb("va", [P, TB, SH, 32])
        fe = sb("fe", [P, 2, SEQ])
        fr = sb("fr", [P, 2, SEQ])
        feats = sb("feats", [P, TILES, SEQ])
        kv = sb("kv", [P, SG, P])
        ou = sb("ou", [P, 2, SEQ])
        rr = sb("rr", [P, 2, SEQ])
        on = sb("on", [P, 2, SEQ])
        block = ctx.enter_context(nc.Block())

        @block.gpsimd
        def _(pool):
            pool.memset(wp[:, :, :], 0.0).then_inc(prep_pool.sem, 1)
            pool.memset(cols[:, 1:2], 1e-8).then_inc(prep_pool.sem, 1)
            pool.memset(va[:, :, :, :], 0.0).then_inc(prep_pool.sem, 1)
            pool.wait_ge(prep_pool.sem, prep_pool.at(3))
            pool.memset(va[:, :, :, SD:SD + 1], 1.0).then_inc(prep_pool.sem, 1)

        @block.sync
        def _(sp):
            sp.dma_start(w[:, :, :], d["L1_attn_a_w_qkv"].rearrange("p (s c) -> p s c", s=3)).then_inc(ld_w.sem, 16)
            sp.dma_start(pm[:, :], d["L1_attn_a_proj_matrix"].rearrange("h c f -> (h c) f")).then_inc(ld_w.sem, 16)
            sp.dma_start(hoc[:, :], d["head_of_channel"]).then_inc(ld_w.sem, 16)
            sp.dma_start(own[:, :], d["own_head"]).then_inc(ld_w.sem, 16)
            sp.dma_start(sums[:, :], d["sum_rows"]).then_inc(ld_w.sem, 16)
            sp.dma_start(cols[:, 0:1], d["L1_attn_a_b_out"].rearrange("(c a) -> c a", a=1)).then_inc(ld_w.sem, 16)
            sp.wait_ge(prep_pool.sem, prep_pool.at(1))
            load_output_weights(core, sp, wp, d["L1_attn_a_w_out"], ld_w.sem)

        @block.tensor
        def _(pe):
            for e in owner["pe"]:
                pe.sem_inc(e.sem, AHEAD)
            pe.wait_ge(ld_w.sem, ld_w.at(160))
            pe.wait_ge(prep_dve.sem, prep_dve.at(1))
            with pe.Fori(0, BATCH) as b:
                turn = Counts(pe, b, per_turn)
                turn.wait(row_kept, 1)
                turn.wait(out_kept, 0)
                for s in range(2):
                    last = pe.matmul(ps[:, s, :], w[:, s, :], hb[:, :], start=True, stop=True)
                last.then_inc(proj_mm.sem, 1)
                turn.wait(ln_done, 0)
                for t in range(TB):
                    last = pe.matmul(ps[:, SUM_BANK, t * P:t * P + P], hb[:, t * P:t * P + P], w[:, 2, :], start=True, stop=True)
                last.then_inc(proj_mm.sem, 1)
                turn.wait(qk_kept, 1)
                for i in range(TILES):
                    turn.wait(exp_done, i - 3)
                    if i < TB:
                        pe.matmul(ps[:, 4 + i % 4, :], qk[:, 1, i * P:i * P + P], feat_w[:, :, :].rearrange("p h f -> p (h f)"),
                                  start=True, stop=True).then_inc(feat_mm.sem, 1)
                    else:
                        g = i - TB
                        pe.matmul(ps[:, 4 + i % 4, :], feat_w[:, 4 * g:4 * g + 4, :].rearrange("p h f -> p (h f)"), qk[:, 0, :],
                                  start=True, stop=True).then_inc(feat_mm.sem, 1)
                turn.wait(v_kept, 1)
                turn.wait(added, 0)
                turn.wait(feat_done, TB)
                for g in range(SG):
                    for t in range(TB):
                        last = pe.matmul(ps[:, KV_BANK, g * P:g * P + P], feats[:, t, g * P:g * P + P],
                                         va[:, t, 4 * g:4 * g + 4, :].rearrange("p h c -> p (h c)"), start=t == 0, stop=t == TB - 1)
                last.then_inc(kv_mm.sem, 1)
                turn.wait(kv_kept, 1)
                for g in range(SG + 2):
                    if g < SG:
                        turn.wait(feat_done, TB + g + 1)
                        turn.wait(out_kept, g - 1)
                        pe.matmul(ps[:, g % 2, :], kv[:, g, :], feats[:, TB + g, :], start=True, stop=True).then_inc(out_mm.sem, 1)
                    if 1 <= g < SG + 1:
                        turn.wait(out_kept, g)
                        turn.wait(ln_done, g - 1)
                        pe.matmul(ps[:, SUM_BANK, :], sums[:, :], ou[:, (g - 1) % 2, :], start=True, stop=True).then_inc(sum_mm.sem, 1)
                    if g >= 2:
                        turn.wait(out_normed, g - 1)
                        last = pe.matmul(ps[:, KV_BANK, :], wp[:, g - 2, :], on[:, g % 2, :], start=g == 2, stop=g == SG + 1)
                last.then_inc(y_mm.sem, 1)

        @block.scalar
        def _(act):
            for e in owner["act"]:
                act.sem_inc(e.sem, AHEAD)
            act.preload_act_table_set("natural_log_exp_and_others")
            act.wait_ge(prep_pool.sem, prep_pool.at(2))
            with act.Fori(0, BATCH) as b:
                turn = Counts(act, b, per_turn)
                turn.wait(proj_mm, 1)
                turn.wait(feat_mm, 0)
                act.activation(qk[:, :, :], ps[:, 0:2, :], ACT.Copy).then_inc(qk_kept.sem, 1)
                for i in range(TILES):
                    turn.wait(feat_mm, i + 1)
                    turn.wait(feat_done, i - 1)
                    act.activation(fe[:, i % 2, :], ps[:, 4 + i % 4, :], ACT.Exp)
                    act.activation(fr[:, i % 2, :], ps[:, 4 + i % 4, :], ACT.Relu).then_inc(exp_done.sem, 1)
                for g in range(SG + 1):
                    if g < SG:
                        turn.wait(out_mm, g + 1)
                        turn.wait(out_normed, g - 1)
                        act.activation(ou[:, g % 2, :], ps[:, g % 2, :], ACT.Copy).then_inc(out_kept.sem, 1)
                    if g >= 1:
                        turn.wait(sum_mm, g)
                        act.activation(rr[:, (g - 1) % 2, :], ps[:, SUM_BANK, :], ACT.Ln, bias=cols[:, 1:2]).then_inc(ln_done.sem, 1)
                        turn.wait(ln_done, g)
                        act.activation(rr[:, (g - 1) % 2, :], rr[:, (g - 1) % 2, :], ACT.Exp, scale=-1.0).then_inc(recip_done.sem, 1)

        @block.vector
        def _(dve):
            for e in owner["dve"]:
                dve.sem_inc(e.sem, AHEAD)
            dve.wait_ge(ld_w.sem, ld_w.at(160))
            dve.wait_ge(prep_pool.sem, prep_pool.at(4))
            dve.tensor_tensor(feat_w[:, :, :], pm[:, None, :].to_broadcast([P, SH, 32]),
                              hoc[:, :, None].to_broadcast([P, SH, 32]), ALU.mult).then_inc(prep_dve.sem, 1)
            with dve.Fori(0, BATCH) as b:
                turn = Counts(dve, b, per_turn)
                turn.wait(proj_mm, 0)
                dve.tensor_scalar(hb[:, :], z[:, bass.ds(b * SEQ, SEQ)], 1.0, None, ALU.mult).then_inc(row_kept.sem, 1)
                turn.wait(proj_mm, 2)
                turn.wait(kv_mm, 0)
                dve.tensor_copy(va[:, :, :, 0:SD], ps[:, SUM_BANK, :].rearrange("p (t h c) -> p t h c", t=TB, h=SH)).then_inc(v_kept.sem, 1)
                for i in range(TILES):
                    turn.wait(exp_done, i + 1)
                    turn.wait(kv_mm, 0)
                    if i >= TB:
                        turn.wait(out_mm, i - TB + 1 - SG)
                    dve.scalar_tensor_tensor(feats[:, i, :], fe[:, i % 2, :], 1.0, fr[:, i % 2, :], ALU.min, ALU.add).then_inc(feat_done.sem, 1)
                turn.wait(kv_mm, 1)
                turn.wait(out_mm, 0)
                dve.tensor_tensor(kv[:, :, :], ps[:, KV_BANK, :].rearrange("p (g c) -> p g c", g=SG),
                                  own[:, None, :].to_broadcast([P, SG, P]), ALU.mult).then_inc(kv_kept.sem, 1)
                for g in range(SG):
                    turn.wait(recip_done, g + 1)
                    dve.tensor_tensor(on[:, g % 2, :], ou[:, g % 2, :], rr[:, g % 2, :], ALU.mult).then_inc(out_normed.sem, 1)
                turn.wait(y_mm, 1)
                xb = x[:, bass.ds(b * SEQ, SEQ)]
                dve.scalar_tensor_tensor(xb, ps[:, KV_BANK, :], cols[:, 0:1], xb, ALU.add, ALU.add).then_inc(added.sem, 1)
    for e, k in per_turn.items():
        e.past(BATCH * k)
    ld_w.past(160)
    prep_pool.past(4)
    prep_dve.past(1)


_INS = ["L0_attn_a_x", "L0_attn_a_w_qkv", "L0_attn_a_w_proj", "L0_attn_a_q_gamma", "L0_attn_a_q_beta",
        "L0_attn_a_k_gamma", "L0_attn_a_k_beta", "L0_attn_b_W_dq", "L0_attn_b_W_uq", "L0_attn_b_W_dkv",
        "L0_attn_b_W_uk", "L0_attn_b_W_uv", "L0_attn_b_W_o", "L0_ffn_Wqkv", "L0_ffn_q_scale", "L0_ffn_k_scale",
        "L0_ffn_Wo", "L0_ffn_ln_g", "L0_ffn_ln_b", "L0_ffn_W1", "L0_ffn_b1", "L0_ffn_W2", "L0_ffn_b2",
        "L1_attn_a_w_qkv", "L1_attn_a_proj_matrix", "L1_attn_a_w_out", "L1_attn_a_b_out",
        "L1_attn_b_w_qkv", "L1_attn_b_w_o", "L1_ffn_w_gate", "L1_ffn_w_up", "L1_ffn_w_down"]


def build(nc, d):
    with ExitStack() as ctx:
        core = Core(nc, ctx, d)
        load_and_transpose(core)
        normalise(core, False)
        small_attention(core, "norm")
        normalise(core, False)
        local_block(core)
        normalise(core, True)
        small_attention(core, "latent")
        normalise(core, False)
        local_block(core)
        normalise(core, True)
        linear_attention(core)
        normalise(core, False)
        swiglu(core, True)
        normalise(core, False)
        small_attention(core, "plain")
        normalise(core, False)
        swiglu(core, False)
        turn_and_store(core)


def kernel(**inputs):
    import numpy as _np
    import concourse.bacc as _bacc
    from concourse import mybir as _mybir
    from concourse.bass_utils import run_bass_kernel_spmd as _run

    nc = _bacc.Bacc("TRN2", target_bir_lowering=False, num_devices=1)
    laid = {name: _np.ascontiguousarray(inputs[name]) for name in _INS}
    laid.update(constants())
    arrays, d = {}, {}
    for name, a in laid.items():
        arrays[f"in_{name}"] = a
        d[name] = nc.dram_tensor(f"in_{name}", a.shape, _mybir.dt.from_np(a.dtype), kind="ExternalInput").ap()
    d["out"] = nc.dram_tensor("out", (BATCH, SEQ, P), _mybir.dt.float32, kind="ExternalOutput").ap()
    build(nc, d)
    r = _run(nc, [arrays], core_ids=[0])
    return r.results[0]["out"]
```
